# Optimizing a Trainium2 kernel written in Bass

```python
import numpy as np
import jax
import jax.numpy as jnp

def _softmax(x, axis=-1):
    return jax.nn.softmax(x, axis=axis)

def _gelu(x):
    return jax.nn.gelu(x, approximate=True)

def _silu(x):
    return jax.nn.silu(x)

def _sigmoid(x):
    return jax.nn.sigmoid(x)

def _layernorm(x, axis=-1, eps=1e-05):
    m = jnp.mean(x, axis=axis, keepdims=True)
    v = jnp.var(x, axis=axis, keepdims=True)
    return (x - m) / jnp.sqrt(v + eps)

def _scatter_add(tgt, idx, src, axis=0):
    return tgt.at[idx].add(src)

def _segment_sum(src, seg, n):
    return jax.ops.segment_sum(src, seg, n)
kernel_name = 'mk_adj_resnorm_d4_adj_r2_b1c58e'

def setup_inputs(seed: int=0):
    np.random.seed(seed)
    _w = jnp.asarray

    def _rec_inputs():
        import jax
        import jax.numpy as jnp
        _gk = jax.random.key(seed)
        x = -0.0002928 + 1 * jax.random.normal(jax.random.fold_in(_gk, 1), (2048, 256), jnp.float32)
        _a = jax.random.bernoulli(jax.random.fold_in(_gk, 2), 0.00390625, (2048, 2048))
        _a = jnp.logical_or(_a, jnp.swapaxes(_a, -1, -2))
        _a = jnp.logical_or(_a, jnp.eye(2048, dtype=bool))
        _af = _a.astype(jnp.float32)
        _af = _af * jax.random.uniform(jax.random.fold_in(_gk, 3), (2048, 2048), jnp.float32, 0.05, 1)
        adj = _af
        return (x, adj)
    x, adj = _rec_inputs()

    def _L0_gnn_setup():
        import jax, jax.numpy as jnp
        import numpy as np
        N = 4096
        IN_F = 256
        OUT_F = 256
        key = jax.random.key(seed)
        k1, k2, k3, k4 = jax.random.split(key, 4)
        input = jax.random.normal(k1, (N, IN_F), dtype=jnp.float32)
        adj = jax.random.uniform(k2, (N, N), dtype=jnp.float32)
        W = jax.random.normal(k3, (OUT_F, IN_F), dtype=jnp.float32) / np.sqrt(IN_F)
        b = jax.random.normal(k4, (OUT_F,), dtype=jnp.float32) * 0.01
        return {'input': input, 'adj': adj, 'W': W, 'b': b}
    _L0_gnn_all = _L0_gnn_setup()
    _L0_gnn_in = {k: v for k, v in _L0_gnn_all.items() if k in ('W', 'b')}
    del _L0_gnn_all

    def _L1_gnn_setup():
        import jax, jax.numpy as jnp
        import numpy as np
        N = 3072
        D_IN = 256
        D_OUT = 256
        DENSITY = 0.005
        key = jax.random.key(seed)
        ks = jax.random.split(key, 12)
        x = jax.random.normal(ks[0], (N, D_IN), dtype=jnp.float32)
        adj_a = (jax.random.uniform(ks[1], (N, N)) < DENSITY).astype(jnp.float32)
        adj_b = (jax.random.uniform(ks[2], (N, N)) < DENSITY).astype(jnp.float32)
        W_sa = jax.random.normal(ks[3], (D_IN, D_OUT), dtype=jnp.float32) * (1.414 / np.sqrt(D_IN + D_OUT))
        a_sa = jax.random.normal(ks[4], (1, 2 * D_OUT), dtype=jnp.float32) * (1.414 / np.sqrt(1 + 2 * D_OUT))
        stdv = 1.0 / np.sqrt(D_OUT)
        W_gcnb = jax.random.uniform(ks[5], (D_IN, D_OUT), minval=-stdv, maxval=stdv, dtype=jnp.float32)
        b_gcnb = jax.random.uniform(ks[6], (D_OUT,), minval=-stdv, maxval=stdv, dtype=jnp.float32)
        s = 1.0 / np.sqrt(2 * D_IN)
        Wa = jax.random.uniform(ks[7], (1, 2 * D_IN), minval=-s, maxval=s, dtype=jnp.float32)
        ba = jax.random.uniform(ks[8], (1,), minval=-s, maxval=s, dtype=jnp.float32)
        Wb = jax.random.uniform(ks[9], (1, 2 * D_IN), minval=-s, maxval=s, dtype=jnp.float32)
        bb = jax.random.uniform(ks[10], (1,), minval=-s, maxval=s, dtype=jnp.float32)
        return {'x': x, 'adj_a': adj_a, 'adj_b': adj_b, 'W_sa': W_sa, 'a_sa': a_sa, 'W_gcnb': W_gcnb, 'b_gcnb': b_gcnb, 'Wa': Wa, 'ba': ba, 'Wb': Wb, 'bb': bb}
    _L1_gnn_all = _L1_gnn_setup()
    _L1_gnn_in = {k: v for k, v in _L1_gnn_all.items() if k in ('W_sa', 'a_sa', 'W_gcnb', 'b_gcnb', 'Wa', 'ba', 'Wb', 'bb')}
    del _L1_gnn_all

    def _L2_gnn_setup():
        import jax, jax.numpy as jnp
        import numpy as np
        N = 2048
        INPUT_DIM = 256
        KEY_DIM = 64
        OUT_DIM = 256
        N_HEADS = 8

        def _xavier_normal(key, shape, gain):
            fan_in, fan_out = (shape[-2], shape[-1])
            std = gain * (2.0 / (fan_in + fan_out)) ** 0.5
            return jax.random.normal(key, shape, dtype=jnp.float32) * std
        key = jax.random.key(seed)
        kx, ka, kk, kq, kv, ko = jax.random.split(key, 6)
        gain = 2.0 ** 0.5
        node_matrix = jax.random.normal(kx, (N, INPUT_DIM), dtype=jnp.float32)
        adjacency_matrix = jax.random.randint(ka, (N, N), 0, 2).astype(jnp.float32)
        Wks = _xavier_normal(kk, (N_HEADS, INPUT_DIM, KEY_DIM), gain)
        Wqs = _xavier_normal(kq, (N_HEADS, INPUT_DIM, KEY_DIM), gain)
        Wvs = _xavier_normal(kv, (N_HEADS, INPUT_DIM, KEY_DIM), gain)
        Wo = _xavier_normal(ko, (N_HEADS, KEY_DIM, OUT_DIM), gain)
        return {'node_matrix': node_matrix, 'adjacency_matrix': adjacency_matrix, 'Wks': Wks, 'Wqs': Wqs, 'Wvs': Wvs, 'Wo': Wo}
    _L2_gnn_all = _L2_gnn_setup()
    _L2_gnn_in = {k: v for k, v in _L2_gnn_all.items() if k in ('Wks', 'Wqs', 'Wvs', 'Wo')}
    del _L2_gnn_all

    def _L3_gnn_setup():
        import jax, jax.numpy as jnp
        import numpy as np
        N = 4096
        D = 256
        L = 2
        NEG_SLOPE = 0.01

        def _gat_layer(x, W, adj):
            proj = x @ W
            Wh, Ws = jnp.split(proj, 2, axis=-1)
            scores = Wh @ Ws.T
            a = jax.nn.softmax(scores, axis=-1) * adj
            out = a @ Wh
            out = out + x
            return jax.nn.leaky_relu(out, NEG_SLOPE)
        key = jax.random.key(seed)
        k1, k2, k3 = jax.random.split(key, 3)
        inputs = jax.random.normal(k1, (N, D), dtype=jnp.float32)
        adj = jax.random.randint(k2, (N, N), 0, 2).astype(jnp.float32)
        W_stack = jax.random.normal(k3, (L, D, 2 * D), dtype=jnp.float32) * (1.0 / np.sqrt(D))
        return {'inputs': inputs, 'adj': adj, 'W_stack': W_stack}
    _L3_gnn_all = _L3_gnn_setup()
    _L3_gnn_in = {k: v for k, v in _L3_gnn_all.items() if k in ('W_stack',)}
    del _L3_gnn_all
    return {'x': x, 'adj': adj, 'L0_gnn_W': _L0_gnn_in['W'], 'L0_gnn_b': _L0_gnn_in['b'], 'L1_gnn_W_sa': _L1_gnn_in['W_sa'], 'L1_gnn_a_sa': _L1_gnn_in['a_sa'], 'L1_gnn_W_gcnb': _L1_gnn_in['W_gcnb'], 'L1_gnn_b_gcnb': _L1_gnn_in['b_gcnb'], 'L1_gnn_Wa': _L1_gnn_in['Wa'], 'L1_gnn_ba': _L1_gnn_in['ba'], 'L1_gnn_Wb': _L1_gnn_in['Wb'], 'L1_gnn_bb': _L1_gnn_in['bb'], 'L2_gnn_Wks': _L2_gnn_in['Wks'], 'L2_gnn_Wqs': _L2_gnn_in['Wqs'], 'L2_gnn_Wvs': _L2_gnn_in['Wvs'], 'L2_gnn_Wo': _L2_gnn_in['Wo'], 'L3_gnn_W_stack': _L3_gnn_in['W_stack']}

def reference(x, adj, L0_gnn_W, L0_gnn_b, L1_gnn_W_sa, L1_gnn_a_sa, L1_gnn_W_gcnb, L1_gnn_b_gcnb, L1_gnn_Wa, L1_gnn_ba, L1_gnn_Wb, L1_gnn_bb, L2_gnn_Wks, L2_gnn_Wqs, L2_gnn_Wvs, L2_gnn_Wo, L3_gnn_W_stack):
    import jax
    import jax.numpy as jnp

    def _L0_gnn_ref(input, adj, W, b):
        import jax, jax.numpy as jnp
        import numpy as np
        N = 4096
        IN_F = 256
        OUT_F = 256
        h = jnp.einsum('ni,oi->no', input, W) + b
        return adj @ h

    def _L1_gnn_ref(x, adj_a, adj_b, W_sa, a_sa, W_gcnb, b_gcnb, Wa, ba, Wb, bb):
        import jax, jax.numpy as jnp
        import numpy as np
        N = 3072
        D_IN = 256
        D_OUT = 256
        DENSITY = 0.005
        type_sum_a = adj_a @ x
        type_sum_b = adj_b @ x
        attn_a = jax.nn.sigmoid(jnp.concatenate([type_sum_a, x], axis=1) @ Wa.T + ba)
        attn_b = jax.nn.sigmoid(jnp.concatenate([type_sum_b, x], axis=1) @ Wb.T + bb)
        h = x @ W_sa
        Hd = h.shape[1]
        s_left = h @ a_sa[0, :Hd]
        s_right = h @ a_sa[0, Hd:]
        scores = s_left[:, None] + s_right[None, :]
        e = jnp.where(adj_a != 0, jnp.exp(-jax.nn.leaky_relu(scores, 0.01)), 0.0)
        attn = e / (jnp.sum(e, axis=1, keepdims=True) + 1e-05)
        x_a = attn @ h
        x_b = adj_b @ (x @ W_gcnb) + b_gcnb
        return jax.nn.sigmoid(attn_a * x_a + attn_b * x_b)

    def _L2_gnn_ref(node_matrix, adjacency_matrix, Wks, Wqs, Wvs, Wo):
        import jax, jax.numpy as jnp
        import numpy as np
        N = 2048
        INPUT_DIM = 256
        KEY_DIM = 64
        OUT_DIM = 256
        N_HEADS = 8

        def _xavier_normal(key, shape, gain):
            fan_in, fan_out = (shape[-2], shape[-1])
            std = gain * (2.0 / (fan_in + fan_out)) ** 0.5
            return jax.random.normal(key, shape, dtype=jnp.float32) * std
        n = adjacency_matrix.shape[0]
        adj = jnp.maximum(adjacency_matrix, jnp.eye(n, dtype=adjacency_matrix.dtype))
        keys = jnp.einsum('nj,hjk->hnk', node_matrix, Wks)
        queries = jnp.einsum('nj,hjk->hnk', node_matrix, Wqs)
        values = jnp.einsum('nj,hjk->hnk', node_matrix, Wvs)
        key_dim = Wks.shape[-1]
        atts = jnp.einsum('hqk,hmk->hqm', queries, keys) / key_dim ** 0.5
        atts = atts - 1e+16 * (1.0 - adj)[None, :, :]
        atts = jax.nn.softmax(atts, axis=-1)
        return jnp.einsum('hqm,hmk,hko->qo', atts, values, Wo)

    def _L3_gnn_ref(inputs, adj, W_stack):
        import jax, jax.numpy as jnp
        import numpy as np
        N = 4096
        D = 256
        L = 2
        NEG_SLOPE = 0.01

        def _gat_layer(x, W, adj):
            proj = x @ W
            Wh, Ws = jnp.split(proj, 2, axis=-1)
            scores = Wh @ Ws.T
            a = jax.nn.softmax(scores, axis=-1) * adj
            out = a @ Wh
            out = out + x
            return jax.nn.leaky_relu(out, NEG_SLOPE)
        x = inputs
        for l in range(W_stack.shape[0]):
            x = _gat_layer(x, W_stack[l], adj)
        return x
    x = _layernorm(x + _L0_gnn_ref(x, adj, L0_gnn_W, L0_gnn_b), axis=-1)
    x = _layernorm(x + _L1_gnn_ref(x, adj, adj, L1_gnn_W_sa, L1_gnn_a_sa, L1_gnn_W_gcnb, L1_gnn_b_gcnb, L1_gnn_Wa, L1_gnn_ba, L1_gnn_Wb, L1_gnn_bb), axis=-1)
    x = _layernorm(x + _L2_gnn_ref(x, adj, L2_gnn_Wks, L2_gnn_Wqs, L2_gnn_Wvs, L2_gnn_Wo), axis=-1)
    x = _layernorm(x + _L3_gnn_ref(x, adj, L3_gnn_W_stack), axis=-1)
    return x

_drawn_inputs = setup_inputs


def setup_inputs(seed=0):
    import zlib

    import numpy as np

    out = dict(_drawn_inputs(seed))
    spreads = {}
    factors = {'L1_gnn_a_sa': 3.99, 'L1_gnn_b_gcnb': 8.0, 'L1_gnn_Wa': 2.684}
    for name, (base, spread) in spreads.items():
        noise = np.random.default_rng([zlib.crc32(name.encode()), seed]).standard_normal(out[name].shape)
        drawn = base * np.exp(spread * noise) if base else spread * noise
        out[name] = jnp.asarray(drawn.astype(out[name].dtype))
    for name, factor in factors.items():
        out[name] = (out[name] * factor).astype(out[name].dtype)
    return out
```

```python
from contextlib import ExitStack

import concourse.bass as bass
from concourse import mybir

F32 = mybir.dt.float32
ALU = mybir.AluOpType
ACT = mybir.ActivationFunctionType
AX = mybir.AxisListType

P = 128
N = 2048
D = 256
NT = N // P
DC = D // P
H = 8
KD = 64
HD = H * KD
HC = HD // P
BANK = 512
Q = 4
QT = NT // Q
GW = D + 4
HW = D + 2
EPS = 1e-5
SLOPE = 0.01
HUGE = 1e16
KEY_SCALE = 0.125
LEAST_SCORE = -88.0


def graph_layers(nc, x, adj, adjT, W0T, b0, W_sa, a_sa, W_gates, b_gcnb, b_gates, Wk, Wq, Wv, Wo, W_stack, out):
    with ExitStack() as ctx:
        def sb(name, *shape):
            return ctx.enter_context(nc.sbuf_tensor(name, [P, *shape], F32))

        def sems(stage, *names):
            return {n: ctx.enter_context(nc.semaphore(f"{stage}_{n}")) for n in names}

        X = sb("X", NT, D)
        even = sb("even", 2 * NT * HD)
        odd = sb("odd", NT * (HW + GW))
        H0 = even[:, 0:NT * D].rearrange("p (t n) -> p t n", t=NT)
        HA = odd[:, 0:NT * HW].rearrange("p (t n) -> p t n", t=NT)
        GB = odd[:, NT * HW:NT * (HW + GW)].rearrange("p (t n) -> p t n", t=NT)
        KT2 = even[:, 0:HC * N].rearrange("p (c n) -> p c n", c=HC)
        V2 = even[:, HC * N:HC * N + NT * HD].rearrange("p (t n) -> p t n", t=NT)
        KT3 = odd[:, 0:DC * N].rearrange("p (c n) -> p c n", c=DC)
        V3 = odd[:, DC * N:DC * N + NT * D].rearrange("p (t n) -> p t n", t=NT)
        KT4 = even[:, 0:DC * N].rearrange("p (c n) -> p c n", c=DC)
        V4 = even[:, DC * N:DC * N + NT * D].rearrange("p (t n) -> p t n", t=NT)
        X4 = even[:, DC * N + NT * D:DC * N + 2 * NT * D].rearrange("p (t n) -> p t n", t=NT)

        slab = sb("slab", 2, N)
        wts = sb("wts", 2, N)
        wtsT = sb("wtsT", Q, BANK)
        mask = slab[:, 1, :]
        left_rows = wtsT[:, :, :].rearrange("p q n -> p (q n)")

        w0 = sb("w0", DC, D)
        wsa = sb("wsa", DC, D)
        wga = sb("wga", DC, GW)
        wk = sb("wk", DC, HD)
        wq = sb("wq", DC, HD)
        wv = sb("wv", DC, HD)
        wo = sb("wo", HC, D)
        ws = sb("ws", 2, DC, 2 * D)
        b0r = sb("b0r", D)
        bgr = sb("bgr", D)
        asr = sb("asr", 2 * D)
        bar = sb("bar", 2)

        ident = sb("ident", P)
        ones = sb("ones", P)
        minus_half = sb("minus_half", 1)
        right_cols = sb("right_cols", NT)
        xnew = sb("xnew", D)
        xnewT = sb("xnewT", DC, P)
        xq = sb("xq", D)
        xqT = sb("xqT", DC, P)
        qT = sb("qT", HC, P)
        mixed = sb("mixed", HD)
        mixedT = sb("mixedT", HC, P)
        res = sb("res", D)
        res2 = sb("res2", D)
        res3 = sb("res3", D)
        outt = sb("outt", 2, D)
        bn = sb("bn", 6)
        mv = sb("mv", 2)
        veps = sb("veps", 1)
        rstd = sb("rstd", 1)
        slr = sb("slr", 2)
        g1 = sb("g1", 8)
        diag = sb("diag", P)
        eye_less_one = sb("eye_less_one", P)
        rmax = sb("rmax", H)
        nmax = sb("nmax", H)
        rsum = sb("rsum", H)
        rinv = sb("rinv", H)

        ps = ctx.enter_context(nc.psum_tensor("ps", [P, 8, BANK], F32))

        init = sems("init", "filled", "consts", "x", "early", "late")
        LN = ("chain", "stats", "var", "std", "new", "stored", "turned", "flat", "proj")
        S0 = sems("s0", "new", "turned", "flat", "proj", "kept")
        S1 = sems("s1", "slab0", "slab1", "agg", "read", *LN, "kept_h", "kept_g", "left", "spread", "kept_left")
        S2 = sems("s2", "slab0", "slab1", "score", "raw", "exp", "edge", "agg", "read", "gate", "gexp", "z", "zexp", *LN, "kept")
        ATT = ("slab0", "slab1", "xq", "xqturned", "xqflat", "query", "qkept", "qk", "max", "exp",
               "trn0", "trn1", "ev0", "ev1", "pv", "read")
        S3 = sems("s3", "step", "masked", "waited", "rowmax", "inv", "mixed", "mturned", "mflat", "wo", *ATT, *LN, "kept")
        S4 = sems("s4", *ATT, *LN, "kept")
        S5 = sems("s5", "out0", "out1", *ATT, "chain", "stats", "var", "std", "new")

        def two_by_two(eng, body, stop=NT):
            for t in range(3):
                body(t, t % 2, t // 2)
            with eng.Fori(1, (stop - 4) // 2) as u:
                body(u * 2 + 1, 1, u)
                body(u * 2 + 2, 0, u + 1)
            for t in range(stop - 3, stop):
                body(t, t % 2, t // 2)

        block = ctx.enter_context(nc.Block())

        @block.sync
        def _(sp):
            def split(a):
                return a.rearrange("(c p) n -> p c n", p=P)

            xv = x.rearrange("(t p) d -> p t d", p=P)
            sp.dma_start(X[:, :, :], xv).then_inc(init["x"], 16)
            sp.dma_start(w0[:, :, :], split(W0T)).then_inc(init["early"], 16)
            sp.dma_start(b0r[:, :], b0.partition_broadcast(P)).then_inc(init["early"], 16)

            def load(s, src, t, k):
                sp.dma_start(slab[:, k, :], src[t]).then_inc(s["slab1"] if k else s["slab0"], 16)

            load(S1, adjT, 0, 0)
            load(S1, adjT, 1, 1)
            for dst, src in ((wsa[:, :, :], split(W_sa)), (wga[:, :, :], split(W_gates)), (wk[:, :, :], split(Wk)),
                             (wq[:, :, :], split(Wq)), (wv[:, :, :], split(Wv)), (wo[:, :, :], split(Wo)),
                             (ws[:, 0], split(W_stack[0])), (ws[:, 1], split(W_stack[1])),
                             (bgr[:, :], b_gcnb.partition_broadcast(P)), (asr[:, :], a_sa.partition_broadcast(P)),
                             (bar[:, :], b_gates.partition_broadcast(P))):
                sp.dma_start(dst, src).then_inc(init["late"], 16)
            with sp.Fori(1, NT // 2) as u:
                for k in range(2):
                    sp.wait_ge(S1["agg"], u * 2 + k - 1)
                    load(S1, adjT, u * 2 + k, k)
            for k in range(2):
                sp.wait_ge(S1["agg"], NT - 1 + k)
                load(S2, adjT, k, k)
            with sp.Fori(1, NT // 2) as u:
                for k in range(2):
                    sp.wait_ge(S2["agg"], u * 2 + k - 1)
                    load(S2, adjT, u * 2 + k, k)
            sp.wait_ge(S2["agg"], NT)
            load(S3, adj, 0, 0)
            with sp.Fori(1, NT) as t:
                sp.wait_ge(S3["masked"], t)
                load(S3, adj, t, 0)
            sp.wait_ge(S3["masked"], NT)
            load(S4, adjT, 0, 0)
            sp.wait_ge(S3["max"], NT * H)
            load(S4, adjT, 1, 1)
            with sp.Fori(1, NT // 2) as u:
                for k in range(2):
                    sp.wait_ge(S4["ev1"], u * 4 + (2 * k - 2))
                    load(S4, adjT, u * 2 + k, k)
            for k in range(2):
                sp.wait_ge(S4["ev1"], 2 * (NT - 1 + k))
                load(S5, adjT, k, k)

            def store(t, k):
                sp.wait_ge(S5["new"], t + 1)
                sp.dma_start(out[t], outt[:, k, :]).then_inc(S5["out1"] if k else S5["out0"], 16)

            with sp.Fori(1, NT // 2) as u:
                for k in range(2):
                    sp.wait_ge(S5["ev1"], u * 4 + (2 * k - 2))
                    load(S5, adjT, u * 2 + k, k)
                for k in range(2):
                    store(u * 2 + (k - 2), k)
            for k in range(2):
                store(NT - 2 + k, k)
            sp.wait_ge(S5["out0"], 16 * NT // 2)
            sp.wait_ge(S5["out1"], 16 * NT // 2)

        @block.gpsimd
        def _(pool):
            nc.gpsimd.memset(ident[:, :], 0.0).then_inc(init["filled"], 1)
            nc.gpsimd.memset(ones[:, :], 1.0).then_inc(init["consts"], 1)
            nc.gpsimd.memset(minus_half[:, :], -0.5).then_inc(init["consts"], 1)
            nc.gpsimd.memset(HA[:, :, D:HW], 1.0).then_inc(init["consts"], 1)
            nc.gpsimd.memset(eye_less_one[:, :], -1.0).then_inc(init["filled"], 1)
            pool.wait_ge(init["filled"], 2)
            nc.gpsimd.affine_select(out=ident[:, :], in_=ident[:, :], compare_op=ALU.not_equal, fill=1.0, base=0,
                                    pattern=[[-1, P]], channel_multiplier=1).then_inc(init["consts"], 1)
            nc.gpsimd.affine_select(out=eye_less_one[:, :], in_=eye_less_one[:, :], compare_op=ALU.not_equal, fill=0.0,
                                    base=0, pattern=[[-1, P]], channel_multiplier=1).then_inc(init["consts"], 1)

            pool.wait_ge(init["x"], 16)
            nc.gpsimd.tensor_copy(xnew[:, :], X[:, 0, :]).then_inc(S0["new"], 1)
            with pool.Fori(1, NT) as t:
                pool.wait_ge(S0["turned"], t)
                nc.gpsimd.tensor_copy(xnew[:, :], X[:, t, :]).then_inc(S0["new"], 1)

            def rsqrt(s, t):
                pool.wait_ge(s["var"], t + 1)
                nc.gpsimd.tensor_tensor(rstd[:, :], veps[:, :], minus_half[:, :], ALU.pow).then_inc(s["std"], 1)

            def store(s, t, to):
                pool.wait_ge(s["new"], t + 1)
                nc.gpsimd.tensor_copy(to[:, t, :], xnew[:, :]).then_inc(s["stored"], 1)

            def next_query(s, t, src):
                pool.wait_ge(s["xqturned"], t)
                nc.gpsimd.tensor_copy(xq[:, :], src[:, t, :]).then_inc(s["xq"], 1)

            pool.wait_ge(init["consts"], 5)
            for s in (S1, S2):
                with pool.Fori(0, NT) as t:
                    rsqrt(s, t)
                    store(s, t, X)
            pool.wait_ge(S2["stored"], NT)
            next_query(S3, 0, X)
            with pool.Fori(0, NT - 1) as t:
                next_query(S3, t + 1, X)
                rsqrt(S3, t)
                store(S3, t, X)
            rsqrt(S3, NT - 1)
            store(S3, NT - 1, X)
            pool.wait_ge(S3["stored"], NT)
            next_query(S4, 0, X)
            next_query(S4, 1, X)
            with pool.Fori(0, NT - 2) as t:
                next_query(S4, t + 2, X)
                store(S4, t, X4)
            store(S4, NT - 2, X4)
            store(S4, NT - 1, X4)
            pool.wait_ge(S4["stored"], NT)
            next_query(S5, 0, X4)
            next_query(S5, 1, X4)
            with pool.Fori(0, NT - 2) as t:
                next_query(S5, t + 2, X4)
                rsqrt(S5, t)
            rsqrt(S5, NT - 2)
            rsqrt(S5, NT - 1)

        @block.tensor
        def _(pe):
            mm = nc.tensor.matmul

            def turn_new(s, t):
                pe.wait_ge(s["new"], t + 1)
                for c in range(DC):
                    last = nc.tensor.transpose(ps[:, 7, c * P:(c + 1) * P], xnew[:, c * P:(c + 1) * P], ident[:, :])
                last.then_inc(s["turned"], 1)

            def rows(bank, col, wt, n):
                for c in range(DC):
                    last = mm(ps[:, bank, col:col + n], xnewT[:, c, :], wt[:, c, 0:n], start=(c == 0), stop=(c == DC - 1))
                return last

            def cols(bank, wt, first, chunks, xt):
                for o in range(chunks):
                    for c in range(DC):
                        last = mm(ps[:, bank, o * P:(o + 1) * P], wt[:, c, first + o * P:first + (o + 1) * P], xt[:, c, :],
                                  start=(c == 0), stop=(c == DC - 1))
                return last

            pe.wait_ge(init["consts"], 5)
            pe.wait_ge(init["early"], 32)
            turn_new(S0, 0)
            pe.wait_ge(S0["flat"], 1)
            rows(5, 0, w0, D).then_inc(S0["proj"], 1)
            with pe.Fori(1, NT) as t:
                pe.wait_ge(S0["flat"], t)
                turn_new(S0, t)
                pe.wait_ge(S0["flat"], t + 1)
                pe.wait_ge(S0["kept"], t)
                rows(5, 0, w0, D).then_inc(S0["proj"], 1)

            def agg0(t, k, r):
                pe.wait_ge(S1["slab1"] if k else S1["slab0"], r * 16 + 16)
                if not (isinstance(t, int) and t < 2):
                    pe.wait_ge(S1["read"], t - 1)
                for j in range(NT):
                    last = mm(ps[:, k, 0:D], slab[:, k, j * P:(j + 1) * P], H0[:, j, :], start=(j == 0), stop=(j == NT - 1))
                last.then_inc(S1["agg"], 1)

            def tail1(t):
                pe.wait_ge(S1["flat"], t)
                turn_new(S1, t)
                pe.wait_ge(S1["flat"], t + 1)
                pe.wait_ge(S1["kept_h"], t)
                pe.wait_ge(S1["kept_g"], t)
                rows(5, 0, wsa, D)
                rows(6, 0, wga, GW).then_inc(S1["proj"], 1)
                pe.wait_ge(S1["left"], t + 1)
                pe.wait_ge(S1["kept_left"], t)
                mm(ps[:, 4, 0:P], ones[:, :], diag[:, :], start=True, stop=True).then_inc(S1["spread"], 1)

            pe.wait_ge(S0["kept"], NT)
            pe.wait_ge(init["late"], 16 * 11)
            agg0(0, 0, 0)
            agg0(1, 1, 0)
            tail1(0)
            with pe.Fori(1, NT // 2) as u:
                agg0(u * 2, 0, u)
                tail1(u * 2 - 1)
                agg0(u * 2 + 1, 1, u)
                tail1(u * 2)
            tail1(NT - 1)

            def agg_gates(t, k, r):
                pe.wait_ge(S2["slab1"] if k else S2["slab0"], r * 16 + 16)
                if not (isinstance(t, int) and t < 2):
                    pe.wait_ge(S2["read"], t - 1)
                for j in range(NT):
                    mm(ps[:, 2 + k, 0:D + 2], slab[:, k, j * P:(j + 1) * P], GB[:, j, 0:D + 2], start=(j == 0), stop=(j == NT - 1))

            def agg_edges(t, k):
                pe.wait_ge(S2["edge"], t + 1)
                for j in range(NT):
                    last = mm(ps[:, k, 0:D + 1], wts[:, k, j * P:(j + 1) * P], HA[:, j, 0:D + 1], start=(j == 0), stop=(j == NT - 1))
                last.then_inc(S2["agg"], 1)

            def tail2(t):
                pe.wait_ge(S2["flat"], t)
                turn_new(S2, t)
                pe.wait_ge(S2["flat"], t + 1)
                pe.wait_ge(S2["kept"], t)
                cols(5, wk, 0, HC, xnewT)
                rows(6, 0, wv, HD).then_inc(S2["proj"], 1)

            pe.wait_ge(S1["kept_h"], NT)
            pe.wait_ge(S1["kept_g"], NT)
            agg_gates(0, 0, 0)
            agg_edges(0, 0)
            agg_gates(1, 1, 0)
            tail2(0)
            agg_edges(1, 1)
            with pe.Fori(1, NT // 2) as u:
                agg_gates(u * 2, 0, u)
                tail2(u * 2 - 1)
                agg_edges(u * 2, 0)
                agg_gates(u * 2 + 1, 1, u)
                tail2(u * 2)
                agg_edges(u * 2 + 1, 1)
            tail2(NT - 1)

            def turn_query(s, t):
                pe.wait_ge(s["xq"], t + 1)
                for c in range(DC):
                    last = nc.tensor.transpose(ps[:, 7, c * P:(c + 1) * P], xq[:, c * P:(c + 1) * P], ident[:, :])
                last.then_inc(s["xqturned"], 1)

            def query(s, t, wt, chunks):
                pe.wait_ge(s["xqflat"], t + 1)
                cols(7, wt, 0, chunks, xqT).then_inc(s["query"], 1)

            def turn(s, n, q, k):
                if q == 0:
                    pe.wait_ge(s["exp"], n + 1)
                b = q % 2
                pe.wait_ge(s["ev1"] if b else s["ev0"], n * 2 + q // 2)
                for j in range(QT):
                    last = nc.tensor.transpose(ps[:, 4 + b, j * P:(j + 1) * P],
                                               wts[:, k, (q * QT + j) * P:(q * QT + j + 1) * P], ident[:, :])
                last.then_inc(s["trn1"] if b else s["trn0"], 1)

            def mix(s, n, q, v, lo, width):
                b = q % 2
                pe.wait_ge(s["ev1"] if b else s["ev0"], n * 2 + (q // 2 + 1))
                for j in range(QT):
                    jt = q * QT + j
                    last = mm(ps[:, 6, lo:lo + width], wtsT[:, q, j * P:(j + 1) * P], v[:, jt, lo:lo + width],
                              start=(jt == 0), stop=(jt == NT - 1))
                if q == Q - 1:
                    last.then_inc(s["pv"], 1)

            def scores2(t, h):
                if h == 0:
                    pe.wait_ge(S3["qkept"], t + 1)
                pe.wait_ge(S3["max"], t * H + h)
                lo = h % 2 * KD
                for q in range(Q):
                    last = mm(ps[:, q, :], qT[lo:lo + KD, h // 2, :], KT2[lo:lo + KD, h // 2, q * BANK:(q + 1) * BANK],
                              start=True, stop=True)
                last.then_inc(S3["qk"], 1)

            def turn_mixed(t):
                pe.wait_ge(S3["mixed"], t + 1)
                for c in range(HC):
                    last = nc.tensor.transpose(ps[:, 7, c * P:(c + 1) * P], mixed[:, c * P:(c + 1) * P], ident[:, :])
                last.then_inc(S3["mturned"], 1)

            def project_mixed(t):
                pe.wait_ge(S3["mflat"], t + 1)
                for c in range(HC):
                    last = mm(ps[:, 7, 0:D], mixedT[:, c, :], wo[:, c, :], start=(c == 0), stop=(c == HC - 1))
                last.then_inc(S3["wo"], 1)

            def next_products(s, t, wt):
                pe.wait_ge(s["flat"], t + 1)
                cols(7, wt, D, DC, xnewT)
                for c in range(DC):
                    last = mm(ps[:, 7, D:2 * D], xnewT[:, c, :], wt[:, c, 0:D], start=(c == 0), stop=(c == DC - 1))
                last.then_inc(s["proj"], 1)

            def body2(t, first, last):
                for h in range(H):
                    n = t * H + h
                    if h < H - 1:
                        scores2(t, h + 1)
                    elif not last:
                        scores2(t + 1, 0)
                    if h == 0 and not first:
                        turn_mixed(t - 1)
                    if h == 1 and not first:
                        project_mixed(t - 1)
                    if h == 3 and not first:
                        turn_new(S3, t - 1)
                    if h == 4 and not first:
                        next_products(S3, t - 1, ws[:, 0])
                    if h == 5 and not last:
                        if not first:
                            pe.wait_ge(S3["kept"], t)
                        turn_query(S3, t + 1)
                    if h == 6 and not last:
                        query(S3, t + 1, wq, HC)
                    lo = h * KD
                    turn(S3, n, 0, h % 2)
                    turn(S3, n, 1, h % 2)
                    mix(S3, n, 0, V2, lo, KD)
                    turn(S3, n, 2, h % 2)
                    mix(S3, n, 1, V2, lo, KD)
                    turn(S3, n, 3, h % 2)
                    mix(S3, n, 2, V2, lo, KD)
                    mix(S3, n, 3, V2, lo, KD)

            pe.wait_ge(S2["kept"], NT)
            turn_query(S3, 0)
            query(S3, 0, wq, HC)
            scores2(0, 0)
            body2(0, True, False)
            with pe.Fori(1, NT - 1) as t:
                body2(t, False, False)
            body2(NT - 1, False, True)
            pe.wait_ge(S3["kept"], NT - 1)
            turn_mixed(NT - 1)
            project_mixed(NT - 1)
            turn_new(S3, NT - 1)
            next_products(S3, NT - 1, ws[:, 0])

            def scores3(s, t, kt):
                pe.wait_ge(s["qkept"], t + 1)
                pe.wait_ge(s["exp"], t)
                for c in range(DC):
                    for q in range(Q):
                        last = mm(ps[:, q, :], qT[:, c, :], kt[:, c, q * BANK:(q + 1) * BANK],
                                  start=(c == 0), stop=(c == DC - 1))
                last.then_inc(s["qk"], 1)

            def step3(s, kt, v, wt, wnext):
                def body(t, k, r):
                    at = t if isinstance(t, int) else NT // 2
                    if at < NT - 1:
                        scores3(s, t + 1, kt)
                    turn(s, t, 0, k)
                    turn(s, t, 1, k)
                    if at > 0:
                        if wnext is not None:
                            if at > 1:
                                pe.wait_ge(s["kept"], t - 1)
                            turn_new(s, t - 1)
                        pe.wait_ge(s["read"], t)
                    mix(s, t, 0, v, 0, D)
                    turn(s, t, 2, k)
                    if at > 0 and wnext is not None:
                        next_products(s, t - 1, wnext)
                    mix(s, t, 1, v, 0, D)
                    turn(s, t, 3, k)
                    if at < NT - 2:
                        if at > 0 and wnext is not None:
                            pe.wait_ge(s["kept"], t)
                        turn_query(s, t + 2)
                    mix(s, t, 2, v, 0, D)
                    if at < NT - 2:
                        query(s, t + 2, wt, DC)
                    mix(s, t, 3, v, 0, D)
                return body

            for s, prev, kt, v, wt, wnext in ((S4, S3, KT3, V3, ws[:, 0], ws[:, 1]), (S5, S4, KT4, V4, ws[:, 1], None)):
                pe.wait_ge(prev["kept"], NT)
                turn_query(s, 0)
                query(s, 0, wt, DC)
                scores3(s, 0, kt)
                turn_query(s, 1)
                query(s, 1, wt, DC)
                two_by_two(pe, step3(s, kt, v, wt, wnext))
                if wnext is not None:
                    pe.wait_ge(s["kept"], NT - 1)
                    turn_new(s, NT - 1)
                    next_products(s, NT - 1, wnext)

        @block.scalar
        def _(act):
            def flatten(s, t):
                act.wait_ge(s["turned"], t + 1)
                nc.scalar.copy(xnewT[:, :, :].rearrange("p c n -> p (c n)"), ps[:, 7, 0:D]).then_inc(s["flat"], 1)

            with act.Fori(0, NT) as t:
                flatten(S0, t)

            with act.Fori(0, NT) as t:
                flatten(S1, t)
                act.wait_ge(S1["proj"], t + 1)
                nc.scalar.copy(GB[:, t, :], ps[:, 6, 0:GW]).then_inc(S1["kept_g"], 1)
                act.wait_ge(S1["spread"], t + 1)
                nc.scalar.copy(left_rows[:, bass.ts(t, P)], ps[:, 4, 0:P]).then_inc(S1["kept_left"], 1)

            def edge_exp(t, k):
                act.wait_ge(S2["raw"], t + 1)
                nc.scalar.activation(wts[:, k, :], wts[:, k, :], ACT.Exp, scale=-1.0).then_inc(S2["exp"], 1)

            def finish2(t):
                act.wait_ge(S2["gate"], t + 1)
                nc.scalar.activation(g1[:, 4:6], g1[:, 2:4], ACT.Exp, scale=-1.0).then_inc(S2["gexp"], 1)
                act.wait_ge(S2["z"], t + 1)
                nc.scalar.activation(res2[:, :], res3[:, :], ACT.Exp, scale=-1.0).then_inc(S2["zexp"], 1)
                flatten(S2, t)
                act.wait_ge(S2["proj"], t + 1)
                nc.scalar.copy(KT2[:, :, bass.ts(t, P)], ps[:, 5, :].rearrange("p (c n) -> p c n", c=HC))
                nc.scalar.copy(V2[:, t, :], ps[:, 6, :]).then_inc(S2["kept"], 1)

            edge_exp(0, 0)
            edge_exp(1, 1)
            finish2(0)
            with act.Fori(1, NT // 2) as u:
                edge_exp(u * 2, 0)
                finish2(u * 2 - 1)
                edge_exp(u * 2 + 1, 1)
                finish2(u * 2)
            finish2(NT - 1)

            def flatten_query(s, t):
                act.wait_ge(s["xqturned"], t + 1)
                nc.scalar.copy(xqT[:, :, :].rearrange("p c n -> p (c n)"), ps[:, 7, 0:D]).then_inc(s["xqflat"], 1)

            def keep_query(s, t, width, scale):
                act.wait_ge(s["query"], t + 1)
                nc.scalar.activation(qT[:, :, :].rearrange("p c n -> p (c n)")[:, 0:width], ps[:, 7, 0:width], ACT.Copy,
                                     scale=scale).then_inc(s["qkept"], 1)

            def keep_next(s, t, kt, v):
                act.wait_ge(s["proj"], t + 1)
                nc.scalar.copy(kt[:, :, bass.ts(t, P)], ps[:, 7, 0:D].rearrange("p (c n) -> p c n", c=DC))
                nc.scalar.copy(v[:, t, :], ps[:, 7, D:2 * D]).then_inc(s["kept"], 1)

            def exp2(n, h):
                act.wait_ge(S3["max"], n + 1)
                nc.scalar.activation(wts[:, h % 2, :], wts[:, h % 2, :], ACT.Exp, bias=nmax[:, h:h + 1],
                                     accum_out=rsum[:, h:h + 1]).then_inc(S3["exp"], 1)

            def flatten_mixed(t):
                act.wait_ge(S3["mturned"], t + 1)
                nc.scalar.copy(mixedT[:, :, :].rearrange("p c n -> p (c n)"), ps[:, 7, :]).then_inc(S3["mflat"], 1)

            def body2(t, first, last):
                for h in range(H):
                    n = t * H + h
                    if h < H - 1 or not last:
                        exp2(n + 1, (h + 1) % H)
                    if h == 0 and not first:
                        flatten_mixed(t - 1)
                    if h == 3 and not first:
                        flatten(S3, t - 1)
                    if h == 4 and not first:
                        keep_next(S3, t - 1, KT3, V3)
                    if h == 5 and not last:
                        flatten_query(S3, t + 1)
                    if h == 6 and not last:
                        keep_query(S3, t + 1, HD, KEY_SCALE)
                    for q in (1, 3):
                        act.wait_ge(S3["trn1"], n * 2 + (q // 2 + 1))
                        nc.scalar.copy(wtsT[:, q, :], ps[:, 5, :]).then_inc(S3["ev1"], 1)

            flatten_query(S3, 0)
            keep_query(S3, 0, HD, KEY_SCALE)
            exp2(0, 0)
            body2(0, True, False)
            with act.Fori(1, NT - 1) as t:
                body2(t, False, False)
            body2(NT - 1, False, True)
            flatten_mixed(NT - 1)
            flatten(S3, NT - 1)
            keep_next(S3, NT - 1, KT3, V3)

            def exp3(s, t, k):
                act.wait_ge(s["max"], t + 1)
                if not (isinstance(t, int) and t < 2):
                    act.wait_ge(s["trn1"], t * 2 - 2)
                nc.scalar.activation(wts[:, k, :], ps[:, 0:Q, :].rearrange("p q n -> p (q n)"), ACT.Exp,
                                     bias=nmax[:, k:k + 1], accum_out=rsum[:, k:k + 1]).then_inc(s["exp"], 1)

            def step3(s, nxt):
                def body(t, k, r):
                    at = t if isinstance(t, int) else NT // 2
                    if at < NT - 1:
                        exp3(s, t + 1, 1 - k)
                    if at > 0 and nxt is not None:
                        flatten(s, t - 1)
                        keep_next(s, t - 1, *nxt)
                    if at < NT - 2:
                        flatten_query(s, t + 2)
                        keep_query(s, t + 2, D, 1.0)
                return body

            for s, nxt in ((S4, (KT4, V4)), (S5, None)):
                flatten_query(s, 0)
                keep_query(s, 0, D, 1.0)
                exp3(s, 0, 0)
                flatten_query(s, 1)
                keep_query(s, 1, D, 1.0)
                two_by_two(act, step3(s, nxt))
                if nxt is not None:
                    flatten(s, NT - 1)
                    keep_next(s, NT - 1, *nxt)

        @block.vector
        def _(dve):
            v = nc.vector

            class Chain:
                def __init__(self, s, t, per_tile):
                    self.sem, self.base, self.per_tile, self.n = s, t * per_tile, per_tile, 0

                def then(self, instruction):
                    instruction.then_inc(self.sem, 1)
                    self.n += 1
                    dve.wait_ge(self.sem, self.base + self.n)

                def done(self):
                    assert self.n == self.per_tile, self.n

            def layernorm(s, t, c, src, dst):
                v.bn_stats(bn[:, :], src).then_inc(s["stats"], 1)
                dve.wait_ge(init["early"], 32)
                dve.wait_ge(s["stats"], t + 1)
                c.then(v.bn_aggr(mv[:, :], bn[:, :]))
                v.tensor_scalar(veps[:, :], mv[:, 1:2], EPS, None, ALU.add).then_inc(s["var"], 1)
                dve.wait_ge(s["std"], t + 1)
                v.tensor_scalar(dst, src, mv[:, 0:1], rstd[:, :], ALU.subtract, ALU.mult).then_inc(s["new"], 1)

            dve.wait_ge(init["early"], 32)
            with dve.Fori(0, NT) as t:
                dve.wait_ge(S0["proj"], t + 1)
                v.tensor_tensor(H0[:, t, :], ps[:, 5, 0:D], b0r[:, :], ALU.add).then_inc(S0["kept"], 1)

            def stage1(t, k):
                c = Chain(S1["chain"], t, 4)
                dve.wait_ge(S1["agg"], t + 1)
                v.tensor_tensor(res[:, :], ps[:, k, 0:D], X[:, t, :], ALU.add).then_inc(S1["read"], 1)
                dve.wait_ge(S1["read"], t + 1)
                dve.wait_ge(S1["turned"], t)
                dve.wait_ge(S1["stored"], t)
                layernorm(S1, t, c, res[:, :], xnew[:, :])
                dve.wait_ge(S1["proj"], t + 1)
                v.tensor_copy(HA[:, t, 0:D], ps[:, 5, 0:D])
                c.then(v.scalar_tensor_tensor(res2[:, :], ps[:, 5, 0:D], 1.0, asr[:, 0:D], ALU.mult, ALU.mult,
                                              accum_out=slr[:, 0:1]))
                c.then(v.scalar_tensor_tensor(res3[:, :], ps[:, 5, 0:D], 1.0, asr[:, D:2 * D], ALU.mult, ALU.mult,
                                              accum_out=slr[:, 1:2]))
                c.then(v.tensor_copy(right_cols[:, bass.ts(t, 1)], slr[:, 1:2]))
                dve.wait_ge(S1["spread"], t)
                v.tensor_scalar(diag[:, :], ident[:, :], slr[:, 0:1], None, ALU.mult).then_inc(S1["left"], 1)
                v.tensor_copy(res2[:, 0:1], slr[:, 1:2]).then_inc(S1["kept_h"], 1)
                c.done()

            dve.wait_ge(init["late"], 16 * 11)
            dve.wait_ge(init["consts"], 5)
            stage1(0, 0)
            stage1(1, 1)
            with dve.Fori(1, NT // 2) as u:
                stage1(u * 2, 0)
                stage1(u * 2 + 1, 1)

            def edges(t, k, r):
                w3 = wts[:, k, :].rearrange("p (j n) -> p j n", j=NT)
                if not (isinstance(t, int) and t < 2):
                    dve.wait_ge(S2["agg"], t - 1)
                v.tensor_tensor(w3, left_rows[:, bass.ts(t, P)].unsqueeze(1).broadcast_to([P, NT, P]),
                                right_cols[:, :].unsqueeze(2).broadcast_to([P, NT, P]), ALU.add).then_inc(S2["score"], 1)
                dve.wait_ge(S2["score"], t * 2 + 1)
                v.scalar_tensor_tensor(wts[:, k, :], wts[:, k, :], SLOPE, wts[:, k, :], ALU.mult, ALU.max).then_inc(S2["score"], 1)
                dve.wait_ge(S2["score"], t * 2 + 2)
                v.tensor_scalar(wts[:, k, :], wts[:, k, :], LEAST_SCORE, None, ALU.max).then_inc(S2["raw"], 1)
                dve.wait_ge(S2["exp"], t + 1)
                dve.wait_ge(S2["slab1"] if k else S2["slab0"], r * 16 + 16)
                v.scalar_tensor_tensor(wts[:, k, :], slab[:, k, :], 0.0, wts[:, k, :], ALU.not_equal, ALU.mult).then_inc(S2["edge"], 1)

            def finish2(t, k):
                c = Chain(S2["chain"], t, 11)
                dve.wait_ge(S2["agg"], t + 1)
                c.then(v.tensor_scalar(g1[:, 0:1], ps[:, k, D:D + 1], EPS, None, ALU.add))
                c.then(v.reciprocal(g1[:, 1:2], g1[:, 0:1]))
                c.then(v.tensor_tensor(g1[:, 2:4], ps[:, 2 + k, D:D + 2], GB[:, t, D + 2:GW], ALU.add))
                v.tensor_tensor(g1[:, 2:4], g1[:, 2:4], bar[:, :], ALU.add).then_inc(S2["gate"], 1)
                dve.wait_ge(S2["gexp"], t + 1)
                c.then(v.tensor_scalar(g1[:, 4:6], g1[:, 4:6], 1.0, None, ALU.add))
                c.then(v.reciprocal(g1[:, 6:8], g1[:, 4:6]))
                c.then(v.tensor_tensor(g1[:, 0:1], g1[:, 6:7], g1[:, 1:2], ALU.mult))
                c.then(v.tensor_tensor(res[:, :], ps[:, 2 + k, 0:D], bgr[:, :], ALU.add))
                v.tensor_scalar(res2[:, :], ps[:, k, 0:D], g1[:, 0:1], None, ALU.mult).then_inc(S2["read"], 1)
                dve.wait_ge(S2["read"], t + 1)
                v.scalar_tensor_tensor(res3[:, :], res[:, :], g1[:, 7:8], res2[:, :], ALU.mult, ALU.add).then_inc(S2["z"], 1)
                dve.wait_ge(S2["zexp"], t + 1)
                c.then(v.tensor_scalar(res[:, :], res2[:, :], 1.0, None, ALU.add))
                c.then(v.reciprocal(res2[:, :], res[:, :]))
                c.then(v.tensor_tensor(res[:, :], res2[:, :], X[:, t, :], ALU.add))
                dve.wait_ge(S2["turned"], t)
                dve.wait_ge(S2["stored"], t)
                layernorm(S2, t, c, res[:, :], xnew[:, :])
                c.done()

            dve.wait_ge(S1["stored"], NT)
            dve.wait_ge(S1["kept_left"], NT)
            edges(0, 0, 0)
            edges(1, 1, 0)
            finish2(0, 0)
            with dve.Fori(1, NT // 2) as u:
                edges(u * 2, 0, u)
                finish2(u * 2 - 1, 1)
                edges(u * 2 + 1, 1, u)
                finish2(u * 2, 0)
            finish2(NT - 1, 1)

            def make_mask(t):
                dve.wait_ge(S3["slab0"], t * 16 + 16)
                v.tensor_scalar(mask, slab[:, 0, :], 0.0, -1.0, ALU.max, ALU.add).then_inc(S3["masked"], 1)
                dve.wait_ge(S3["masked"], t + 1)
                v.tensor_tensor(mask[:, bass.ts(t, P)], mask[:, bass.ts(t, P)], eye_less_one[:, :], ALU.max).then_inc(S3["step"], 1)
                dve.wait_ge(S3["step"], t * 2 + 1)
                v.tensor_scalar(mask, mask, HUGE, None, ALU.mult).then_inc(S3["step"], 1)
                dve.wait_ge(S3["step"], t * 2 + 2)

            def mask_scores(n, h):
                dve.wait_ge(S3["qk"], n + 1)
                if not (isinstance(n, int) and n < 2):
                    dve.wait_ge(S3["trn1"], n * 2 - 2)
                dve.sem_inc(S3["waited"], 1)
                v.tensor_tensor_reduce(wts[:, h % 2, :], ps[:, 0:Q, :].rearrange("p q n -> p (q n)"), mask, 1.0, -3e38,
                                       ALU.add, ALU.max, rmax[:, h:h + 1]).then_inc(S3["rowmax"], 1)
                dve.wait_ge(S3["rowmax"], n + 1)
                v.tensor_scalar(nmax[:, h:h + 1], rmax[:, h:h + 1], -1.0, None, ALU.mult).then_inc(S3["max"], 1)

            def invert_sums(t):
                dve.wait_ge(S3["exp"], t * H + H)
                v.reciprocal(rinv[:, :], rsum[:, :]).then_inc(S3["inv"], 1)

            def scale_mixed(t):
                dve.wait_ge(S3["pv"], t * H + H)
                dve.wait_ge(S3["inv"], t + 1)
                v.tensor_tensor(mixed[:, :].rearrange("p (h k) -> p h k", h=H), ps[:, 6, :].rearrange("p (h k) -> p h k", h=H),
                                rinv[:, :].unsqueeze(2).broadcast_to([P, H, KD]), ALU.mult).then_inc(S3["mixed"], 1)

            def finish3(t):
                c = Chain(S3["chain"], t, 1)
                dve.wait_ge(S3["wo"], t + 1)
                v.tensor_tensor(res[:, :], ps[:, 7, 0:D], X[:, t, :], ALU.add).then_inc(S3["read"], 1)
                dve.wait_ge(S3["read"], t + 1)
                layernorm(S3, t, c, res[:, :], xnew[:, :])
                c.done()

            def body2(t, first, last):
                for h in range(H):
                    n = t * H + h
                    if h == 0 and not first:
                        scale_mixed(t - 1)
                    if h == H - 1:
                        invert_sums(t)
                        if not last:
                            make_mask(t + 1)
                    if h < H - 1 or not last:
                        mask_scores(n + 1, (h + 1) % H)
                    if h == 2 and not first:
                        finish3(t - 1)
                    for q in (0, 2):
                        dve.wait_ge(S3["trn0"], n * 2 + (q // 2 + 1))
                        v.tensor_copy(wtsT[:, q, :], ps[:, 4, :]).then_inc(S3["ev0"], 1)

            dve.wait_ge(S2["stored"], NT)
            make_mask(0)
            mask_scores(0, 0)
            body2(0, True, False)
            with dve.Fori(1, NT - 1) as t:
                body2(t, False, False)
            body2(NT - 1, False, True)
            scale_mixed(NT - 1)
            finish3(NT - 1)

            def row_max(s, t, k):
                dve.wait_ge(s["qk"], t + 1)
                v.tensor_reduce(nmax[:, k:k + 1], ps[:, 0:Q, :].rearrange("p q n -> p (q n)"), AX.X, ALU.max,
                                negate=True).then_inc(s["max"], 1)

            def weigh(s, t, k, r):
                dve.wait_ge(s["slab1"] if k else s["slab0"], r * 16 + 16)
                for q in range(Q):
                    b = q % 2
                    dve.wait_ge(s["trn1"] if b else s["trn0"], t * 2 + (q // 2 + 1))
                    v.tensor_tensor(wtsT[:, q, :], ps[:, 4 + b, :], slab[:, k, q * BANK:(q + 1) * BANK],
                                    ALU.mult).then_inc(s["ev1"] if b else s["ev0"], 1)

            def finish4(t, k, r):
                c = Chain(S4["chain"], t, 1)
                dve.wait_ge(S4["pv"], t + 1)
                c.then(v.reciprocal(rinv[:, 0:1], rsum[:, k:k + 1]))
                v.scalar_tensor_tensor(res[:, :], ps[:, 6, 0:D], rinv[:, 0:1], X[:, t, :], ALU.mult, ALU.add).then_inc(S4["read"], 1)
                dve.wait_ge(S4["read"], t + 1)
                dve.wait_ge(S4["turned"], t)
                dve.wait_ge(S4["stored"], t)
                v.scalar_tensor_tensor(xnew[:, :], res[:, :], SLOPE, res[:, :], ALU.mult, ALU.max).then_inc(S4["new"], 1)
                c.done()

            def finish5(t, k, r):
                c = Chain(S5["chain"], t, 4)
                dve.wait_ge(S5["pv"], t + 1)
                c.then(v.reciprocal(rinv[:, 0:1], rsum[:, k:k + 1]))
                v.scalar_tensor_tensor(res[:, :], ps[:, 6, 0:D], rinv[:, 0:1], X4[:, t, :], ALU.mult, ALU.add).then_inc(S5["read"], 1)
                dve.wait_ge(S5["read"], t + 1)
                c.then(v.scalar_tensor_tensor(res2[:, :], res[:, :], SLOPE, res[:, :], ALU.mult, ALU.max))
                c.then(v.tensor_tensor(res3[:, :], res2[:, :], X[:, t, :], ALU.add))
                if not (isinstance(r, int) and r == 0):
                    dve.wait_ge(S5["out1"] if k else S5["out0"], r * 16)
                layernorm(S5, t, c, res3[:, :], outt[:, k, :])
                c.done()

            def step3(s, finish):
                def body(t, k, r):
                    at = t if isinstance(t, int) else NT // 2
                    if at > 0:
                        finish(t - 1, 1 - k, r if k == 0 and False else (r if k else r - 1))
                    if at < NT - 1:
                        row_max(s, t + 1, 1 - k)
                    weigh(s, t, k, r)
                return body

            for s, prev, finish in ((S4, S3, finish4), (S5, S4, finish5)):
                dve.wait_ge(prev["stored"], NT)
                row_max(s, 0, 0)
                two_by_two(dve, step3(s, finish))
                finish(NT - 1, 1, NT // 2 - 1)


def kernel(x, adj, L0_gnn_W, L0_gnn_b, L1_gnn_W_sa, L1_gnn_a_sa, L1_gnn_W_gcnb, L1_gnn_b_gcnb, L1_gnn_Wa, L1_gnn_ba,
           L1_gnn_Wb, L1_gnn_bb, L2_gnn_Wks, L2_gnn_Wqs, L2_gnn_Wvs, L2_gnn_Wo, L3_gnn_W_stack):
    import numpy as np
    import concourse.bacc as bacc
    from concourse.bass_utils import run_bass_kernel_spmd

    x, adj = np.asarray(x), np.asarray(adj)
    Wa, Wb = np.asarray(L1_gnn_Wa), np.asarray(L1_gnn_Wb)

    def heads_side_by_side(a):
        return np.asarray(a).transpose(1, 0, 2).reshape(D, HD)

    arrays = {
        "x": x,
        "adj": adj.reshape(NT, P, N),
        "adjT": adj.reshape(NT, P, NT, P).transpose(0, 3, 2, 1).reshape(NT, P, N),
        "W0T": np.asarray(L0_gnn_W).T,
        "b0": np.asarray(L0_gnn_b),
        "W_sa": np.asarray(L1_gnn_W_sa),
        "a_sa": np.asarray(L1_gnn_a_sa).reshape(2 * D),
        "W_gates": np.concatenate([np.asarray(L1_gnn_W_gcnb), Wa[:, :D].T, Wb[:, :D].T, Wa[:, D:].T, Wb[:, D:].T], axis=1),
        "b_gcnb": np.asarray(L1_gnn_b_gcnb),
        "b_gates": np.concatenate([np.asarray(L1_gnn_ba), np.asarray(L1_gnn_bb)]),
        "Wk": heads_side_by_side(L2_gnn_Wks),
        "Wq": heads_side_by_side(L2_gnn_Wqs),
        "Wv": heads_side_by_side(L2_gnn_Wvs),
        "Wo": np.asarray(L2_gnn_Wo).reshape(HD, D),
        "W_stack": np.asarray(L3_gnn_W_stack),
    }
    arrays = {n: np.ascontiguousarray(a) for n, a in arrays.items()}
    nc = bacc.Bacc("TRN2", target_bir_lowering=False, num_devices=1)
    args = [nc.dram_tensor(n, a.shape, F32, kind="ExternalInput").ap() for n, a in arrays.items()]
    args_by_name = dict(zip(arrays, args))
    out = nc.dram_tensor("out", (NT, P, D), F32, kind="ExternalOutput").ap()
    graph_layers(nc, **args_by_name, out=out)
    r = run_bass_kernel_spmd(nc, [arrays], core_ids=[0])
    return r.results[0]["out"].reshape(N, D)
```

```python
from contextlib import ExitStack

import concourse.bass as bass
from concourse import mybir

F32 = mybir.dt.float32
I32 = mybir.dt.int32
ALU = mybir.AluOpType
ACT = mybir.ActivationFunctionType
AX = mybir.AxisListType

P = 128
N = 2048
D = 256
NT = N // P
DC = D // P
H = 8
KD = 64
HD = H * KD
HC = HD // P
BANK = 512
Q = 4
QT = NT // Q
GW = D + 4
HW = D + 2
EPS = 1e-5
SLOPE = 0.01
HUGE = 1e16
KEY_SCALE = 0.125
LEAST_SCORE = -88.0
WEIGHT_BOUND = 200.0


def graph_layers(nc, x, adj, adjT, W0T, b0, W_sa, a_sa, W_gates, b_gcnb, b_gates, Wk, Wq, Wv, Wo, W_stack, out):
    with ExitStack() as ctx:
        def sb(name, *shape):
            return ctx.enter_context(nc.sbuf_tensor(name, [P, *shape], F32))

        def sems(stage, *names):
            return {n: ctx.enter_context(nc.semaphore(f"{stage}_{n}")) for n in names}

        K = 1024
        base = -(-nc.sbuf_base // 32) * 32
        ctx.enter_context(nc.sbuf_tensor("arena", [P, 188 * K // 4], F32))

        def at(name, offset, *shape):
            return nc.alloc_sbuf_tensor_at(name, [P, *shape], F32, offset=base + offset)

        X = at("X", 0, NT, D)
        slab = at("slab", 16 * K, 2, N)
        wts = at("wts", 32 * K, 2, N)
        ws = at("ws", 48 * K, 2, DC, 2 * D)
        H0 = at("H0", 56 * K, NT, D)
        HA = at("HA", 88 * K, NT, HW)
        GB = at("GB", 88 * K + NT * HW * 4, NT, GW)
        left_rows = at("left_rows", 122 * K, N)
        KT3 = at("KT3", 152 * K, DC, N)
        V3 = at("V3", 168 * K, NT, D)
        x3 = at("x3", 56 * K, D)
        x3res = at("x3res", 80 * K, D)
        x3T = at("x3T", 57 * K, DC, P)
        kb = at("kb", 58 * K, HC, 2, P)
        vb = at("vb", 62 * K, HD)
        pb = at("pb", 64 * K, H, P)
        pbT = at("pbT", 68 * K, H, P)
        mb = at("mb", 72 * K, NT, P)
        KT2 = at("KT2", 56 * K, HC, N)
        V2 = at("V2", 88 * K, NT, HD)
        mask = slab[:, 1, :]
        wtsT = at("wtsT", 122 * K, Q, BANK)
        KT4 = at("KT4", 56 * K, DC, N)
        V4 = at("V4", 72 * K, NT, D)
        X4 = at("X4", 88 * K, NT, D)
        wk = at("wk", 130 * K, DC, HD)
        wq = at("wq", 134 * K, DC, HD)
        wv = at("wv", 138 * K, DC, HD)
        wo = at("wo", 142 * K, HC, D)
        w0 = at("w0", 146 * K, DC, D)
        wsa = at("wsa", 148 * K, DC, HW)
        b0r = at("b0r", 121 * K, D)
        bgr = at("bgr", 151 * K, D)
        wga = sb("wga", DC, GW)
        asr = at("asr", 184 * K, 2 * D)
        bar = sb("bar", 2)

        ident = sb("ident", P)
        minus_half = sb("minus_half", 1)
        right_cols = sb("right_cols", NT)
        xnew = sb("xnew", D)
        xnewT = sb("xnewT", DC, P)
        qT = sb("qT", HC, P)
        xq = at("xq", 186 * K, D)
        xqT = at("xqT", 187 * K, DC, P)
        left_wt = at("left_wt", 186 * K, DC, P)
        mixed = sb("mixed", HD)
        mixedT = sb("mixedT", HC, P)
        res = sb("res", D)
        res2 = sb("res2", D)
        res3 = sb("res3", D)
        outt = sb("outt", 2, D)
        bn = sb("bn", 6)
        mv = sb("mv", 2)
        veps = sb("veps", 1)
        rstd = sb("rstd", 1)
        bn3 = sb("bn3", 6)
        mv3 = sb("mv3", 2)
        veps3 = sb("veps3", 1)
        rstd3 = sb("rstd3", 1)
        wleft = sb("wleft", DC)
        g1 = sb("g1", 8)
        eye_less_one = sb("eye_less_one", P)
        rmax = sb("rmax", H)
        nmax = sb("nmax", H)
        rsum = sb("rsum", H)
        rinv = sb("rinv", H)
        block_max = sb("block_max", NT * NT)
        extremes = sb("extremes", 5)
        extremes_all = sb("extremes_all", 5)
        tests = sb("tests", 4)
        blocks_only = ctx.enter_context(nc.sbuf_tensor("blocks_only", [P, 1], I32))

        ps = ctx.enter_context(nc.psum_tensor("ps", [P, 8, BANK], F32))

        init = sems("init", "filled", "consts", "x0", "x", "early", "late")
        LN = ("chain", "stats", "var", "std", "new", "stored", "turned", "flat")
        S0 = sems("s0", "new", "turned", "flat", "proj", "kept")
        S1 = sems("s1", "slab0", "slab1", "agg", "read", *LN, "proj", "kept_h", "kept_g", "weights")
        S2 = sems("s2", "slab0", "slab1", "score", "raw", "exp", "edge", "agg", "read", "gate", "gexp", "z", "zexp", "mixing", *LN)
        B2 = sems("b2", "cleared", "qkv", "qflat", "kvkept", "scores", "max", "less", "exp", "sum", "inv", "pturned",
                  "pflat_a", "pflat_d", "ctx", "mixed", "mturned", "mflat", "wo", "res", "stats", "agg", "var", "std", "new",
                  "stored", "turned", "flat", "proj")
        BL = sems("adj", "blocks", "masked")
        FL = sems("flag", "seen", "cleared", "reduced", "all", "tests", "ready")
        ATT = ("slab0", "slab1", "xq", "xqturned", "xqflat", "query", "qkept", "qk", "max", "exp",
               "trn0", "trn1", "ev0", "ev1", "pv", "read")
        spare = list(B2.values())

        def sharing(*names):
            return {n: spare.pop() for n in names}

        S3 = sharing("waited", "rowmax", "step", "masked", "inv", "mixed", "mturned", "mflat", "wo", "slab0", "xq", "xqturned",
                     "xqflat", "query", "qkept", "qk", "max", "exp", "trn0", "trn1", "ev0", "ev1", "pv", "read")
        S3.update(sems("s3", "chain", "stats", "var", "std", "new", "stored"))
        PJ2 = sems("p2", "xq", "turned", "flat", "proj", "kept")
        PJ3 = sems("p3", "xq", "turned", "flat", "proj", "kept")
        L2 = sems("l2", "kept")
        S4 = sems("s4", *ATT, "chain", "new", "stored", "turned", "flat", "proj", "kept")
        S5 = sems("s5", "out0", "out1", *ATT, "chain", "stats", "var", "std", "new")

        def chosen(eng):
            eng.wait_ge(FL["ready"], 1)
            return eng.value_load(blocks_only[0:1, 0:1], min_val=0, max_val=1)

        def two_by_two(eng, body, stop=NT):
            for t in range(3):
                body(t, t % 2, t // 2)
            with eng.Fori(1, (stop - 4) // 2) as u:
                body(u * 2 + 1, 1, u)
                body(u * 2 + 2, 0, u + 1)
            for t in range(stop - 3, stop):
                body(t, t % 2, t // 2)

        def staggered(eng, body):
            for t in range(4):
                body(t, t % 2, t // 2)
            with eng.Fori(2, NT // 2 - 1) as u:
                body(u * 2, 0, u)
                body(u * 2 + 1, 1, u)
            for t in range(NT - 2, NT + 2):
                body(t, t % 2, t // 2)

        block = ctx.enter_context(nc.Block())

        @block.sync
        def _(sp):
            def split(a):
                return a.rearrange("(c p) n -> p c n", p=P)

            xv = x.rearrange("(t p) d -> p t d", p=P)
            sp.dma_start(X[:, 0:2, :], xv[:, 0:2, :]).then_inc(init["x0"], 16)
            sp.dma_start(w0[:, :, :], split(W0T)).then_inc(init["early"], 16)
            sp.dma_start(X[:, 2:NT, :], xv[:, 2:NT, :]).then_inc(init["x"], 16)
            sp.dma_start(b0r[:, :], b0.partition_broadcast(P)).then_inc(init["early"], 16)

            def load(s, src, t, k):
                sp.dma_start(slab[:, k, :], src[t]).then_inc(s["slab1"] if k else s["slab0"], 16)

            load(S1, adjT, 0, 0)
            load(S1, adjT, 1, 1)
            for dst, src in ((wsa[:, :, 0:D], split(W_sa)), (wga[:, :, :], split(W_gates)), (wk[:, :, :], split(Wk)),
                             (wq[:, :, :], split(Wq)), (wv[:, :, :], split(Wv)), (wo[:, :, :], split(Wo)),
                             (ws[:, 0], split(W_stack[0])), (ws[:, 1], split(W_stack[1])),
                             (bgr[:, :], b_gcnb.partition_broadcast(P)), (asr[:, :], a_sa.partition_broadcast(P)),
                             (bar[:, :], b_gates.partition_broadcast(P))):
                sp.dma_start(dst, src).then_inc(init["late"], 16)
            with sp.Fori(0, NT) as t:
                sp.dma_start(mb[:, t, :], adj[t, :, bass.ts(t, P)]).then_inc(BL["blocks"], 16)
            with sp.Fori(1, NT // 2) as u:
                for k in range(2):
                    sp.wait_ge(S1["agg"], u * 2 + k - 1)
                    sp.wait_ge(FL["seen"], u * 2 + k - 1)
                    load(S1, adjT, u * 2 + k, k)
            for k in range(2):
                sp.wait_ge(S1["agg"], NT - 1 + k)
                sp.wait_ge(FL["seen"], NT - 1 + k)
                load(S2, adjT, k, k)
            with sp.Fori(1, NT // 2) as u:
                for k in range(2):
                    sp.wait_ge(S2["agg"], u * 2 + k - 1)
                    load(S2, adjT, u * 2 + k, k)
            flag = chosen(sp)
            with sp.If(flag > 0):
                sp.wait_ge(S2["agg"], NT)
                load(S4, adjT, 0, 0)
                load(S4, adjT, 1, 1)
            with sp.Else():
                sp.wait_ge(S2["agg"], NT)
                load(S3, adj, 0, 0)
                with sp.Fori(1, NT) as t:
                    sp.wait_ge(S3["masked"], t)
                    load(S3, adj, t, 0)
                sp.wait_ge(S3["masked"], NT)
                load(S4, adjT, 0, 0)
                sp.wait_ge(S3["max"], NT * H)
                load(S4, adjT, 1, 1)
            with sp.Fori(1, NT // 2) as u:
                for k in range(2):
                    sp.wait_ge(S4["ev1"], u * 4 + (2 * k - 2))
                    load(S4, adjT, u * 2 + k, k)
            for k in range(2):
                sp.wait_ge(S4["ev1"], 2 * (NT - 1 + k))
                load(S5, adjT, k, k)

            def store(t, k):
                sp.wait_ge(S5["new"], t + 1)
                sp.dma_start(out[t], outt[:, k, :]).then_inc(S5["out1"] if k else S5["out0"], 16)

            with sp.Fori(1, NT // 2) as u:
                for k in range(2):
                    sp.wait_ge(S5["ev1"], u * 4 + (2 * k - 2))
                    load(S5, adjT, u * 2 + k, k)
                for k in range(2):
                    store(u * 2 + (k - 2), k)
            for k in range(2):
                store(NT - 2 + k, k)
            sp.wait_ge(S5["out0"], 16 * NT // 2)
            sp.wait_ge(S5["out1"], 16 * NT // 2)

        @block.gpsimd
        def _(pool):
            nc.gpsimd.memset(ident[:, :], 0.0).then_inc(init["filled"], 1)
            nc.gpsimd.memset(minus_half[:, :], -0.5).then_inc(init["consts"], 1)
            nc.gpsimd.memset(HA[:, :, D:HW], 1.0).then_inc(init["consts"], 1)
            nc.gpsimd.memset(eye_less_one[:, :], -1.0).then_inc(init["filled"], 1)
            pool.wait_ge(init["filled"], 2)
            nc.gpsimd.affine_select(out=ident[:, :], in_=ident[:, :], compare_op=ALU.not_equal, fill=1.0, base=0,
                                    pattern=[[-1, P]], channel_multiplier=1).then_inc(init["consts"], 1)
            nc.gpsimd.affine_select(out=eye_less_one[:, :], in_=eye_less_one[:, :], compare_op=ALU.not_equal, fill=0.0,
                                    base=0, pattern=[[-1, P]], channel_multiplier=1).then_inc(init["consts"], 1)

            pool.wait_ge(init["x0"], 16)
            nc.gpsimd.tensor_copy(xnew[:, :], X[:, 0, :]).then_inc(S0["new"], 1)
            nc.gpsimd.tensor_copy(xq[:, :], X[:, 1, :]).then_inc(S0["new"], 1)
            pool.wait_ge(init["x"], 16)
            with pool.Fori(1, NT // 2) as u:
                for k, to in enumerate((xnew, xq)):
                    pool.wait_ge(S0["turned"], u * 2 + (k - 1))
                    nc.gpsimd.tensor_copy(to[:, :], X[:, u * 2 + k, :]).then_inc(S0["new"], 1)

            def rsqrt(s, t):
                pool.wait_ge(s["var"], t + 1)
                nc.gpsimd.tensor_tensor(rstd[:, :], veps[:, :], minus_half[:, :], ALU.pow).then_inc(s["std"], 1)

            def store(s, t, to):
                pool.wait_ge(s["new"], t + 1)
                nc.gpsimd.tensor_copy(to[:, t, :], xnew[:, :]).then_inc(s["stored"], 1)

            def next_query(s, t, src):
                pool.wait_ge(s["xqturned"], t)
                nc.gpsimd.tensor_copy(xq[:, :], src[:, t, :]).then_inc(s["xq"], 1)

            pool.wait_ge(init["consts"], 4)
            with pool.Fori(0, NT) as t:
                rsqrt(S1, t)
                store(S1, t, X)

            pool.wait_ge(FL["reduced"], 1)
            nc.gpsimd.partition_all_reduce(extremes_all[:, :], extremes[:, :], P, bass.bass_isa.ReduceOp.max).then_inc(FL["all"], 1)

            def blocks_tile(t):
                at_t = t if isinstance(t, int) else NT // 2
                if at_t < NT:
                    rsqrt(S2, t)
                    store(S2, t, X)
                if at_t > 0:
                    pool.wait_ge(B2["var"], t)
                    nc.gpsimd.tensor_tensor(rstd3[:, :], veps3[:, :], minus_half[:, :], ALU.pow).then_inc(B2["std"], 1)
                    pool.wait_ge(B2["new"], t)
                    nc.gpsimd.tensor_copy(X[:, t - 1, :], x3[:, :]).then_inc(B2["stored"], 1)

            flag = chosen(pool)
            with pool.If(flag > 0):
                nc.gpsimd.memset(kb[:, :, :, :], 0.0).then_inc(B2["cleared"], 1)
                blocks_tile(0)
                with pool.Fori(1, NT) as t:
                    blocks_tile(t)
                blocks_tile(NT)
                pool.wait_ge(B2["stored"], NT)
            with pool.Else():
                with pool.Fori(0, NT) as t:
                    rsqrt(S2, t)
                    store(S2, t, X)

                def hand_tiles(s):
                    next_xq(s, "turned", 0, X)
                    with pool.Fori(1, NT) as t:
                        next_xq(s, "turned", t, X)

                def next_xq(s, turned, t, src):
                    pool.wait_ge(s[turned], t)
                    nc.gpsimd.tensor_copy(xq[:, :], src[:, t, :]).then_inc(s["xq"], 1)

                pool.wait_ge(S2["stored"], NT)
                hand_tiles(PJ2)
                pool.wait_ge(PJ2["turned"], NT)
                next_query(S3, 0, X)
                with pool.Fori(0, NT - 1) as t:
                    next_query(S3, t + 1, X)
                    rsqrt(S3, t)
                    store(S3, t, X)
                rsqrt(S3, NT - 1)
                store(S3, NT - 1, X)
                pool.wait_ge(S3["stored"], NT)
                hand_tiles(PJ3)
                pool.wait_ge(PJ3["turned"], NT)
            next_query(S4, 0, X)
            next_query(S4, 1, X)
            with pool.Fori(0, NT - 2) as t:
                next_query(S4, t + 2, X)
                store(S4, t, X4)
            store(S4, NT - 2, X4)
            store(S4, NT - 1, X4)
            pool.wait_ge(S4["stored"], NT)
            next_query(S5, 0, X4)
            next_query(S5, 1, X4)
            with pool.Fori(0, NT - 2) as t:
                next_query(S5, t + 2, X4)
                rsqrt(S5, t)
            rsqrt(S5, NT - 2)
            rsqrt(S5, NT - 1)

        @block.tensor
        def _(pe):
            mm = nc.tensor.matmul

            def turn_new(s, t):
                pe.wait_ge(s["new"], t + 1)
                for c in range(DC):
                    last = nc.tensor.transpose(ps[:, 7, c * P:(c + 1) * P], xnew[:, c * P:(c + 1) * P], ident[:, :])
                last.then_inc(s["turned"], 1)

            def rows(bank, col, wt, n):
                for c in range(DC):
                    last = mm(ps[:, bank, col:col + n], xnewT[:, c, :], wt[:, c, 0:n], start=(c == 0), stop=(c == DC - 1))
                return last

            def cols(bank, wt, first, chunks, xt):
                for o in range(chunks):
                    for c in range(DC):
                        last = mm(ps[:, bank, o * P:(o + 1) * P], wt[:, c, first + o * P:first + (o + 1) * P], xt[:, c, :],
                                  start=(c == 0), stop=(c == DC - 1))
                return last

            def turn0(t, k):
                pe.wait_ge(S0["new"], t + 1)
                if not (isinstance(t, int) and t < 2):
                    pe.wait_ge(S0["flat"], t - 1)
                src = xq if k else xnew
                for c in range(DC):
                    last = nc.tensor.transpose(ps[:, 7 - k, c * P:(c + 1) * P], src[:, c * P:(c + 1) * P], ident[:, :])
                last.then_inc(S0["turned"], 1)

            def products0(t, k):
                pe.wait_ge(S0["flat"], t + 1)
                if not (isinstance(t, int) and t < 2):
                    pe.wait_ge(S0["kept"], t - 1)
                src = xqT if k else xnewT
                for c in range(DC):
                    last = mm(ps[:, 5 - k, 0:D], src[:, c, :], w0[:, c, :], start=(c == 0), stop=(c == DC - 1))
                last.then_inc(S0["proj"], 1)

            pe.wait_ge(init["consts"], 4)
            turn0(0, 0)
            turn0(1, 1)
            pe.wait_ge(init["early"], 32)
            products0(0, 0)
            turn0(2, 0)
            products0(1, 1)
            with pe.Fori(1, NT // 2 - 1) as u:
                for k in range(2):
                    turn0(u * 2 + (k + 1), 1 - k)
                    products0(u * 2 + k, k)
            turn0(NT - 1, 1)
            products0(NT - 2, 0)
            products0(NT - 1, 1)

            def agg0(t, k, r, q):
                if q == 0:
                    pe.wait_ge(S1["slab1"] if k else S1["slab0"], r * 16 + 16)
                    if not (isinstance(t, int) and t < 2):
                        pe.wait_ge(S1["read"], t - 1)
                for j in range(q * QT, q * QT + QT):
                    last = mm(ps[:, k, 0:D], slab[:, k, j * P:(j + 1) * P], H0[:, j, :], start=(j == 0), stop=(j == NT - 1))
                if q == Q - 1:
                    last.then_inc(S1["agg"], 1)

            def products1(t):
                pe.wait_ge(S1["flat"], t + 1)
                if not (isinstance(t, int) and t == 0):
                    pe.wait_ge(S1["kept_h"], t)
                    pe.wait_ge(S1["kept_g"], t)
                rows(5, 0, wsa, D + 1)
                for c in range(DC):
                    mm(ps[:, 4, 0:P], left_wt[:, c, :], xnewT[:, c, :], start=(c == 0), stop=(c == DC - 1))
                rows(6, 0, wga, GW).then_inc(S1["proj"], 1)

            def stage1(t, k, r):
                agg0(t, k, r, 0)
                agg0(t, k, r, 1)
                turn_new(S1, t - 1)
                agg0(t, k, r, 2)
                products1(t - 1)
                agg0(t, k, r, 3)

            pe.wait_ge(S0["kept"], NT)
            for q in range(Q):
                agg0(0, 0, 0, q)
            pe.wait_ge(init["late"], 16 * 11)
            pe.wait_ge(S1["weights"], 3 * DC)
            stage1(1, 1, 0)
            with pe.Fori(1, NT // 2) as u:
                stage1(u * 2, 0, u)
                stage1(u * 2 + 1, 1, u)
            turn_new(S1, NT - 1)
            products1(NT - 1)

            def agg_gates(t, k, r, q):
                if q == 0:
                    pe.wait_ge(S2["slab1"] if k else S2["slab0"], r * 16 + 16)
                    if not (isinstance(t, int) and t < 2):
                        pe.wait_ge(S2["read"], t - 1)
                for j in range(q * QT, q * QT + QT):
                    mm(ps[:, 2 + k, 0:D + 2], slab[:, k, j * P:(j + 1) * P], GB[:, j, 0:D + 2], start=(j == 0), stop=(j == NT - 1))

            def agg_edges(t, k, q):
                if q == 0:
                    pe.wait_ge(S2["edge"], t + 1)
                for j in range(q * QT, q * QT + QT):
                    last = mm(ps[:, k, 0:D + 1], wts[:, k, j * P:(j + 1) * P], HA[:, j, 0:D + 1], start=(j == 0), stop=(j == NT - 1))
                if q == Q - 1:
                    last.then_inc(S2["agg"], 1)

            def block_qkv(t):
                pe.wait_ge(S2["flat"], t + 1)
                cols(4, wq, 0, HC, xnewT).then_inc(B2["qkv"], 1)
                cols(6, wk, 0, HC, xnewT).then_inc(B2["qkv"], 1)
                rows(7, 0, wv, HD).then_inc(B2["qkv"], 1)

            def block_scores(t):
                pe.wait_ge(B2["qflat"], t + 1)
                pe.wait_ge(B2["kvkept"], t + 1)
                for c in range(HC):
                    last = mm(ps[:, 6 + c // 2, c % 2 * 2 * P:(c % 2 + 1) * 2 * P], qT[:, c, :],
                              kb[:, c, :, :].rearrange("p a n -> p (a n)"), start=True, stop=True)
                last.then_inc(B2["scores"], 1)

            def block_turn_weights(t):
                pe.wait_ge(B2["exp"], t + 1)
                for h in range(H):
                    last = nc.tensor.transpose(ps[:, 6 + h // 4, h % 4 * P:(h % 4 + 1) * P], pb[:, h, :], ident[:, :])
                last.then_inc(B2["pturned"], 1)

            def block_mix(t):
                pe.wait_ge(B2["pflat_a"], t + 1)
                pe.wait_ge(B2["pflat_d"], t + 1)
                for h in range(H):
                    last = mm(ps[:, 4, h * KD:(h + 1) * KD], pbT[:, h, :], vb[:, h * KD:(h + 1) * KD], start=True, stop=True)
                last.then_inc(B2["ctx"], 1)

            def block_turn_mixed(t):
                if not (isinstance(t, int) and t == 0):
                    pe.wait_ge(L2["kept"], t)
                pe.wait_ge(B2["mixed"], t + 1)
                for c in range(HC):
                    last = nc.tensor.transpose(ps[:, 5, c * P:(c + 1) * P], mixed[:, c * P:(c + 1) * P], ident[:, :])
                last.then_inc(B2["mturned"], 1)

            def block_out(t):
                pe.wait_ge(B2["mflat"], t + 1)
                for c in range(HC):
                    last = mm(ps[:, 6, 0:D], mixedT[:, c, :], wo[:, c, :], start=(c == 0), stop=(c == HC - 1))
                last.then_inc(B2["wo"], 1)

            def block_turn_new(t):
                pe.wait_ge(B2["new"], t + 1)
                for c in range(DC):
                    last = nc.tensor.transpose(ps[:, 5, c * P:(c + 1) * P], x3[:, c * P:(c + 1) * P], ident[:, :])
                last.then_inc(B2["turned"], 1)

            def block_products(t):
                pe.wait_ge(B2["flat"], t + 1)
                cols(5, ws[:, 0], D, DC, x3T)
                for c in range(DC):
                    last = mm(ps[:, 5, D:2 * D], x3T[:, c, :], ws[:, 0][:, c, 0:D], start=(c == 0), stop=(c == DC - 1))
                last.then_inc(B2["proj"], 1)

            def stage2_blocks(t, k, r):
                at = t if isinstance(t, int) else NT // 2
                now, after1, after2 = at < NT, 0 < at <= NT, 1 < at
                if at == 0:
                    for q in range(Q):
                        agg_edges(t, k, q)
                    return
                if now:
                    agg_gates(t, k, r, 0)
                    agg_gates(t, k, r, 1)
                if after2:
                    block_turn_weights(t - 2)
                if now:
                    agg_gates(t, k, r, 2)
                if after2:
                    block_mix(t - 2)
                if now:
                    agg_gates(t, k, r, 3)
                if after2:
                    block_turn_mixed(t - 2)
                if now:
                    agg_edges(t, k, 0)
                if after2:
                    block_out(t - 2)
                if after1:
                    turn_new(S2, t - 1)
                if now:
                    agg_edges(t, k, 1)
                if after1:
                    if after2:
                        pe.wait_ge(B2["res"], t - 1)
                    block_qkv(t - 1)
                if after2:
                    block_turn_new(t - 2)
                if now:
                    agg_edges(t, k, 2)
                if after2:
                    block_products(t - 2)
                if after1:
                    block_scores(t - 1)
                if now:
                    agg_edges(t, k, 3)

            def turn_query(s, t):
                pe.wait_ge(s["xq"], t + 1)
                for c in range(DC):
                    last = nc.tensor.transpose(ps[:, 7, c * P:(c + 1) * P], xq[:, c * P:(c + 1) * P], ident[:, :])
                last.then_inc(s["xqturned"], 1)

            def query(s, t, wt, chunks):
                pe.wait_ge(s["xqflat"], t + 1)
                cols(7, wt, 0, chunks, xqT).then_inc(s["query"], 1)

            def turn(s, n, q, k):
                if q == 0:
                    pe.wait_ge(s["exp"], n + 1)
                b = q % 2
                pe.wait_ge(s["ev1"] if b else s["ev0"], n * 2 + q // 2)
                for j in range(QT):
                    last = nc.tensor.transpose(ps[:, 4 + b, j * P:(j + 1) * P],
                                               wts[:, k, (q * QT + j) * P:(q * QT + j + 1) * P], ident[:, :])
                last.then_inc(s["trn1"] if b else s["trn0"], 1)

            def mix(s, n, q, v, lo, width):
                b = q % 2
                pe.wait_ge(s["ev1"] if b else s["ev0"], n * 2 + (q // 2 + 1))
                for j in range(QT):
                    jt = q * QT + j
                    last = mm(ps[:, 6, lo:lo + width], wtsT[:, q, j * P:(j + 1) * P], v[:, jt, lo:lo + width],
                              start=(jt == 0), stop=(jt == NT - 1))
                if q == Q - 1:
                    last.then_inc(s["pv"], 1)

            def scores2(t, h):
                if h == 0:
                    pe.wait_ge(S3["qkept"], t + 1)
                pe.wait_ge(S3["max"], t * H + h)
                lo = h % 2 * KD
                for q in range(Q):
                    last = mm(ps[:, q, :], qT[lo:lo + KD, h // 2, :], KT2[lo:lo + KD, h // 2, q * BANK:(q + 1) * BANK],
                              start=True, stop=True)
                last.then_inc(S3["qk"], 1)

            def turn_mixed(t):
                pe.wait_ge(S3["mixed"], t + 1)
                for c in range(HC):
                    last = nc.tensor.transpose(ps[:, 7, c * P:(c + 1) * P], mixed[:, c * P:(c + 1) * P], ident[:, :])
                last.then_inc(S3["mturned"], 1)

            def project_mixed(t):
                pe.wait_ge(S3["mflat"], t + 1)
                for c in range(HC):
                    last = mm(ps[:, 7, 0:D], mixedT[:, c, :], wo[:, c, :], start=(c == 0), stop=(c == HC - 1))
                last.then_inc(S3["wo"], 1)

            def next_products(s, t, wt):
                pe.wait_ge(s["flat"], t + 1)
                cols(7, wt, D, DC, xnewT)
                for c in range(DC):
                    last = mm(ps[:, 7, D:2 * D], xnewT[:, c, :], wt[:, c, 0:D], start=(c == 0), stop=(c == DC - 1))
                last.then_inc(s["proj"], 1)

            def body2(t, first, last):
                for h in range(H):
                    n = t * H + h
                    if h < H - 1:
                        scores2(t, h + 1)
                    elif not last:
                        scores2(t + 1, 0)
                    if h == 0 and not first:
                        turn_mixed(t - 1)
                    if h == 1 and not first:
                        project_mixed(t - 1)
                    if h == 5 and not last:
                        if not first:
                            pe.wait_ge(S3["read"], t)
                        turn_query(S3, t + 1)
                    if h == 6 and not last:
                        query(S3, t + 1, wq, HC)
                    lo = h * KD
                    turn(S3, n, 0, h % 2)
                    turn(S3, n, 1, h % 2)
                    mix(S3, n, 0, V2, lo, KD)
                    turn(S3, n, 2, h % 2)
                    mix(S3, n, 1, V2, lo, KD)
                    turn(S3, n, 3, h % 2)
                    mix(S3, n, 2, V2, lo, KD)
                    mix(S3, n, 3, V2, lo, KD)

            def product_pass(s, products):
                def tile(t, first):
                    pe.wait_ge(s["xq"], t + 1)
                    if not first:
                        pe.wait_ge(s["kept"], t)
                    for c in range(DC):
                        last = nc.tensor.transpose(ps[:, 7, c * P:(c + 1) * P], xq[:, c * P:(c + 1) * P], ident[:, :])
                    last.then_inc(s["turned"], 1)
                    pe.wait_ge(s["flat"], t + 1)
                    products().then_inc(s["proj"], 1)

                tile(0, True)
                with pe.Fori(1, NT) as t:
                    tile(t, False)
                pe.wait_ge(s["kept"], NT)

            def products2():
                cols(5, wk, 0, HC, xnewT)
                return rows(6, 0, wv, HD)

            def products3():
                cols(5, ws[:, 0], D, DC, xnewT)
                return rows(6, 0, ws[:, 0], D)

            def general_layer2():
                pe.wait_ge(S2["read"], NT)
                product_pass(PJ2, products2)
                turn_query(S3, 0)
                query(S3, 0, wq, HC)
                scores2(0, 0)
                body2(0, True, False)
                with pe.Fori(1, NT - 1) as t:
                    body2(t, False, False)
                body2(NT - 1, False, True)
                turn_mixed(NT - 1)
                project_mixed(NT - 1)
                product_pass(PJ3, products3)

            pe.wait_ge(S1["kept_g"], NT)
            for q in range(Q):
                agg_gates(0, 0, 0, q)
            pe.wait_ge(S1["kept_h"], NT)
            flag = chosen(pe)
            with pe.If(flag > 0):
                staggered(pe, stage2_blocks)
            with pe.Else():
                def stage2_alone(t, k, r):
                    for q in range(Q):
                        agg_gates(t, k, r, q)
                    for q in range(Q):
                        agg_edges(t, k, q)

                for q in range(Q):
                    agg_edges(0, 0, q)
                stage2_alone(1, 1, 0)
                with pe.Fori(1, NT // 2) as u:
                    stage2_alone(u * 2, 0, u)
                    stage2_alone(u * 2 + 1, 1, u)
                general_layer2()

            def scores3(s, t, kt):
                pe.wait_ge(s["qkept"], t + 1)
                pe.wait_ge(s["exp"], t)
                for c in range(DC):
                    for q in range(Q):
                        last = mm(ps[:, q, :], qT[:, c, :], kt[:, c, q * BANK:(q + 1) * BANK],
                                  start=(c == 0), stop=(c == DC - 1))
                last.then_inc(s["qk"], 1)

            def step3(s, kt, v, wt, wnext):
                def body(t, k, r):
                    at = t if isinstance(t, int) else NT // 2
                    turn(s, t, 0, k)
                    turn(s, t, 1, k)
                    if at < NT - 1:
                        scores3(s, t + 1, kt)
                    if at > 0:
                        if wnext is not None:
                            if at > 1:
                                pe.wait_ge(s["kept"], t - 1)
                            turn_new(s, t - 1)
                        pe.wait_ge(s["read"], t)
                    mix(s, t, 0, v, 0, D)
                    turn(s, t, 2, k)
                    if at > 0 and wnext is not None:
                        next_products(s, t - 1, wnext)
                    mix(s, t, 1, v, 0, D)
                    turn(s, t, 3, k)
                    if at < NT - 2:
                        if at > 0 and wnext is not None:
                            pe.wait_ge(s["kept"], t)
                        turn_query(s, t + 2)
                    mix(s, t, 2, v, 0, D)
                    if at < NT - 2:
                        query(s, t + 2, wt, DC)
                    mix(s, t, 3, v, 0, D)
                return body

            for s, prev, kt, v, wt, wnext in ((S4, L2, KT3, V3, ws[:, 0], ws[:, 1]), (S5, S4, KT4, V4, ws[:, 1], None)):
                pe.wait_ge(prev["kept"], NT)
                turn_query(s, 0)
                query(s, 0, wt, DC)
                scores3(s, 0, kt)
                turn_query(s, 1)
                query(s, 1, wt, DC)
                two_by_two(pe, step3(s, kt, v, wt, wnext))
                if wnext is not None:
                    pe.wait_ge(s["kept"], NT - 1)
                    turn_new(s, NT - 1)
                    next_products(s, NT - 1, wnext)

        @block.scalar
        def _(act):
            def flatten(s, t):
                act.wait_ge(s["turned"], t + 1)
                nc.scalar.copy(xnewT[:, :, :].rearrange("p c n -> p (c n)"), ps[:, 7, 0:D]).then_inc(s["flat"], 1)

            with act.Fori(0, NT // 2) as u:
                for k, to in enumerate((xnewT, xqT)):
                    act.wait_ge(S0["turned"], u * 2 + (k + 1))
                    nc.scalar.copy(to[:, :, :].rearrange("p c n -> p (c n)"), ps[:, 7 - k, 0:D]).then_inc(S0["flat"], 1)

            with act.Fori(0, NT) as t:
                flatten(S1, t)
                act.wait_ge(S1["proj"], t + 1)
                nc.scalar.copy(left_rows[:, bass.ts(t, P)], ps[:, 4, 0:P])
                nc.scalar.copy(GB[:, t, :], ps[:, 6, 0:GW]).then_inc(S1["kept_g"], 1)

            def edge_exp(t, k):
                act.wait_ge(S2["raw"], t + 1)
                nc.scalar.activation(wts[:, k, :], wts[:, k, :], ACT.Exp, scale=-1.0).then_inc(S2["exp"], 1)

            def gate_exp(t):
                act.wait_ge(S2["gate"], t + 1)
                nc.scalar.activation(g1[:, 4:6], g1[:, 2:4], ACT.Exp, scale=-1.0).then_inc(S2["gexp"], 1)

            def z_exp(t):
                act.wait_ge(S2["z"], t + 1)
                nc.scalar.activation(res2[:, :], res3[:, :], ACT.Exp, scale=-1.0).then_inc(S2["zexp"], 1)

            def flat2(a):
                return a.rearrange("p c n -> p (c n)")

            def stage2_blocks(t, k, r):
                at = t if isinstance(t, int) else NT // 2
                now, after1, after2 = at < NT, 0 < at <= NT, 1 < at
                if after2:
                    act.wait_ge(B2["pturned"], t - 1)
                    nc.scalar.copy(flat2(pbT[:, 4:8, :]), ps[:, 7, :]).then_inc(B2["pflat_a"], 1)
                if after1:
                    gate_exp(t - 1)
                    z_exp(t - 1)
                if after2:
                    act.wait_ge(B2["mturned"], t - 1)
                    nc.scalar.copy(flat2(mixedT[:, :, :]), ps[:, 5, :]).then_inc(B2["mflat"], 1)
                if after1:
                    flatten(S2, t - 1)
                    act.wait_ge(B2["qkv"], t * 3 - 2)
                    nc.scalar.activation(flat2(qT[:, :, :]), ps[:, 4, :], ACT.Copy, scale=KEY_SCALE).then_inc(B2["qflat"], 1)
                    act.wait_ge(B2["qkv"], t * 3 - 1)
                    for a in range(2):
                        half = slice(a * KD, (a + 1) * KD)
                        nc.scalar.copy(kb[half, :, a, :], ps[half, 6, :].rearrange("p (c n) -> p c n", c=HC))
                    act.wait_ge(B2["qkv"], t * 3)
                    nc.scalar.copy(vb[:, :], ps[:, 7, :]).then_inc(B2["kvkept"], 1)
                if after2:
                    act.wait_ge(B2["turned"], t - 1)
                    nc.scalar.copy(flat2(x3T[:, :, :]), ps[:, 5, 0:D]).then_inc(B2["flat"], 1)
                if at < NT - 1:
                    edge_exp(t + 1, 1 - k)
                if after2:
                    act.wait_ge(B2["proj"], t - 1)
                    nc.scalar.copy(KT3[:, :, bass.ts(t - 2, P)], ps[:, 5, 0:D].rearrange("p (c n) -> p c n", c=DC))
                    nc.scalar.copy(V3[:, t - 2, :], ps[:, 5, D:2 * D]).then_inc(L2["kept"], 1)
                if after1:
                    act.wait_ge(B2["less"], t)
                    nc.scalar.activation(flat2(pb[:, :, :]), flat2(pb[:, :, :]), ACT.Exp).then_inc(B2["exp"], 1)

            def flatten_query(s, t):
                act.wait_ge(s["xqturned"], t + 1)
                nc.scalar.copy(xqT[:, :, :].rearrange("p c n -> p (c n)"), ps[:, 7, 0:D]).then_inc(s["xqflat"], 1)

            def keep_query(s, t, width, scale):
                act.wait_ge(s["query"], t + 1)
                nc.scalar.activation(qT[:, :, :].rearrange("p c n -> p (c n)")[:, 0:width], ps[:, 7, 0:width], ACT.Copy,
                                     scale=scale).then_inc(s["qkept"], 1)

            def keep_next(s, t, kt, v):
                act.wait_ge(s["proj"], t + 1)
                nc.scalar.copy(kt[:, :, bass.ts(t, P)], ps[:, 7, 0:D].rearrange("p (c n) -> p c n", c=DC))
                nc.scalar.copy(v[:, t, :], ps[:, 7, D:2 * D]).then_inc(s["kept"], 1)

            def exp2(n, h):
                act.wait_ge(S3["max"], n + 1)
                nc.scalar.activation(wts[:, h % 2, :], wts[:, h % 2, :], ACT.Exp, bias=nmax[:, h:h + 1],
                                     accum_out=rsum[:, h:h + 1]).then_inc(S3["exp"], 1)

            def flatten_mixed(t):
                act.wait_ge(S3["mturned"], t + 1)
                nc.scalar.copy(mixedT[:, :, :].rearrange("p c n -> p (c n)"), ps[:, 7, :]).then_inc(S3["mflat"], 1)

            def body2(t, first, last):
                for h in range(H):
                    n = t * H + h
                    if h < H - 1 or not last:
                        exp2(n + 1, (h + 1) % H)
                    if h == 0 and not first:
                        flatten_mixed(t - 1)
                    if h == 5 and not last:
                        flatten_query(S3, t + 1)
                    if h == 6 and not last:
                        keep_query(S3, t + 1, HD, KEY_SCALE)
                    for q in (1, 3):
                        act.wait_ge(S3["trn1"], n * 2 + (q // 2 + 1))
                        nc.scalar.copy(wtsT[:, q, :], ps[:, 5, :]).then_inc(S3["ev1"], 1)

            def general_layer2():
                edge_exp(1, 1)
                gate_exp(0)
                z_exp(0)
                with act.Fori(1, NT // 2) as u:
                    edge_exp(u * 2, 0)
                    gate_exp(u * 2 - 1)
                    z_exp(u * 2 - 1)
                    edge_exp(u * 2 + 1, 1)
                    gate_exp(u * 2)
                    z_exp(u * 2)
                gate_exp(NT - 1)
                z_exp(NT - 1)
                act.wait_ge(BL["blocks"], 16 * NT)
                act.wait_ge(S2["read"], NT)
                with act.Fori(0, NT) as t:
                    flatten(PJ2, t)
                    act.wait_ge(PJ2["proj"], t + 1)
                    nc.scalar.copy(KT2[:, :, bass.ts(t, P)], ps[:, 5, :].rearrange("p (c n) -> p c n", c=HC))
                    nc.scalar.copy(V2[:, t, :], ps[:, 6, :]).then_inc(PJ2["kept"], 1)
                flatten_query(S3, 0)
                keep_query(S3, 0, HD, KEY_SCALE)
                exp2(0, 0)
                body2(0, True, False)
                with act.Fori(1, NT - 1) as t:
                    body2(t, False, False)
                body2(NT - 1, False, True)
                flatten_mixed(NT - 1)
                with act.Fori(0, NT) as t:
                    flatten(PJ3, t)
                    act.wait_ge(PJ3["proj"], t + 1)
                    nc.scalar.copy(KT3[:, :, bass.ts(t, P)], ps[:, 5, 0:D].rearrange("p (c n) -> p c n", c=DC))
                    nc.scalar.copy(V3[:, t, :], ps[:, 6, 0:D]).then_inc(PJ3["kept"], 1)
                    act.wait_ge(PJ3["kept"], t + 1)
                    act.sem_inc(L2["kept"], 1)

            edge_exp(0, 0)
            flag = chosen(act)
            with act.If(flag > 0):
                act.wait_ge(B2["cleared"], 1)
                staggered(act, stage2_blocks)
            with act.Else():
                general_layer2()

            def exp3(s, t, k):
                act.wait_ge(s["max"], t + 1)
                if not (isinstance(t, int) and t < 2):
                    act.wait_ge(s["trn1"], t * 2 - 2)
                nc.scalar.activation(wts[:, k, :], ps[:, 0:Q, :].rearrange("p q n -> p (q n)"), ACT.Exp,
                                     bias=nmax[:, k:k + 1], accum_out=rsum[:, k:k + 1]).then_inc(s["exp"], 1)

            def step3(s, nxt):
                def body(t, k, r):
                    at = t if isinstance(t, int) else NT // 2
                    if at < NT - 1:
                        exp3(s, t + 1, 1 - k)
                    if at > 0 and nxt is not None:
                        flatten(s, t - 1)
                        keep_next(s, t - 1, *nxt)
                    if at < NT - 2:
                        flatten_query(s, t + 2)
                        keep_query(s, t + 2, D, 1.0)
                return body

            for s, nxt in ((S4, (KT4, V4)), (S5, None)):
                flatten_query(s, 0)
                keep_query(s, 0, D, 1.0)
                exp3(s, 0, 0)
                flatten_query(s, 1)
                keep_query(s, 1, D, 1.0)
                two_by_two(act, step3(s, nxt))
                if nxt is not None:
                    flatten(s, NT - 1)
                    keep_next(s, NT - 1, *nxt)

        @block.vector
        def _(dve):
            v = nc.vector

            class Chain:
                def __init__(self, s, t, per_tile):
                    self.sem, self.base, self.per_tile, self.n = s, t * per_tile, per_tile, 0

                def then(self, instruction):
                    instruction.then_inc(self.sem, 1)
                    self.n += 1
                    dve.wait_ge(self.sem, self.base + self.n)

                def done(self):
                    assert self.n == self.per_tile, self.n

            def layernorm(s, t, c, src, dst):
                v.bn_stats(bn[:, :], src).then_inc(s["stats"], 1)
                dve.wait_ge(init["early"], 32)
                dve.wait_ge(s["stats"], t + 1)
                c.then(v.bn_aggr(mv[:, :], bn[:, :]))
                v.tensor_scalar(veps[:, :], mv[:, 1:2], EPS, None, ALU.add).then_inc(s["var"], 1)
                dve.wait_ge(s["std"], t + 1)
                v.tensor_scalar(dst, src, mv[:, 0:1], rstd[:, :], ALU.subtract, ALU.mult).then_inc(s["new"], 1)

            dve.wait_ge(init["early"], 32)
            with dve.Fori(0, NT // 2) as u:
                for k in range(2):
                    dve.wait_ge(S0["proj"], u * 2 + (k + 1))
                    v.tensor_tensor(H0[:, u * 2 + k, :], ps[:, 5 - k, 0:D], b0r[:, :], ALU.add).then_inc(S0["kept"], 1)

            dve.wait_ge(init["late"], 16 * 11)
            dve.wait_ge(init["consts"], 4)
            for c in range(DC):
                v.scalar_tensor_tensor(res[:, :], wsa[:, c, 0:D], 1.0, asr[:, 0:D], ALU.mult, ALU.mult,
                                       accum_out=wleft[:, c:c + 1]).then_inc(S1["weights"], 1)
                dve.wait_ge(S1["weights"], 2 * c + 1)
                v.scalar_tensor_tensor(res[:, :], wsa[:, c, 0:D], 1.0, asr[:, D:2 * D], ALU.mult, ALU.mult,
                                       accum_out=wsa[:, c, D:D + 1]).then_inc(S1["weights"], 1)
                dve.wait_ge(S1["weights"], 2 * c + 2)
            for c in range(DC):
                v.tensor_scalar(left_wt[:, c, :], ident[:, :], 0.0, wleft[:, c:c + 1], ALU.mult,
                                ALU.add).then_inc(S1["weights"], 1)

            for i, wt in ((1, wq), (3, wk)):
                v.tensor_reduce(extremes[:, i:i + 1], wt[:, :, :].rearrange("p c n -> p (c n)"), AX.X, ALU.max)
                v.tensor_reduce(extremes[:, i + 1:i + 2], wt[:, :, :].rearrange("p c n -> p (c n)"), AX.X, ALU.min, negate=True)

            def stage1(t, k, r):
                c = Chain(S1["chain"], t, 1)
                dve.wait_ge(S1["agg"], t + 1)
                v.tensor_tensor(res[:, :], ps[:, k, 0:D], X[:, t, :], ALU.add).then_inc(S1["read"], 1)
                dve.wait_ge(S1["read"], t + 1)
                if not (isinstance(t, int) and t == 0):
                    dve.wait_ge(S1["turned"], t)
                    dve.wait_ge(S1["stored"], t)
                layernorm(S1, t, c, res[:, :], xnew[:, :])
                dve.wait_ge(S1["slab1"] if k else S1["slab0"], r * 16 + 16)
                v.tensor_reduce(block_max[:, bass.ts(t, NT)], slab[:, k, :].rearrange("p (j n) -> p j n", j=NT), AX.X,
                                ALU.max).then_inc(FL["seen"], 1)
                dve.wait_ge(S1["proj"], t + 1)
                v.tensor_copy(HA[:, t, 0:D], ps[:, 5, 0:D])
                v.tensor_copy(right_cols[:, bass.ts(t, 1)], ps[:, 5, D:D + 1]).then_inc(S1["kept_h"], 1)
                c.done()

            flat_masks = mb[:, :, :].rearrange("p t n -> p (t n)")
            dve.wait_ge(BL["blocks"], 16 * NT)
            v.tensor_scalar(flat_masks, flat_masks, 0.0, -1.0, ALU.max, ALU.add).then_inc(BL["masked"], 1)
            stage1(0, 0, 0)
            dve.wait_ge(BL["masked"], 1)
            v.tensor_tensor(mb[:, :, :], mb[:, :, :], eye_less_one[:, :].unsqueeze(1).broadcast_to([P, NT, P]),
                            ALU.max).then_inc(BL["masked"], 1)
            stage1(1, 1, 0)
            dve.wait_ge(BL["masked"], 2)
            v.tensor_scalar(flat_masks, flat_masks, HUGE, None, ALU.mult).then_inc(BL["masked"], 1)
            with dve.Fori(1, NT // 2) as u:
                stage1(u * 2, 0, u)
                stage1(u * 2 + 1, 1, u)

            def edges(t, k, r):
                w3 = wts[:, k, :].rearrange("p (j n) -> p j n", j=NT)
                if not (isinstance(t, int) and t < 2):
                    dve.wait_ge(S2["agg"], t - 1)
                v.tensor_tensor(w3, left_rows[:, bass.ts(t, P)].unsqueeze(1).broadcast_to([P, NT, P]),
                                right_cols[:, :].unsqueeze(2).broadcast_to([P, NT, P]), ALU.add).then_inc(S2["score"], 1)
                dve.wait_ge(S2["score"], t * 2 + 1)
                v.scalar_tensor_tensor(wts[:, k, :], wts[:, k, :], SLOPE, wts[:, k, :], ALU.mult, ALU.max).then_inc(S2["score"], 1)
                dve.wait_ge(S2["score"], t * 2 + 2)
                v.tensor_scalar(wts[:, k, :], wts[:, k, :], LEAST_SCORE, None, ALU.max).then_inc(S2["raw"], 1)
                dve.wait_ge(S2["exp"], t + 1)
                dve.wait_ge(S2["slab1"] if k else S2["slab0"], r * 16 + 16)
                v.scalar_tensor_tensor(wts[:, k, :], slab[:, k, :], 0.0, wts[:, k, :], ALU.not_equal, ALU.mult).then_inc(S2["edge"], 1)

            def mix_gates2(t, k):
                c = Chain(S2["mixing"], t, 7)
                dve.wait_ge(S2["agg"], t + 1)
                c.then(v.tensor_scalar(g1[:, 0:1], ps[:, k, D:D + 1], EPS, None, ALU.add))
                c.then(v.reciprocal(g1[:, 1:2], g1[:, 0:1]))
                c.then(v.tensor_tensor(g1[:, 2:4], ps[:, 2 + k, D:D + 2], GB[:, t, D + 2:GW], ALU.add))
                v.tensor_tensor(g1[:, 2:4], g1[:, 2:4], bar[:, :], ALU.add).then_inc(S2["gate"], 1)
                dve.wait_ge(S2["gexp"], t + 1)
                c.then(v.tensor_scalar(g1[:, 4:6], g1[:, 4:6], 1.0, None, ALU.add))
                c.then(v.reciprocal(g1[:, 6:8], g1[:, 4:6]))
                c.then(v.tensor_tensor(g1[:, 0:1], g1[:, 6:7], g1[:, 1:2], ALU.mult))
                c.then(v.tensor_tensor(res[:, :], ps[:, 2 + k, 0:D], bgr[:, :], ALU.add))
                v.tensor_scalar(res2[:, :], ps[:, k, 0:D], g1[:, 0:1], None, ALU.mult).then_inc(S2["read"], 1)
                dve.wait_ge(S2["read"], t + 1)
                v.scalar_tensor_tensor(res3[:, :], res[:, :], g1[:, 7:8], res2[:, :], ALU.mult, ALU.add).then_inc(S2["z"], 1)
                c.done()

            def finish2(t):
                c = Chain(S2["chain"], t, 4)
                dve.wait_ge(S2["zexp"], t + 1)
                c.then(v.tensor_scalar(res[:, :], res2[:, :], 1.0, None, ALU.add))
                c.then(v.reciprocal(res2[:, :], res[:, :]))
                c.then(v.tensor_tensor(res[:, :], res2[:, :], X[:, t, :], ALU.add))
                dve.wait_ge(S2["stored"], t)
                layernorm(S2, t, c, res[:, :], xnew[:, :])
                c.done()

            def block_softmax(t):
                dve.wait_ge(B2["scores"], t + 1)
                v.tensor_tensor(pb[:, :, :], ps[:, 6:8, :].rearrange("p b (h n) -> p (b h) n", h=4),
                                mb[:, t, :].unsqueeze(1).broadcast_to([P, H, P]), ALU.add).then_inc(B2["max"], 1)
                dve.wait_ge(B2["max"], t * 2 + 1)
                v.tensor_reduce(rmax[:, :], pb[:, :, :], AX.X, ALU.max).then_inc(B2["max"], 1)
                dve.wait_ge(B2["max"], t * 2 + 2)
                v.tensor_tensor(pb[:, :, :], pb[:, :, :], rmax[:, :].unsqueeze(2).broadcast_to([P, H, P]),
                                ALU.subtract).then_inc(B2["less"], 1)

            def block_sums(t):
                dve.wait_ge(B2["exp"], t + 1)
                v.tensor_reduce(rsum[:, :], pb[:, :, :], AX.X, ALU.add).then_inc(B2["sum"], 1)

            def block_flat(t):
                dve.wait_ge(B2["pturned"], t + 1)
                v.tensor_copy(pbT[:, 0:4, :].rearrange("p h n -> p (h n)"), ps[:, 6, :]).then_inc(B2["pflat_d"], 1)

            def block_invert(t):
                dve.wait_ge(B2["sum"], t + 1)
                v.reciprocal(rinv[:, :], rsum[:, :]).then_inc(B2["inv"], 1)

            def block_scale(t):
                dve.wait_ge(B2["ctx"], t + 1)
                dve.wait_ge(B2["inv"], t + 1)
                v.tensor_tensor(mixed[:, :].rearrange("p (h k) -> p h k", h=H), ps[:, 4, :].rearrange("p (h k) -> p h k", h=H),
                                rinv[:, :].unsqueeze(2).broadcast_to([P, H, KD]), ALU.mult).then_inc(B2["mixed"], 1)

            def block_finish(t):
                dve.wait_ge(B2["wo"], t + 1)
                v.tensor_tensor(x3res[:, :], ps[:, 6, 0:D], X[:, t, :], ALU.add).then_inc(B2["res"], 1)
                dve.wait_ge(B2["res"], t + 1)
                v.bn_stats(bn3[:, :], x3res[:, :]).then_inc(B2["stats"], 1)
                dve.wait_ge(init["early"], 32)
                dve.wait_ge(B2["stats"], t + 1)
                v.bn_aggr(mv3[:, :], bn3[:, :]).then_inc(B2["agg"], 1)
                dve.wait_ge(B2["agg"], t + 1)
                v.tensor_scalar(veps3[:, :], mv3[:, 1:2], EPS, None, ALU.add).then_inc(B2["var"], 1)
                dve.wait_ge(B2["std"], t + 1)
                v.tensor_scalar(x3[:, :], x3res[:, :], mv3[:, 0:1], rstd3[:, :], ALU.subtract, ALU.mult).then_inc(B2["new"], 1)

            def stage2_blocks(t, k, r):
                at = t if isinstance(t, int) else NT // 2
                now, after1, after2 = at < NT, 0 < at <= NT, 1 < at
                if after2:
                    block_sums(t - 2)
                    block_flat(t - 2)
                    block_invert(t - 2)
                if after1:
                    mix_gates2(t - 1, 1 - k)
                if after2:
                    block_scale(t - 2)
                if after1:
                    finish2(t - 1)
                if after2:
                    block_finish(t - 2)
                if at < NT - 1:
                    edges(t + 1, 1 - k, r + k)
                if after1:
                    block_softmax(t - 1)

            def make_mask(t):
                dve.wait_ge(S3["slab0"], t * 16 + 16)
                v.tensor_scalar(mask, slab[:, 0, :], 0.0, -1.0, ALU.max, ALU.add).then_inc(S3["masked"], 1)
                dve.wait_ge(S3["masked"], t + 1)
                v.tensor_tensor(mask[:, bass.ts(t, P)], mask[:, bass.ts(t, P)], eye_less_one[:, :], ALU.max).then_inc(S3["step"], 1)
                dve.wait_ge(S3["step"], t * 2 + 1)
                v.tensor_scalar(mask, mask, HUGE, None, ALU.mult).then_inc(S3["step"], 1)
                dve.wait_ge(S3["step"], t * 2 + 2)

            def mask_scores(n, h):
                dve.wait_ge(S3["qk"], n + 1)
                if not (isinstance(n, int) and n < 2):
                    dve.wait_ge(S3["trn1"], n * 2 - 2)
                dve.sem_inc(S3["waited"], 1)
                v.tensor_tensor_reduce(wts[:, h % 2, :], ps[:, 0:Q, :].rearrange("p q n -> p (q n)"), mask, 1.0, -3e38,
                                       ALU.add, ALU.max, rmax[:, h:h + 1]).then_inc(S3["rowmax"], 1)
                dve.wait_ge(S3["rowmax"], n + 1)
                v.tensor_scalar(nmax[:, h:h + 1], rmax[:, h:h + 1], -1.0, None, ALU.mult).then_inc(S3["max"], 1)

            def invert_sums(t):
                dve.wait_ge(S3["exp"], t * H + H)
                v.reciprocal(rinv[:, :], rsum[:, :]).then_inc(S3["inv"], 1)

            def scale_mixed(t):
                dve.wait_ge(S3["pv"], t * H + H)
                dve.wait_ge(S3["inv"], t + 1)
                v.tensor_tensor(mixed[:, :].rearrange("p (h k) -> p h k", h=H), ps[:, 6, :].rearrange("p (h k) -> p h k", h=H),
                                rinv[:, :].unsqueeze(2).broadcast_to([P, H, KD]), ALU.mult).then_inc(S3["mixed"], 1)

            def finish3(t):
                c = Chain(S3["chain"], t, 1)
                dve.wait_ge(S3["wo"], t + 1)
                v.tensor_tensor(res[:, :], ps[:, 7, 0:D], X[:, t, :], ALU.add).then_inc(S3["read"], 1)
                dve.wait_ge(S3["read"], t + 1)
                layernorm(S3, t, c, res[:, :], xnew[:, :])
                c.done()

            def body2(t, first, last):
                for h in range(H):
                    n = t * H + h
                    if h == 0 and not first:
                        scale_mixed(t - 1)
                    if h == H - 1:
                        invert_sums(t)
                        if not last:
                            make_mask(t + 1)
                    if h < H - 1 or not last:
                        mask_scores(n + 1, (h + 1) % H)
                    if h == 2 and not first:
                        finish3(t - 1)
                    for q in (0, 2):
                        dve.wait_ge(S3["trn0"], n * 2 + (q // 2 + 1))
                        v.tensor_copy(wtsT[:, q, :], ps[:, 4, :]).then_inc(S3["ev0"], 1)

            def general_layer2():
                def both(t, k):
                    mix_gates2(t, k)
                    finish2(t)

                edges(1, 1, 0)
                both(0, 0)
                with dve.Fori(1, NT // 2) as u:
                    edges(u * 2, 0, u)
                    both(u * 2 - 1, 1)
                    edges(u * 2 + 1, 1, u)
                    both(u * 2, 0)
                both(NT - 1, 1)
                dve.wait_ge(S2["stored"], NT)
                dve.wait_ge(PJ2["kept"], NT)
                make_mask(0)
                mask_scores(0, 0)
                body2(0, True, False)
                with dve.Fori(1, NT - 1) as t:
                    body2(t, False, False)
                body2(NT - 1, False, True)
                scale_mixed(NT - 1)
                finish3(NT - 1)

            dve.wait_ge(FL["seen"], NT)
            v.memset(block_max[:, ::NT + 1], 0.0).then_inc(FL["cleared"], 1)
            dve.wait_ge(FL["cleared"], 1)
            v.tensor_reduce(extremes[:, 0:1], block_max[:, :], AX.X, ALU.max).then_inc(FL["reduced"], 1)
            dve.wait_ge(S1["stored"], NT)
            dve.wait_ge(S1["kept_g"], NT)
            edges(0, 0, 0)
            dve.wait_ge(FL["all"], 1)
            v.tensor_tensor(tests[:, 0:2], extremes_all[:, 1:4:2], extremes_all[:, 2:5:2], ALU.max).then_inc(FL["tests"], 1)
            dve.wait_ge(FL["tests"], 1)
            v.tensor_tensor(tests[:, 2:3], tests[:, 0:1], tests[:, 1:2], ALU.mult).then_inc(FL["tests"], 1)
            v.tensor_scalar(tests[:, 3:4], extremes_all[:, 0:1], 1.0, None, ALU.is_lt).then_inc(FL["tests"], 1)
            dve.wait_ge(FL["tests"], 3)
            v.scalar_tensor_tensor(blocks_only[:, :], tests[:, 2:3], WEIGHT_BOUND, tests[:, 3:4], ALU.is_le,
                                   ALU.mult).then_inc(FL["ready"], 1)
            flag = chosen(dve)
            with dve.If(flag > 0):
                dve.wait_ge(BL["masked"], 3)
                staggered(dve, stage2_blocks)
            with dve.Else():
                general_layer2()

            def row_max(s, t, k):
                dve.wait_ge(s["qk"], t + 1)
                v.tensor_reduce(nmax[:, k:k + 1], ps[:, 0:Q, :].rearrange("p q n -> p (q n)"), AX.X, ALU.max,
                                negate=True).then_inc(s["max"], 1)

            def weigh(s, t, k, quarters):
                for q in quarters:
                    b = q % 2
                    dve.wait_ge(s["trn1"] if b else s["trn0"], t * 2 + (q // 2 + 1))
                    v.tensor_tensor(wtsT[:, q, :], ps[:, 4 + b, :], slab[:, k, q * BANK:(q + 1) * BANK],
                                    ALU.mult).then_inc(s["ev1"] if b else s["ev0"], 1)

            def finish4(t, k, r):
                c = Chain(S4["chain"], t, 1)
                dve.wait_ge(S4["pv"], t + 1)
                c.then(v.reciprocal(rinv[:, 0:1], rsum[:, k:k + 1]))
                v.scalar_tensor_tensor(res[:, :], ps[:, 6, 0:D], rinv[:, 0:1], X[:, t, :], ALU.mult, ALU.add).then_inc(S4["read"], 1)
                dve.wait_ge(S4["read"], t + 1)
                dve.wait_ge(S4["turned"], t)
                dve.wait_ge(S4["stored"], t)
                v.scalar_tensor_tensor(xnew[:, :], res[:, :], SLOPE, res[:, :], ALU.mult, ALU.max).then_inc(S4["new"], 1)
                c.done()

            def finish5(t, k, r):
                c = Chain(S5["chain"], t, 4)
                dve.wait_ge(S5["pv"], t + 1)
                c.then(v.reciprocal(rinv[:, 0:1], rsum[:, k:k + 1]))
                v.scalar_tensor_tensor(res[:, :], ps[:, 6, 0:D], rinv[:, 0:1], X4[:, t, :], ALU.mult, ALU.add).then_inc(S5["read"], 1)
                dve.wait_ge(S5["read"], t + 1)
                c.then(v.scalar_tensor_tensor(res2[:, :], res[:, :], SLOPE, res[:, :], ALU.mult, ALU.max))
                c.then(v.tensor_tensor(res3[:, :], res2[:, :], X[:, t, :], ALU.add))
                if not (isinstance(r, int) and r == 0):
                    dve.wait_ge(S5["out1"] if k else S5["out0"], r * 16)
                layernorm(S5, t, c, res3[:, :], outt[:, k, :])
                c.done()

            def step3(s, finish):
                def body(t, k, r):
                    at = t if isinstance(t, int) else NT // 2
                    if at > 0:
                        finish(t - 1, 1 - k, r if k else r - 1)
                    dve.wait_ge(s["slab1"] if k else s["slab0"], r * 16 + 16)
                    weigh(s, t, k, (0, 1))
                    if at < NT - 1:
                        row_max(s, t + 1, 1 - k)
                    weigh(s, t, k, (2, 3))
                return body

            for s, prev, finish in ((S4, L2, finish4), (S5, S4, finish5)):
                dve.wait_ge(prev["kept"], NT)
                row_max(s, 0, 0)
                two_by_two(dve, step3(s, finish))
                finish(NT - 1, 1, NT // 2 - 1)


def kernel(x, adj, L0_gnn_W, L0_gnn_b, L1_gnn_W_sa, L1_gnn_a_sa, L1_gnn_W_gcnb, L1_gnn_b_gcnb, L1_gnn_Wa, L1_gnn_ba,
           L1_gnn_Wb, L1_gnn_bb, L2_gnn_Wks, L2_gnn_Wqs, L2_gnn_Wvs, L2_gnn_Wo, L3_gnn_W_stack):
    import numpy as np
    import concourse.bacc as bacc
    from concourse.bass_utils import run_bass_kernel_spmd

    x, adj = np.asarray(x), np.asarray(adj)
    Wa, Wb = np.asarray(L1_gnn_Wa), np.asarray(L1_gnn_Wb)

    def heads_side_by_side(a):
        return np.asarray(a).transpose(1, 0, 2).reshape(D, HD)

    arrays = {
        "x": x,
        "adj": adj.reshape(NT, P, N),
        "adjT": adj.reshape(NT, P, NT, P).transpose(0, 3, 2, 1).reshape(NT, P, N),
        "W0T": np.asarray(L0_gnn_W).T,
        "b0": np.asarray(L0_gnn_b),
        "W_sa": np.asarray(L1_gnn_W_sa),
        "a_sa": np.asarray(L1_gnn_a_sa).reshape(2 * D),
        "W_gates": np.concatenate([np.asarray(L1_gnn_W_gcnb), Wa[:, :D].T, Wb[:, :D].T, Wa[:, D:].T, Wb[:, D:].T], axis=1),
        "b_gcnb": np.asarray(L1_gnn_b_gcnb),
        "b_gates": np.concatenate([np.asarray(L1_gnn_ba), np.asarray(L1_gnn_bb)]),
        "Wk": heads_side_by_side(L2_gnn_Wks),
        "Wq": heads_side_by_side(L2_gnn_Wqs),
        "Wv": heads_side_by_side(L2_gnn_Wvs),
        "Wo": np.asarray(L2_gnn_Wo).reshape(HD, D),
        "W_stack": np.asarray(L3_gnn_W_stack),
    }
    arrays = {n: np.ascontiguousarray(a) for n, a in arrays.items()}
    nc = bacc.Bacc("TRN2", target_bir_lowering=False, num_devices=1)
    args = [nc.dram_tensor(n, a.shape, F32, kind="ExternalInput").ap() for n, a in arrays.items()]
    args_by_name = dict(zip(arrays, args))
    out = nc.dram_tensor("out", (NT, P, D), F32, kind="ExternalOutput").ap()
    graph_layers(nc, **args_by_name, out=out)
    r = run_bass_kernel_spmd(nc, [arrays], core_ids=[0])
    return r.results[0]["out"].reshape(N, D)
```

```python
from contextlib import ExitStack

import concourse.bass as bass
from concourse import mybir

F32 = mybir.dt.float32
I32 = mybir.dt.int32
F32R = mybir.dt.float32r
ALU = mybir.AluOpType
ACT = mybir.ActivationFunctionType
AX = mybir.AxisListType

P = 128
N = 2048
D = 256
NT = N // P
DC = D // P
H = 8
KD = 64
HD = H * KD
HC = HD // P
BANK = 512
Q = 4
QT = NT // Q
GW = D + 4
HW = D + 2
EPS = 1e-5
SLOPE = 0.01
HUGE = 1e16
KEY_SCALE = 0.125
CUT = N * 3 // 8
LATE = 15
LEAST_SCORE = -88.0
WEIGHT_BOUND = 200.0


def graph_layers(nc, x, adj, adjT, W0T, b0, W_sa, a_sa, W_gates, b_gcnb, b_gates, Wk, Wq, Wv, Wo, W_values, W_sT, W_hT, out):
    with ExitStack() as ctx:
        def sb(name, *shape):
            return ctx.enter_context(nc.sbuf_tensor(name, [P, *shape], F32))

        def sems(stage, *names):
            return {n: ctx.enter_context(nc.semaphore(f"{stage}_{n}")) for n in names}

        K = 1024
        base = -(-nc.sbuf_base // 32) * 32
        ctx.enter_context(nc.sbuf_tensor("arena", [P, 188 * K // 4], F32))

        def at(name, offset, *shape, dtype=F32):
            return nc.alloc_sbuf_tensor_at(name, [P, *shape], dtype, offset=base + offset)

        X = at("X", 0, NT, D)
        slab = at("slab", 16 * K, 2, N)
        wts = at("wts", 32 * K, 2, N)
        w_query = at("w_query", 48 * K, 2, DC, D)
        w_value = at("w_value", 52 * K, 2, DC, D)
        H0H = at("H0H", 56 * K, NT, D, dtype=F32R)
        H0L = at("H0L", 160 * K, NT, D, dtype=F32R)
        AH = [at(f"AH{k}", place * K, N, dtype=F32R) for k, place in enumerate((32, 176))]
        AL = [at(f"AL{k}", place * K, N, dtype=F32R) for k, place in enumerate((40, 80))]
        HA = at("HA", 88 * K, NT, HW)
        GB = at("GB", 88 * K + NT * HW * 4, NT, GW)
        left_rows = at("left_rows", 122 * K, N)
        KT3 = at("KT3", 152 * K, DC, N)
        V3 = at("V3", 168 * K, NT, D)
        W_hT_in = at("W_hT_in", 152 * K, 2, DC, D)
        W_sT_in = at("W_sT_in", 156 * K, 2, DC, D)
        x3 = at("x3", 56 * K, D)
        x3res = at("x3res", 80 * K, D)
        x3T = at("x3T", 57 * K, DC, P)
        kb = at("kb", 58 * K, HC, 2, P)
        vb = at("vb", 62 * K, HD)
        pb = at("pb", 64 * K, H, P)
        pbT = at("pbT", 68 * K, H, P)
        mb = at("mb", 72 * K, NT, P)
        WvH = at("WvH", 184 * K, DC, HD, dtype=F32R)
        WvL = at("WvL", 138 * K, DC, HD, dtype=F32R)
        WoH = at("WoH", 146 * K, HC, D, dtype=F32R)
        WoL = at("WoL", 142 * K, HC, D, dtype=F32R)
        xTH = at("xTH", 150 * K, DC, P, dtype=F32R)
        xTL = at("xTL", 121 * K, DC, P, dtype=F32R)
        mixedTH = at("mixedTH", 81 * K, HC, P, dtype=F32R)
        mixedTL = at("mixedTL", 83 * K, HC, P, dtype=F32R)
        KT2 = at("KT2", 56 * K, HC, N)
        V2 = at("V2", 88 * K, NT, HD)
        mask = slab[:, 1, :]
        wtsT = at("wtsT", 122 * K, Q, BANK)
        VH = at("VH", 56 * K, NT, D, dtype=F32R)
        VL = at("VL", 72 * K, NT, D, dtype=F32R)
        KH = at("KH", 88 * K, DC, N, dtype=F32R)
        KL = at("KL", 104 * K, DC, N, dtype=F32R)
        X4 = at("X4", 120 * K, NT, D)
        WH = at("WH", 136 * K, Q, BANK, dtype=F32R)
        WL = at("WL", 144 * K, Q, BANK, dtype=F32R)
        QH = at("QH", 184 * K, DC, P, dtype=F32R)
        QL = at("QL", 185 * K, DC, P, dtype=F32R)
        wk = at("wk", 130 * K, DC, HD)
        wq = at("wq", 134 * K, DC, HD)
        wv = at("wv", 138 * K, DC, HD)
        wo = at("wo", 142 * K, HC, D)
        w0 = at("w0", 146 * K, DC, D)
        wsa = at("wsa", 148 * K, DC, HW)
        b0r = at("b0r", 121 * K, D)
        bgr = at("bgr", 151 * K, D)
        wga = sb("wga", DC, GW)
        asr = at("asr", 184 * K, 2 * D)
        bar = sb("bar", 2)

        ident = sb("ident", P)
        minus_half = sb("minus_half", 1)
        right_cols = sb("right_cols", NT)
        xnew = sb("xnew", D)
        xnewT = sb("xnewT", DC, P)
        qT = sb("qT", HC, P)
        xq = at("xq", 186 * K, D)
        xqT = at("xqT", 187 * K, DC, P)
        left_wt = at("left_wt", 186 * K, DC, P)
        mixed = sb("mixed", HD)
        mixedT = sb("mixedT", HC, P)
        whole = (mixed[:, :], mixedT[:, :, :].rearrange("p c n -> p (c n)"))
        res = sb("res", D)
        res2 = sb("res2", D)
        res3 = sb("res3", D)
        outt = sb("outt", 2, D)
        h0 = (res2[:, :], res3[:, :])
        bn = sb("bn", 6)
        mv = sb("mv", 2)
        veps = sb("veps", 1)
        rstd = sb("rstd", 1)
        bn3 = sb("bn3", 6)
        mv3 = sb("mv3", 2)
        veps3 = sb("veps3", 1)
        rstd3 = sb("rstd3", 1)
        wleft = sb("wleft", DC)
        g1 = sb("g1", 8)
        eye_less_one = sb("eye_less_one", P)
        rmax = sb("rmax", H)
        nmax = sb("nmax", H)
        rsum = sb("rsum", H)
        rinv = sb("rinv", H)
        block_max = sb("block_max", NT * NT)
        extremes = sb("extremes", 5)
        extremes_all = sb("extremes_all", 5)
        tests = sb("tests", 4)
        blocks_only = ctx.enter_context(nc.sbuf_tensor("blocks_only", [P, 1], I32))

        ps = ctx.enter_context(nc.psum_tensor("ps", [P, 8, BANK], F32))

        init = sems("init", "filled", "consts", "x0", "x", "early", "late")
        LN = ("chain", "stats", "var", "std", "new", "stored", "turned", "flat")
        S0 = sems("s0", "new", "turned", "flat", "proj", "read", "high", "kept")
        S1 = sems("s1", "slab0", "slab1", "high", "low", "low_start", "agg", "read", *LN, "proj", "kept_h", "kept_g",
                  "weights", "query_weights")
        S2 = sems("s2", "slab0", "slab1", "first", "sum", "score", "raw", "exp", "edge", "agg", "read", "gate", "gexp", "z",
                  "zexp", "mixing", "norm", *LN)
        B2 = sems("b2", "whigh", "wlow", "xhigh", "xlow", "mlow", "cleared", "qkv", "qflat", "kvkept", "scores", "masked",
                  "max", "exp", "inv", "pturned", "pflat_a", "pflat_d", "ctx", "mixed", "mturned", "mflat", "wo", "res",
                  "stats", "agg", "var", "std", "new", "stored", "turned", "flat", "proj")
        BL = sems("adj", "blocks", "masked")
        FL = sems("flag", "seen", "cleared", "reduced", "all", "tests", "ready")
        L3 = ("slab0", "slab1", "xq", "query", "qhigh", "qlow", "qk", "max", "exp",
              "trn0", "trn1", "cut", "high", "low", "pv", "read")
        SPLIT = sems("split", "khigh", "klow", "vhigh", "vlow")
        spare = list(B2.values())

        def sharing(*names):
            return {n: spare.pop() for n in names}

        S3 = sharing("waited", "rowmax", "step", "masked", "inv", "mixed", "mturned", "mflat", "wo", "slab0", "xq", "xqturned",
                     "xqflat", "query", "qkept", "qk", "max", "exp", "trn0", "trn1", "ev0", "ev1", "pv", "read")
        S3.update(sems("s3", "chain", "stats", "var", "std", "new", "stored"))
        PJ = sharing("xq", "turned", "flat", "proj", "kept")
        L2 = sems("l2", "kept")
        S4 = sems("s4", *L3, "inv", "new", "stored", "turned", "flat", "proj", "kept")
        S5 = sems("s5", "out0", "out1", *L3, "inv", "chain", "stats", "var", "std", "new")

        def key_pieces(stage, quarters):
            for q in quarters:
                for c in range(DC):
                    yield slice((c * Q + q) * BANK, (c * Q + q + 1) * BANK), (stage * Q + q) * DC + c + 1

        def chosen(eng):
            eng.wait_ge(FL["ready"], 1)
            return eng.value_load(blocks_only[0:1, 0:1], min_val=0, max_val=1)

        def two_by_two(eng, body, stop=NT):
            for t in range(3):
                body(t, t % 2, t // 2)
            with eng.Fori(1, (stop - 4) // 2) as u:
                body(u * 2 + 1, 1, u)
                body(u * 2 + 2, 0, u + 1)
            for t in range(stop - 3, stop):
                body(t, t % 2, t // 2)

        def staggered(eng, body):
            for t in range(4):
                body(t, t % 2, t // 2)
            with eng.Fori(2, NT // 2 - 1) as u:
                body(u * 2, 0, u)
                body(u * 2 + 1, 1, u)
            for t in range(NT - 2, NT + 2):
                body(t, t % 2, t // 2)

        block = ctx.enter_context(nc.Block())

        @block.sync
        def _(sp):
            def split(a):
                return a.rearrange("(c p) n -> p c n", p=P)

            xv = x.rearrange("(t p) d -> p t d", p=P)
            sp.dma_start(X[:, 0:2, :], xv[:, 0:2, :]).then_inc(init["x0"], 16)
            sp.dma_start(w0[:, :, :], split(W0T)).then_inc(init["early"], 16)
            sp.dma_start(X[:, 2:NT, :], xv[:, 2:NT, :]).then_inc(init["x"], 16)
            sp.dma_start(b0r[:, :], b0.partition_broadcast(P)).then_inc(init["early"], 16)

            def load(s, src, t, k):
                sp.dma_start(slab[:, k, :], src[t]).then_inc(s["slab1"] if k else s["slab0"], 16)

            load(S1, adjT, 0, 0)
            load(S1, adjT, 1, 1)
            for dst, src in ((wsa[:, :, 0:D], split(W_sa)), (wga[:, :, :], split(W_gates)), (wk[:, :, :], split(Wk)),
                             (wq[:, :, :], split(Wq)), (wv[:, :, :], split(Wv)), (wo[:, :, :], split(Wo)),
                             *((to[:, i], split(src[i])) for to, src in
                               ((W_hT_in, W_hT), (W_sT_in, W_sT), (w_value, W_values)) for i in range(2)),
                             (bgr[:, :], b_gcnb.partition_broadcast(P)), (asr[:, :], a_sa.partition_broadcast(P)),
                             (bar[:, :], b_gates.partition_broadcast(P))):
                sp.dma_start(dst, src).then_inc(init["late"], 16)
            with sp.Fori(0, NT) as t:
                sp.dma_start(mb[:, t, :], adj[t, :, bass.ts(t, P)]).then_inc(BL["blocks"], 16)
            with sp.Fori(1, NT // 2) as u:
                for k in range(2):
                    sp.wait_ge(S1["low"], u * 2 + k - 1)
                    sp.wait_ge(FL["seen"], u * 2 + k - 1)
                    load(S1, adjT, u * 2 + k, k)
            for k in range(2):
                sp.wait_ge(S1["low"], NT - 1 + k)
                sp.wait_ge(FL["seen"], NT - 1 + k)
                load(S2, adjT, k, k)
            with sp.Fori(1, NT // 2) as u:
                for k in range(2):
                    sp.wait_ge(S2["agg"], u * 2 + k - 1)
                    load(S2, adjT, u * 2 + k, k)
            flag = chosen(sp)
            with sp.If(flag > 0):
                sp.wait_ge(S2["agg"], NT)
                load(S4, adjT, 0, 0)
                load(S4, adjT, 1, 1)
            with sp.Else():
                sp.wait_ge(S2["agg"], NT)
                load(S3, adj, 0, 0)
                with sp.Fori(1, NT) as t:
                    sp.wait_ge(S3["masked"], t)
                    load(S3, adj, t, 0)
                sp.wait_ge(S3["masked"], NT)
                load(S4, adjT, 0, 0)
                sp.wait_ge(S3["max"], NT * H)
                load(S4, adjT, 1, 1)
            with sp.Fori(1, NT // 2) as u:
                for k in range(2):
                    sp.wait_ge(S4["cut"], u * 8 + (4 * k - 4))
                    load(S4, adjT, u * 2 + k, k)
            for k in range(2):
                sp.wait_ge(S4["cut"], Q * (NT - 1 + k))
                load(S5, adjT, k, k)

            def store(t, k):
                sp.wait_ge(S5["new"], t + 1)
                sp.dma_start(out[t], outt[:, k, :]).then_inc(S5["out1"] if k else S5["out0"], 16)

            with sp.Fori(1, NT // 2) as u:
                for k in range(2):
                    sp.wait_ge(S5["cut"], u * 8 + (4 * k - 4))
                    load(S5, adjT, u * 2 + k, k)
                for k in range(2):
                    store(u * 2 + (k - 2), k)
            for k in range(2):
                store(NT - 2 + k, k)
            sp.wait_ge(S5["out0"], 16 * NT // 2)
            sp.wait_ge(S5["out1"], 16 * NT // 2)

        @block.gpsimd
        def _(pool):
            nc.gpsimd.memset(ident[:, :], 0.0).then_inc(init["filled"], 1)
            nc.gpsimd.memset(minus_half[:, :], -0.5).then_inc(init["consts"], 1)
            nc.gpsimd.memset(HA[:, :, D:HW], 1.0).then_inc(init["consts"], 1)
            nc.gpsimd.memset(eye_less_one[:, :], -1.0).then_inc(init["filled"], 1)
            pool.wait_ge(init["filled"], 2)
            nc.gpsimd.affine_select(out=ident[:, :], in_=ident[:, :], compare_op=ALU.not_equal, fill=1.0, base=0,
                                    pattern=[[-1, P]], channel_multiplier=1).then_inc(init["consts"], 1)
            nc.gpsimd.affine_select(out=eye_less_one[:, :], in_=eye_less_one[:, :], compare_op=ALU.not_equal, fill=0.0,
                                    base=0, pattern=[[-1, P]], channel_multiplier=1).then_inc(init["consts"], 1)

            pool.wait_ge(init["x0"], 16)
            nc.gpsimd.tensor_copy(xnew[:, :], X[:, 0, :]).then_inc(S0["new"], 1)
            nc.gpsimd.tensor_copy(xq[:, :], X[:, 1, :]).then_inc(S0["new"], 1)
            pool.wait_ge(init["x"], 16)
            with pool.Fori(1, NT // 2) as u:
                for k, to in enumerate((xnew, xq)):
                    pool.wait_ge(S0["turned"], u * 2 + (k - 1))
                    nc.gpsimd.tensor_copy(to[:, :], X[:, u * 2 + k, :]).then_inc(S0["new"], 1)

            def rsqrt(s, t):
                pool.wait_ge(s["var"], t + 1)
                nc.gpsimd.tensor_tensor(rstd[:, :], veps[:, :], minus_half[:, :], ALU.pow).then_inc(s["std"], 1)

            def store(s, t, to):
                pool.wait_ge(init["early"], 32)
                pool.wait_ge(s["new"], t + 1)
                nc.gpsimd.tensor_copy(to[:, t, :], xnew[:, :]).then_inc(s["stored"], 1)

            def next_query(s, t, src):
                pool.wait_ge(s["xqturned"], t)
                nc.gpsimd.tensor_copy(xq[:, :], src[:, t, :]).then_inc(s["xq"], 1)

            def slab_low(t, k):
                pool.wait_ge(S1["high"], t + 1)
                nc.gpsimd.tensor_tensor(AL[k][:, CUT:], slab[:, k, CUT:], AH[k][:, CUT:], ALU.subtract).then_inc(S1["low"], 1)

            pool.wait_ge(init["consts"], 4)
            pool.wait_ge(S1["low"], 2)
            with pool.Fori(0, NT // 2 - 1) as u:
                for k in range(2):
                    rsqrt(S1, u * 2 + k)
                    store(S1, u * 2 + k, X)
                    slab_low(u * 2 + (k + 2), k)
            for t in (NT - 2, NT - 1):
                rsqrt(S1, t)
                store(S1, t, X)

            pool.wait_ge(FL["reduced"], 1)
            nc.gpsimd.partition_all_reduce(extremes_all[:, :], extremes[:, :], P, bass.bass_isa.ReduceOp.max).then_inc(FL["all"], 1)

            def edge_scores(t, k):
                if not (isinstance(t, int) and t < 2):
                    pool.wait_ge(S2["agg"], t - 1)
                nc.gpsimd.tensor_tensor(wts[:, k, :].rearrange("p (j n) -> p j n", j=NT),
                                        left_rows[:, bass.ts(t, P)].unsqueeze(1).broadcast_to([P, NT, P]),
                                        right_cols[:, :].unsqueeze(2).broadcast_to([P, NT, P]), ALU.add).then_inc(S2["sum"], 1)

            pool.wait_ge(S1["kept_g"], NT)
            pool.wait_ge(S1["kept_h"], NT)
            edge_scores(1, 1)

            def blocks_tile(t, k):
                at_t = t if isinstance(t, int) else NT // 2
                if at_t < NT - 2:
                    edge_scores(t + 2, k)
                if at_t < NT:
                    rsqrt(S2, t)
                    store(S2, t, X)
                if at_t > 0:
                    pool.wait_ge(B2["var"], t)
                    nc.gpsimd.tensor_tensor(rstd3[:, :], veps3[:, :], minus_half[:, :], ALU.pow).then_inc(B2["std"], 1)
                    pool.wait_ge(init["early"], 32)
                    pool.wait_ge(B2["new"], t)
                    nc.gpsimd.tensor_copy(X[:, t - 1, :], x3[:, :]).then_inc(B2["stored"], 1)

            flag = chosen(pool)
            with pool.If(flag > 0):
                nc.gpsimd.memset(kb[:, :, :, :], 0.0).then_inc(B2["cleared"], 1)
                blocks_tile(0, 0)
                with pool.Fori(0, NT // 2 - 2) as u:
                    blocks_tile(u * 2 + 1, 1)
                    blocks_tile(u * 2 + 2, 0)
                for t in range(NT - 3, NT + 1):
                    blocks_tile(t, t % 2)
                pool.wait_ge(B2["stored"], NT)
            with pool.Else():
                with pool.Fori(0, NT // 2 - 1) as u:
                    for k in range(2):
                        edge_scores(u * 2 + (k + 2), k)
                        rsqrt(S2, u * 2 + k)
                        store(S2, u * 2 + k, X)
                for t in (NT - 2, NT - 1):
                    rsqrt(S2, t)
                    store(S2, t, X)

                def hand_tiles(before):
                    nc.gpsimd.tensor_copy(xq[:, :], X[:, 0, :]).then_inc(PJ["xq"], 1)
                    with pool.Fori(1, NT) as t:
                        pool.wait_ge(PJ["turned"], t + before)
                        nc.gpsimd.tensor_copy(xq[:, :], X[:, t, :]).then_inc(PJ["xq"], 1)
                    pool.wait_ge(PJ["turned"], before + NT)

                pool.wait_ge(S2["stored"], NT)
                hand_tiles(0)
                next_query(S3, 0, X)
                with pool.Fori(0, NT - 1) as t:
                    next_query(S3, t + 1, X)
                    rsqrt(S3, t)
                    store(S3, t, X)
                rsqrt(S3, NT - 1)
                store(S3, NT - 1, X)
                pool.wait_ge(S3["stored"], NT)
                hand_tiles(NT)

            def next_turned(s, t):
                if not (isinstance(t, int) and t == 0):
                    pool.wait_ge(init["early"], 32)
                    pool.wait_ge(s["query"], t)
                nc.gpsimd.tensor_copy(xqT[:, :, :], KT3[:, :, bass.ts(t, P)]).then_inc(s["xq"], 1)

            pool.wait_ge(L2["kept"], 2)
            next_turned(S4, 0)
            next_turned(S4, 1)
            pool.wait_ge(L2["kept"], NT)
            with pool.Fori(0, NT - 2) as t:
                next_turned(S4, t + 2)
                store(S4, t, X4)
            store(S4, NT - 2, X4)
            store(S4, NT - 1, X4)
            pool.wait_ge(S4["kept"], 2)
            next_turned(S5, 0)
            next_turned(S5, 1)
            pool.wait_ge(S4["kept"], NT)
            with pool.Fori(0, NT - 2) as t:
                next_turned(S5, t + 2)
                rsqrt(S5, t)
            rsqrt(S5, NT - 2)
            rsqrt(S5, NT - 1)

        @block.tensor
        def _(pe):
            mm = nc.tensor.matmul

            def turn_new(s, t):
                pe.wait_ge(s["new"], t + 1)
                for c in range(DC):
                    last = nc.tensor.transpose(ps[:, 7, c * P:(c + 1) * P], xnew[:, c * P:(c + 1) * P], ident[:, :])
                last.then_inc(s["turned"], 1)

            def rows(bank, col, wt, n):
                for c in range(DC):
                    last = mm(ps[:, bank, col:col + n], xnewT[:, c, :], wt[:, c, 0:n], start=(c == 0), stop=(c == DC - 1))
                return last

            def cols(bank, wt, first, chunks, xt):
                for o in range(chunks):
                    for c in range(DC):
                        last = mm(ps[:, bank, o * P:(o + 1) * P], wt[:, c, first + o * P:first + (o + 1) * P], xt[:, c, :],
                                  start=(c == 0), stop=(c == DC - 1))
                return last

            def turn0(t, k):
                pe.wait_ge(S0["new"], t + 1)
                if not (isinstance(t, int) and t < 2):
                    pe.wait_ge(S0["flat"], t - 1)
                src = xq if k else xnew
                for c in range(DC):
                    last = nc.tensor.transpose(ps[:, 7 - k, c * P:(c + 1) * P], src[:, c * P:(c + 1) * P], ident[:, :])
                last.then_inc(S0["turned"], 1)

            def products0(t, k):
                pe.wait_ge(S0["flat"], t + 1)
                if not (isinstance(t, int) and t < 2):
                    pe.wait_ge(S0["read"], t - 1)
                src = xqT if k else xnewT
                for c in range(DC):
                    last = mm(ps[:, 5 - k, 0:D], src[:, c, :], w0[:, c, :], start=(c == 0), stop=(c == DC - 1))
                last.then_inc(S0["proj"], 1)

            pe.wait_ge(init["consts"], 4)
            turn0(0, 0)
            turn0(1, 1)
            pe.wait_ge(init["early"], 32)
            products0(0, 0)
            turn0(2, 0)
            products0(1, 1)
            with pe.Fori(1, NT // 2 - 1) as u:
                for k in range(2):
                    turn0(u * 2 + (k + 1), 1 - k)
                    products0(u * 2 + k, k)
            turn0(NT - 1, 1)
            products0(NT - 2, 0)
            products0(NT - 1, 1)

            def agg0(t, k, first, end):
                if first == 0:
                    pe.wait_ge(S1["low"], t + 1)
                    if not (isinstance(t, int) and t < 2):
                        pe.wait_ge(S1["low_start"], t - 1)
                        pe.wait_ge(S1["read"], t - 1)
                for j in range(first, end):
                    for n, (a, b) in enumerate(((AH[k], H0H), (AH[k], H0L), (AL[k], H0H))):
                        last = mm(ps[:, k, 0:D], a[:, j * P:(j + 1) * P], b[:, j, :],
                                  start=(j == 0 and n == 0), stop=(j == NT - 1 and n == 2))
                if end == NT:
                    last.then_inc(S1["agg"], 1)

            def products1(t):
                pe.wait_ge(S1["flat"], t + 1)
                if not (isinstance(t, int) and t == 0):
                    pe.wait_ge(S1["kept_h"], t)
                    pe.wait_ge(S1["kept_g"], t)
                rows(5, 0, wsa, D + 1)
                for c in range(DC):
                    mm(ps[:, 4, 0:P], left_wt[:, c, :], xnewT[:, c, :], start=(c == 0), stop=(c == DC - 1))
                rows(6, 0, wga, GW).then_inc(S1["proj"], 1)

            def stage1(t, k):
                agg0(t, k, 0, 10)
                turn_new(S1, t - 1)
                agg0(t, k, 10, 13)
                products1(t - 1)
                agg0(t, k, 13, NT)

            pe.wait_ge(S0["kept"], NT)
            agg0(0, 0, 0, NT)
            pe.wait_ge(init["late"], 16 * LATE)
            pe.wait_ge(S1["weights"], 3 * DC)
            for i in range(2):
                for o in range(DC):
                    for c in range(DC):
                        last = mm(ps[:, 2 + i, o * D:(o + 1) * D], W_hT_in[:, i, c, o * P:(o + 1) * P], W_sT_in[:, i, c, :],
                                  start=(c == 0), stop=(c == DC - 1))
            last.then_inc(S1["query_weights"], 1)
            stage1(1, 1)
            with pe.Fori(1, NT // 2) as u:
                stage1(u * 2, 0)
                stage1(u * 2 + 1, 1)
            turn_new(S1, NT - 1)
            products1(NT - 1)

            def agg_gates(t, k, r, q):
                if q == 0:
                    pe.wait_ge(S2["slab1"] if k else S2["slab0"], r * 16 + 16)
                    if not (isinstance(t, int) and t < 2):
                        pe.wait_ge(S2["read"], t - 1)
                for j in range(q * QT, q * QT + QT):
                    mm(ps[:, 2 + k, 0:D + 2], slab[:, k, j * P:(j + 1) * P], GB[:, j, 0:D + 2], start=(j == 0), stop=(j == NT - 1))

            def agg_edges(t, k, q):
                if q == 0:
                    pe.wait_ge(S2["edge"], t + 1)
                for j in range(q * QT, q * QT + QT):
                    last = mm(ps[:, k, 0:D + 1], wts[:, k, j * P:(j + 1) * P], HA[:, j, 0:D + 1], start=(j == 0), stop=(j == NT - 1))
                if q == Q - 1:
                    last.then_inc(S2["agg"], 1)

            def in_parts(to, chunks, a, b):
                terms = [(c, x, y) for c in range(chunks) for x, y in ((a[0], b[0]), (a[0], b[1]), (a[1], b[0]))]
                for n, (c, x, y) in enumerate(terms):
                    last = mm(to, x[:, c, :], y[:, c, :], start=(n == 0), stop=(n == len(terms) - 1))
                return last

            def block_qkv(t, after_another):
                pe.wait_ge(S2["flat"], t + 1)
                cols(4, wq, 0, HC, xnewT).then_inc(B2["qkv"], 1)
                if after_another:
                    pe.wait_ge(B2["res"], t)
                cols(6, wk, 0, HC, xnewT).then_inc(B2["qkv"], 1)
                pe.wait_ge(B2["xlow"], t + 1)
                in_parts(ps[:, 7, :], DC, (xTH, xTL), (WvH, WvL)).then_inc(B2["qkv"], 1)

            def block_scores(t):
                pe.wait_ge(B2["qflat"], t + 1)
                pe.wait_ge(B2["kvkept"], t + 1)
                for c in range(HC):
                    last = mm(ps[:, 6 + c // 2, c % 2 * 2 * P:(c % 2 + 1) * 2 * P], qT[:, c, :],
                              kb[:, c, :, :].rearrange("p a n -> p (a n)"), start=True, stop=True)
                last.then_inc(B2["scores"], 1)

            def block_turn_weights(t):
                pe.wait_ge(B2["exp"], t + 1)
                for h in range(H):
                    last = nc.tensor.transpose(ps[:, 6 + h // 4, h % 4 * P:(h % 4 + 1) * P], pb[:, h, :], ident[:, :])
                last.then_inc(B2["pturned"], 1)

            def block_mix(t):
                pe.wait_ge(B2["pflat_a"], t + 1)
                pe.wait_ge(B2["pflat_d"], t + 1)
                for h in range(H):
                    last = mm(ps[:, 4, h * KD:(h + 1) * KD], pbT[:, h, :], vb[:, h * KD:(h + 1) * KD], start=True, stop=True)
                last.then_inc(B2["ctx"], 1)

            def block_turn_mixed(t):
                if not (isinstance(t, int) and t == 0):
                    pe.wait_ge(L2["kept"], t)
                pe.wait_ge(B2["mixed"], t + 1)
                for c in range(HC):
                    last = nc.tensor.transpose(ps[:, 5, c * P:(c + 1) * P], mixed[:, c * P:(c + 1) * P], ident[:, :])
                last.then_inc(B2["mturned"], 1)

            def block_out(t):
                pe.wait_ge(B2["mlow"], t + 1)
                in_parts(ps[:, 6, 0:D], HC, (mixedTH, mixedTL), (WoH, WoL)).then_inc(B2["wo"], 1)

            def block_turn_new(t):
                pe.wait_ge(B2["new"], t + 1)
                for c in range(DC):
                    last = nc.tensor.transpose(ps[:, 5, c * P:(c + 1) * P], x3[:, c * P:(c + 1) * P], ident[:, :])
                last.then_inc(B2["turned"], 1)

            def block_products(t):
                pe.wait_ge(B2["flat"], t + 1)
                for c in range(DC):
                    last = mm(ps[:, 5, D:2 * D], x3T[:, c, :], w_value[:, 0, c, :], start=(c == 0), stop=(c == DC - 1))
                last.then_inc(B2["proj"], 1)

            def stage2_blocks(t, k, r):
                at = t if isinstance(t, int) else NT // 2
                now, after1, after2 = at < NT, 0 < at <= NT, 1 < at
                if at == 0:
                    for q in range(Q):
                        agg_edges(t, k, q)
                    return
                if now:
                    for q in range(3):
                        agg_gates(t, k, r, q)
                if after2:
                    block_turn_weights(t - 2)
                if now:
                    agg_gates(t, k, r, 3)
                if after2:
                    block_mix(t - 2)
                if now:
                    agg_edges(t, k, 0)
                if after2:
                    block_turn_mixed(t - 2)
                if now:
                    agg_edges(t, k, 1)
                if after1:
                    turn_new(S2, t - 1)
                if after2:
                    block_out(t - 2)
                if after1:
                    if at == 1:
                        pe.wait_ge(B2["wlow"], 2)
                    block_qkv(t - 1, after2)
                if after2:
                    block_turn_new(t - 2)
                if now:
                    agg_edges(t, k, 2)
                if after2:
                    block_products(t - 2)
                if after1:
                    block_scores(t - 1)
                if now:
                    agg_edges(t, k, 3)

            def turn_query(s, t):
                pe.wait_ge(s["xq"], t + 1)
                for c in range(DC):
                    last = nc.tensor.transpose(ps[:, 7, c * P:(c + 1) * P], xq[:, c * P:(c + 1) * P], ident[:, :])
                last.then_inc(s["xqturned"], 1)

            def query3(s, t, wt):
                pe.wait_ge(s["xq"], t + 1)
                cols(7, wt, 0, DC, xqT).then_inc(s["query"], 1)

            def query(s, t, wt, chunks):
                pe.wait_ge(s["xqflat"], t + 1)
                cols(7, wt, 0, chunks, xqT).then_inc(s["query"], 1)

            def turn(s, n, q, k):
                if q == 0:
                    pe.wait_ge(s["exp"], n + 1)
                b = q % 2
                pe.wait_ge(s["ev1"] if b else s["ev0"], n * 2 + q // 2)
                for j in range(QT):
                    last = nc.tensor.transpose(ps[:, 4 + b, j * P:(j + 1) * P],
                                               wts[:, k, (q * QT + j) * P:(q * QT + j + 1) * P], ident[:, :])
                last.then_inc(s["trn1"] if b else s["trn0"], 1)

            def mix(s, n, q, v, lo, width):
                b = q % 2
                pe.wait_ge(s["ev1"] if b else s["ev0"], n * 2 + (q // 2 + 1))
                for j in range(QT):
                    jt = q * QT + j
                    last = mm(ps[:, 6, lo:lo + width], wtsT[:, q, j * P:(j + 1) * P], v[:, jt, lo:lo + width],
                              start=(jt == 0), stop=(jt == NT - 1))
                if q == Q - 1:
                    last.then_inc(s["pv"], 1)

            def scores2(t, h):
                if h == 0:
                    pe.wait_ge(S3["qkept"], t + 1)
                pe.wait_ge(S3["max"], t * H + h)
                lo = h % 2 * KD
                for q in range(Q):
                    last = mm(ps[:, q, :], qT[lo:lo + KD, h // 2, :], KT2[lo:lo + KD, h // 2, q * BANK:(q + 1) * BANK],
                              start=True, stop=True)
                last.then_inc(S3["qk"], 1)

            def turn_mixed(t):
                pe.wait_ge(S3["mixed"], t + 1)
                for c in range(HC):
                    last = nc.tensor.transpose(ps[:, 7, c * P:(c + 1) * P], mixed[:, c * P:(c + 1) * P], ident[:, :])
                last.then_inc(S3["mturned"], 1)

            def project_mixed(t):
                pe.wait_ge(S3["mflat"], t + 1)
                for c in range(HC):
                    last = mm(ps[:, 7, 0:D], mixedT[:, c, :], wo[:, c, :], start=(c == 0), stop=(c == HC - 1))
                last.then_inc(S3["wo"], 1)

            def next_products(s, t, wt):
                pe.wait_ge(s["flat"], t + 1)
                for c in range(DC):
                    last = mm(ps[:, 7, D:2 * D], xnewT[:, c, :], wt[:, c, :], start=(c == 0), stop=(c == DC - 1))
                last.then_inc(s["proj"], 1)

            def body2(t, first, last):
                for h in range(H):
                    n = t * H + h
                    if h < H - 1:
                        scores2(t, h + 1)
                    elif not last:
                        scores2(t + 1, 0)
                    if h == 0 and not first:
                        turn_mixed(t - 1)
                    if h == 1 and not first:
                        project_mixed(t - 1)
                    if h == 5 and not last:
                        if not first:
                            pe.wait_ge(S3["read"], t)
                        turn_query(S3, t + 1)
                    if h == 6 and not last:
                        query(S3, t + 1, wq, HC)
                    lo = h * KD
                    turn(S3, n, 0, h % 2)
                    turn(S3, n, 1, h % 2)
                    mix(S3, n, 0, V2, lo, KD)
                    turn(S3, n, 2, h % 2)
                    mix(S3, n, 1, V2, lo, KD)
                    turn(S3, n, 3, h % 2)
                    mix(S3, n, 2, V2, lo, KD)
                    mix(S3, n, 3, V2, lo, KD)

            def product_pass(before, products):
                def tile(t, first):
                    pe.wait_ge(PJ["xq"], t + (before + 1))
                    if not first:
                        pe.wait_ge(PJ["kept"], t + before)
                    for c in range(DC):
                        last = nc.tensor.transpose(ps[:, 7, c * P:(c + 1) * P], xq[:, c * P:(c + 1) * P], ident[:, :])
                    last.then_inc(PJ["turned"], 1)
                    pe.wait_ge(PJ["flat"], t + (before + 1))
                    products().then_inc(PJ["proj"], 1)

                tile(0, True)
                with pe.Fori(1, NT) as t:
                    tile(t, False)
                pe.wait_ge(PJ["kept"], before + NT)

            def products2():
                cols(5, wk, 0, HC, xnewT)
                return rows(6, 0, wv, HD)

            def products3():
                return rows(6, 0, w_value[:, 0], D)

            def general_layer2():
                pe.wait_ge(S2["read"], NT)
                product_pass(0, products2)
                turn_query(S3, 0)
                query(S3, 0, wq, HC)
                scores2(0, 0)
                body2(0, True, False)
                with pe.Fori(1, NT - 1) as t:
                    body2(t, False, False)
                body2(NT - 1, False, True)
                turn_mixed(NT - 1)
                project_mixed(NT - 1)
                product_pass(NT, products3)

            pe.wait_ge(S1["query_weights"], 3)
            pe.wait_ge(S1["kept_g"], NT)
            for q in range(Q):
                agg_gates(0, 0, 0, q)
            pe.wait_ge(S1["kept_h"], NT)
            flag = chosen(pe)
            with pe.If(flag > 0):
                staggered(pe, stage2_blocks)
            with pe.Else():
                def stage2_alone(t, k, r):
                    for q in range(Q):
                        agg_gates(t, k, r, q)
                    for q in range(Q):
                        agg_edges(t, k, q)

                for q in range(Q):
                    agg_edges(0, 0, q)
                stage2_alone(1, 1, 0)
                with pe.Fori(1, NT // 2) as u:
                    stage2_alone(u * 2, 0, u)
                    stage2_alone(u * 2 + 1, 1, u)
                general_layer2()

            def scores3(s, t, c, chunks_ready=None):
                if c == 0:
                    pe.wait_ge(s["qlow"], t + 1)
                    if chunks_ready is None:
                        pe.wait_ge(s["exp"], t)
                for n, (a, b) in enumerate(((QH, KH), (QH, KL), (QL, KH))):
                    for q in range(Q):
                        if chunks_ready is not None and n < 2:
                            pe.wait_ge(SPLIT["klow"] if n else SPLIT["khigh"], chunks_ready + q * DC + c + 1)
                        last = mm(ps[:, q, :], a[:, c, :], b[:, c, q * BANK:(q + 1) * BANK],
                                  start=(c == 0 and n == 0), stop=(c == DC - 1 and n == 2))
                if c == DC - 1:
                    last.then_inc(s["qk"], 1)

            def turn3(s, t, q, k):
                if q == 0:
                    pe.wait_ge(s["exp"], t + 1)
                b = q % 2
                if not (isinstance(t, int) and t == 0 and q < 2):
                    pe.wait_ge(s["cut"], t * Q + (q - 1))
                for j in range(QT):
                    last = nc.tensor.transpose(ps[:, 4 + b, j * P:(j + 1) * P],
                                               wts[:, k, (q * QT + j) * P:(q * QT + j + 1) * P], ident[:, :])
                last.then_inc(s["trn1"] if b else s["trn0"], 1)

            def mix3(s, t, q):
                pe.wait_ge(s["low"], t * Q + (q + 1))
                for j in range(QT):
                    jt = q * QT + j
                    for n, (a, b) in enumerate(((WH, VH), (WH, VL), (WL, VH))):
                        last = mm(ps[:, 6, 0:D], a[:, q, j * P:(j + 1) * P], b[:, jt, :],
                                  start=(jt == 0 and n == 0), stop=(jt == NT - 1 and n == 2))
                if q == Q - 1:
                    last.then_inc(s["pv"], 1)

            def step3(s, wt, wnext, values_split):
                def body(t, k, r):
                    at = t if isinstance(t, int) else NT // 2
                    turn3(s, t, 0, k)
                    turn3(s, t, 1, k)
                    if at < NT - 1:
                        scores3(s, t + 1, 0)
                    turn3(s, t, 2, k)
                    turn3(s, t, 3, k)
                    if at < NT - 1:
                        scores3(s, t + 1, 1)
                    if at > 0:
                        if wnext is not None:
                            if at > 1:
                                pe.wait_ge(s["kept"], t - 1)
                            turn_new(s, t - 1)
                        pe.wait_ge(s["read"], t)
                    else:
                        pe.wait_ge(SPLIT["vlow"], values_split)
                    mix3(s, t, 0)
                    if at > 0 and wnext is not None:
                        next_products(s, t - 1, wnext)
                    mix3(s, t, 1)
                    mix3(s, t, 2)
                    if at < NT - 2:
                        if at > 0 and wnext is not None:
                            pe.wait_ge(s["kept"], t)
                        query3(s, t + 2, wt)
                    mix3(s, t, 3)
                return body

            for i, (s, prev, wt, wnext) in enumerate(((S4, L2, w_query[:, 0], w_value[:, 1]), (S5, S4, w_query[:, 1], None))):
                pe.wait_ge(prev["kept"], NT)
                query3(s, 0, wt)
                for c in range(DC):
                    scores3(s, 0, c, i * DC * Q)
                query3(s, 1, wt)
                two_by_two(pe, step3(s, wt, wnext, (i + 1) * DC * Q))
                if wnext is not None:
                    pe.wait_ge(s["kept"], NT - 1)
                    turn_new(s, NT - 1)
                    next_products(s, NT - 1, wnext)

        @block.scalar
        def _(act):
            def flatten(s, t):
                act.wait_ge(s["turned"], t + 1)
                nc.scalar.copy(xnewT[:, :, :].rearrange("p c n -> p (c n)"), ps[:, 7, 0:D]).then_inc(s["flat"], 1)

            def stage0(t, k):
                act.wait_ge(S0["turned"], t + 1)
                to = xqT if k else xnewT
                nc.scalar.copy(to[:, :, :].rearrange("p c n -> p (c n)"), ps[:, 7 - k, 0:D]).then_inc(S0["flat"], 1)

            def h0_high(t, k):
                act.wait_ge(S0["read"], t + 1)
                nc.scalar.copy(H0H[:, t, :], h0[k]).then_inc(S0["high"], 1)

            def slab_high(t, k, r):
                act.wait_ge(S1["slab1"] if k else S1["slab0"], r * 16 + 16)
                if not (isinstance(t, int) and t < 2):
                    act.wait_ge(S1["agg"], t - 1)
                nc.scalar.copy(AH[k][:, :], slab[:, k, :]).then_inc(S1["high"], 1)

            stage0(0, 0)
            for first, end in ((0, NT // 2 - 3), (NT // 2 - 3, NT // 2 - 1)):
                with act.Fori(first, end) as u:
                    stage0(u * 2 + 1, 1)
                    h0_high(u * 2, 0)
                    stage0(u * 2 + 2, 0)
                    h0_high(u * 2 + 1, 1)
                if first == 0:
                    slab_high(0, 0, 0)
            stage0(NT - 1, 1)
            h0_high(NT - 2, 0)
            h0_high(NT - 1, 1)
            slab_high(1, 1, 0)

            act.wait_ge(S1["query_weights"], 1)
            for i in range(2):
                nc.scalar.copy(w_query[:, i].rearrange("p c n -> p (c n)"), ps[:, 2 + i, :]).then_inc(S1["query_weights"], 1)

            def stage1(t):
                flatten(S1, t)
                act.wait_ge(S1["proj"], t + 1)
                nc.scalar.copy(left_rows[:, bass.ts(t, P)], ps[:, 4, 0:P])
                nc.scalar.copy(GB[:, t, :], ps[:, 6, 0:GW]).then_inc(S1["kept_g"], 1)

            with act.Fori(0, NT // 2 - 1) as u:
                for k in range(2):
                    slab_high(u * 2 + (k + 2), k, u + 1)
                    stage1(u * 2 + k)
            stage1(NT - 2)
            stage1(NT - 1)

            def edge_exp(t, k):
                act.wait_ge(S2["raw"], t + 1)
                nc.scalar.activation(wts[:, k, :], wts[:, k, :], ACT.Exp, scale=-1.0).then_inc(S2["exp"], 1)

            def gate_exp(t):
                act.wait_ge(S2["gate"], t + 1)
                nc.scalar.activation(g1[:, 4:6], g1[:, 2:4], ACT.Exp, scale=-1.0).then_inc(S2["gexp"], 1)

            def z_exp(t):
                act.wait_ge(S2["z"], t + 1)
                nc.scalar.activation(res2[:, :], res3[:, :], ACT.Exp, scale=-1.0).then_inc(S2["zexp"], 1)

            def flat2(a):
                return a.rearrange("p c n -> p (c n)")

            def keys_high(stage, quarters):
                for piece, _ in key_pieces(stage, quarters):
                    nc.scalar.copy(flat2(KH[:, :, :])[:, piece], flat2(KT3[:, :, :])[:, piece]).then_inc(SPLIT["khigh"], 1)

            def stage2_blocks(t, k, r):
                at = t if isinstance(t, int) else NT // 2
                now, after1, after2 = at < NT, 0 < at <= NT, 1 < at
                if after1:
                    gate_exp(t - 1)
                    z_exp(t - 1)
                if after2:
                    act.wait_ge(B2["pturned"], t - 1)
                    nc.scalar.copy(flat2(pbT[:, 4:8, :]), ps[:, 7, :]).then_inc(B2["pflat_a"], 1)
                if at == NT + 1:
                    keys_high(0, range(Q - 1))
                if after2:
                    act.wait_ge(B2["mturned"], t - 1)
                    nc.scalar.copy(flat2(mixedTH[:, :, :]), ps[:, 5, :]).then_inc(B2["mflat"], 1)
                if after1:
                    flatten(S2, t - 1)
                    act.wait_ge(S2["flat"], t)
                    nc.scalar.copy(xTH[:, :, :], xnewT[:, :, :]).then_inc(B2["xhigh"], 1)
                    act.wait_ge(B2["qkv"], t * 3 - 2)
                    nc.scalar.activation(flat2(qT[:, :, :]), ps[:, 4, :], ACT.Copy, scale=KEY_SCALE).then_inc(B2["qflat"], 1)
                    act.wait_ge(B2["qkv"], t * 3 - 1)
                    for a in range(2):
                        half = slice(a * KD, (a + 1) * KD)
                        nc.scalar.copy(kb[half, :, a, :], ps[half, 6, :].rearrange("p (c n) -> p c n", c=HC))
                    act.wait_ge(B2["qkv"], t * 3)
                    nc.scalar.copy(vb[:, :], ps[:, 7, :]).then_inc(B2["kvkept"], 1)
                if after2:
                    act.wait_ge(B2["turned"], t - 1)
                    nc.scalar.copy(flat2(x3T[:, :, :]), ps[:, 5, 0:D]).then_inc(B2["flat"], 1)
                    act.wait_ge(B2["flat"], t - 1)
                    nc.scalar.copy(KT3[:, :, bass.ts(t - 2, P)], x3T[:, :, :])
                if at < NT - 1:
                    edge_exp(t + 1, 1 - k)
                if after2:
                    act.wait_ge(B2["proj"], t - 1)
                    nc.scalar.copy(V3[:, t - 2, :], ps[:, 5, D:2 * D]).then_inc(L2["kept"], 1)
                if after1:
                    act.wait_ge(B2["max"], t)
                    for h in range(H):
                        last = nc.scalar.activation(pb[:, h, :], pb[:, h, :], ACT.Exp, bias=nmax[:, h:h + 1],
                                                    accum_out=rsum[:, h:h + 1])
                    last.then_inc(B2["exp"], 1)

            def flatten_query(s, t):
                act.wait_ge(s["xqturned"], t + 1)
                nc.scalar.copy(xqT[:, :, :].rearrange("p c n -> p (c n)"), ps[:, 7, 0:D]).then_inc(s["xqflat"], 1)

            def keep_query(s, t, width, scale):
                act.wait_ge(s["query"], t + 1)
                nc.scalar.activation(qT[:, :, :].rearrange("p c n -> p (c n)")[:, 0:width], ps[:, 7, 0:width], ACT.Copy,
                                     scale=scale).then_inc(s["qkept"], 1)

            def keep_next(s, t):
                act.wait_ge(s["flat"], t + 1)
                nc.scalar.copy(KT3[:, :, bass.ts(t, P)], xnewT[:, :, :])
                act.wait_ge(s["proj"], t + 1)
                nc.scalar.copy(V3[:, t, :], ps[:, 7, D:2 * D]).then_inc(s["kept"], 1)

            def exp2(n, h):
                act.wait_ge(S3["max"], n + 1)
                nc.scalar.activation(wts[:, h % 2, :], wts[:, h % 2, :], ACT.Exp, bias=nmax[:, h:h + 1],
                                     accum_out=rsum[:, h:h + 1]).then_inc(S3["exp"], 1)

            def flatten_mixed(t):
                act.wait_ge(S3["mturned"], t + 1)
                nc.scalar.copy(mixedT[:, :, :].rearrange("p c n -> p (c n)"), ps[:, 7, :]).then_inc(S3["mflat"], 1)

            def body2(t, first, last):
                for h in range(H):
                    n = t * H + h
                    if h < H - 1 or not last:
                        exp2(n + 1, (h + 1) % H)
                    if h == 0 and not first:
                        flatten_mixed(t - 1)
                    if h == 5 and not last:
                        flatten_query(S3, t + 1)
                    if h == 6 and not last:
                        keep_query(S3, t + 1, HD, KEY_SCALE)
                    for q in (1, 3):
                        act.wait_ge(S3["trn1"], n * 2 + (q // 2 + 1))
                        nc.scalar.copy(wtsT[:, q, :], ps[:, 5, :]).then_inc(S3["ev1"], 1)

            def general_layer2():
                edge_exp(1, 1)
                gate_exp(0)
                z_exp(0)
                with act.Fori(1, NT // 2) as u:
                    edge_exp(u * 2, 0)
                    gate_exp(u * 2 - 1)
                    z_exp(u * 2 - 1)
                    edge_exp(u * 2 + 1, 1)
                    gate_exp(u * 2)
                    z_exp(u * 2)
                gate_exp(NT - 1)
                z_exp(NT - 1)
                act.wait_ge(BL["blocks"], 16 * NT)
                act.wait_ge(S2["read"], NT)
                with act.Fori(0, NT) as t:
                    flatten(PJ, t)
                    act.wait_ge(PJ["proj"], t + 1)
                    nc.scalar.copy(KT2[:, :, bass.ts(t, P)], ps[:, 5, :].rearrange("p (c n) -> p c n", c=HC))
                    nc.scalar.copy(V2[:, t, :], ps[:, 6, :]).then_inc(PJ["kept"], 1)
                flatten_query(S3, 0)
                keep_query(S3, 0, HD, KEY_SCALE)
                exp2(0, 0)
                body2(0, True, False)
                with act.Fori(1, NT - 1) as t:
                    body2(t, False, False)
                body2(NT - 1, False, True)
                flatten_mixed(NT - 1)
                with act.Fori(0, NT) as t:
                    flatten(PJ, t + NT)
                    act.wait_ge(PJ["flat"], t + (NT + 1))
                    nc.scalar.copy(KT3[:, :, bass.ts(t, P)], xnewT[:, :, :])
                    act.wait_ge(PJ["proj"], t + (NT + 1))
                    nc.scalar.copy(V3[:, t, :], ps[:, 6, 0:D]).then_inc(PJ["kept"], 1)
                    act.wait_ge(PJ["kept"], t + (NT + 1))
                    act.sem_inc(L2["kept"], 1)

            edge_exp(0, 0)
            flag = chosen(act)
            with act.If(flag > 0):
                act.wait_ge(B2["cleared"], 1)
                for whole_weights, high in ((wv, WvH), (wo, WoH)):
                    nc.scalar.copy(flat2(high[:, :, :]), flat2(whole_weights[:, :, :])).then_inc(B2["whigh"], 1)
                staggered(act, stage2_blocks)
            with act.Else():
                general_layer2()
                keys_high(0, range(Q - 1))

            def exp3(s, t, k):
                act.wait_ge(s["max"], t + 1)
                if not (isinstance(t, int) and t < 2):
                    act.wait_ge(s["trn1"], t * 2 - 2)
                nc.scalar.activation(wts[:, k, :], ps[:, 0:Q, :].rearrange("p q n -> p (q n)"), ACT.Exp,
                                     bias=nmax[:, k:k + 1], accum_out=rsum[:, k:k + 1]).then_inc(s["exp"], 1)

            def query_high(s, t):
                act.wait_ge(s["query"], t + 1)
                nc.scalar.copy(QH[:, :, :].rearrange("p c n -> p (c n)"), ps[:, 7, 0:D]).then_inc(s["qhigh"], 1)

            def weights_high(s, t, q):
                act.wait_ge(s["cut"], t * Q + (q + 1))
                nc.scalar.copy(WH[:, q, :], whole[q % 2]).then_inc(s["high"], 1)

            def step3(s, makes_next):
                def body(t, k, r):
                    at = t if isinstance(t, int) else NT // 2
                    for q in range(Q):
                        weights_high(s, t, q)
                    if at > 0 and makes_next:
                        flatten(s, t - 1)
                    if at > 0 and makes_next:
                        if at == 1:
                            act.wait_ge(SPLIT["klow"], DC * Q)
                            act.wait_ge(SPLIT["vlow"], DC * Q)
                        keep_next(s, t - 1)
                    if at < NT - 1:
                        exp3(s, t + 1, 1 - k)
                    if at < NT - 2:
                        query_high(s, t + 2)
                    if at == NT - 1 and makes_next:
                        act.wait_ge(s["qk"], NT)
                        keys_high(1, range(Q - 1))
                return body

            for i, (s, prev) in enumerate(((S4, L2), (S5, S4))):
                act.wait_ge(prev["kept"], NT)
                query_high(s, 0)
                keys_high(i, (Q - 1,))
                for n in range(DC * Q):
                    piece = slice(n * BANK, (n + 1) * BANK)
                    nc.scalar.copy(flat2(VH[:, :, :])[:, piece], flat2(V3[:, :, :])[:, piece]).then_inc(SPLIT["vhigh"], 1)
                exp3(s, 0, 0)
                query_high(s, 1)
                two_by_two(act, step3(s, s is S4))
                if s is S4:
                    flatten(s, NT - 1)
                    keep_next(s, NT - 1)

        @block.vector
        def _(dve):
            v = nc.vector

            class Chain:
                def __init__(self, s, t, per_tile):
                    self.sem, self.base, self.per_tile, self.n = s, t * per_tile, per_tile, 0

                def then(self, instruction):
                    instruction.then_inc(self.sem, 1)
                    self.n += 1
                    dve.wait_ge(self.sem, self.base + self.n)

                def done(self):
                    assert self.n == self.per_tile, self.n

            def layernorm(s, t, c, src, dst):
                v.bn_stats(bn[:, :], src).then_inc(s["stats"], 1)
                dve.wait_ge(init["early"], 32)
                dve.wait_ge(s["stats"], t + 1)
                c.then(v.bn_aggr(mv[:, :], bn[:, :]))
                v.tensor_scalar(veps[:, :], mv[:, 1:2], EPS, None, ALU.add).then_inc(s["var"], 1)
                dve.wait_ge(s["std"], t + 1)
                v.tensor_scalar(dst, src, mv[:, 0:1], rstd[:, :], ALU.subtract, ALU.mult).then_inc(s["new"], 1)

            dve.wait_ge(init["early"], 32)
            def h0_whole(t, k):
                dve.wait_ge(S0["proj"], t + 1)
                if not (isinstance(t, int) and t < 2):
                    dve.wait_ge(S0["kept"], t - 1)
                v.tensor_tensor(h0[k], ps[:, 5 - k, 0:D], b0r[:, :], ALU.add).then_inc(S0["read"], 1)

            def h0_low(t, k):
                dve.wait_ge(S0["high"], t + 1)
                v.tensor_tensor(H0L[:, t, :], h0[k], H0H[:, t, :], ALU.subtract).then_inc(S0["kept"], 1)

            def slab_low(k):
                dve.wait_ge(S1["high"], k + 1)
                v.tensor_tensor(AL[k][:, :], slab[:, k, :], AH[k][:, :], ALU.subtract).then_inc(S1["low"], 1)

            h0_whole(0, 0)
            h0_whole(1, 1)
            h0_low(0, 0)
            with dve.Fori(1, NT // 2 - 1) as u:
                h0_whole(u * 2, 0)
                h0_low(u * 2 - 1, 1)
                h0_whole(u * 2 + 1, 1)
                h0_low(u * 2, 0)
            h0_whole(NT - 2, 0)
            h0_low(NT - 3, 1)
            slab_low(0)
            h0_whole(NT - 1, 1)
            h0_low(NT - 2, 0)
            h0_low(NT - 1, 1)
            slab_low(1)

            dve.wait_ge(init["late"], 16 * LATE)
            dve.wait_ge(init["consts"], 4)
            for c in range(DC):
                v.scalar_tensor_tensor(res[:, :], wsa[:, c, 0:D], 1.0, asr[:, 0:D], ALU.mult, ALU.mult,
                                       accum_out=wleft[:, c:c + 1]).then_inc(S1["weights"], 1)
                dve.wait_ge(S1["weights"], 2 * c + 1)
                v.scalar_tensor_tensor(res[:, :], wsa[:, c, 0:D], 1.0, asr[:, D:2 * D], ALU.mult, ALU.mult,
                                       accum_out=wsa[:, c, D:D + 1]).then_inc(S1["weights"], 1)
                dve.wait_ge(S1["weights"], 2 * c + 2)
            for c in range(DC):
                v.tensor_scalar(left_wt[:, c, :], ident[:, :], 0.0, wleft[:, c:c + 1], ALU.mult,
                                ALU.add).then_inc(S1["weights"], 1)

            for i, wt in ((1, wq), (3, wk)):
                v.tensor_reduce(extremes[:, i:i + 1], wt[:, :, :].rearrange("p c n -> p (c n)"), AX.X, ALU.max)
                v.tensor_reduce(extremes[:, i + 1:i + 2], wt[:, :, :].rearrange("p c n -> p (c n)"), AX.X, ALU.min, negate=True)

            def find_block_max(t, k, r):
                dve.wait_ge(S1["slab1"] if k else S1["slab0"], r * 16 + 16)
                v.tensor_reduce(block_max[:, bass.ts(t, NT)], slab[:, k, :].rearrange("p (j n) -> p j n", j=NT), AX.X,
                                ALU.max).then_inc(FL["seen"], 1)

            def stage1(t, k, r, more=2):
                c = Chain(S1["chain"], t, 1)
                dve.wait_ge(S1["agg"], t + 1)
                v.tensor_tensor(res[:, :], ps[:, k, 0:D], X[:, t, :], ALU.add).then_inc(S1["read"], 1)
                dve.wait_ge(S1["read"], t + 1)
                if not (isinstance(t, int) and t == 0):
                    dve.wait_ge(S1["turned"], t)
                    dve.wait_ge(S1["stored"], t)
                layernorm(S1, t, c, res[:, :], xnew[:, :])
                if more:
                    find_block_max(t + 1, 1 - k, r + k)
                if more > 1:
                    dve.wait_ge(S1["high"], t + 3)
                    v.tensor_tensor(AL[k][:, 0:CUT], slab[:, k, 0:CUT], AH[k][:, 0:CUT],
                                    ALU.subtract).then_inc(S1["low_start"], 1)
                dve.wait_ge(S1["proj"], t + 1)
                v.tensor_copy(HA[:, t, 0:D], ps[:, 5, 0:D])
                v.tensor_copy(right_cols[:, bass.ts(t, 1)], ps[:, 5, D:D + 1]).then_inc(S1["kept_h"], 1)
                c.done()

            flat_masks = mb[:, :, :].rearrange("p t n -> p (t n)")
            dve.wait_ge(BL["blocks"], 16 * NT)
            v.tensor_scalar(flat_masks, flat_masks, 0.0, -1.0, ALU.max, ALU.add).then_inc(BL["masked"], 1)
            find_block_max(0, 0, 0)
            stage1(0, 0, 0)
            dve.wait_ge(BL["masked"], 1)
            v.tensor_tensor(mb[:, :, :], mb[:, :, :], eye_less_one[:, :].unsqueeze(1).broadcast_to([P, NT, P]),
                            ALU.max).then_inc(BL["masked"], 1)
            stage1(1, 1, 0)
            dve.wait_ge(BL["masked"], 2)
            v.tensor_scalar(flat_masks, flat_masks, HUGE, None, ALU.mult).then_inc(BL["masked"], 1)
            with dve.Fori(1, NT // 2 - 1) as u:
                stage1(u * 2, 0, u)
                stage1(u * 2 + 1, 1, u)
            stage1(NT - 2, 0, NT // 2 - 1, more=1)
            stage1(NT - 1, 1, NT // 2 - 1, more=0)

            def slope_scores(t, k):
                if isinstance(t, int) and t == 0:
                    v.tensor_tensor(wts[:, k, :].rearrange("p (j n) -> p j n", j=NT),
                                    left_rows[:, 0:P].unsqueeze(1).broadcast_to([P, NT, P]),
                                    right_cols[:, :].unsqueeze(2).broadcast_to([P, NT, P]), ALU.add).then_inc(S2["first"], 1)
                    dve.wait_ge(S2["first"], 1)
                else:
                    dve.wait_ge(S2["sum"], t)
                v.scalar_tensor_tensor(wts[:, k, :], wts[:, k, :], SLOPE, wts[:, k, :], ALU.mult, ALU.max).then_inc(S2["score"], 1)

            def clamp_scores(t, k):
                dve.wait_ge(S2["score"], t + 1)
                v.tensor_scalar(wts[:, k, :], wts[:, k, :], LEAST_SCORE, None, ALU.max).then_inc(S2["raw"], 1)

            def keep_edges(t, k, r):
                dve.wait_ge(S2["exp"], t + 1)
                dve.wait_ge(S2["slab1"] if k else S2["slab0"], r * 16 + 16)
                v.scalar_tensor_tensor(wts[:, k, :], slab[:, k, :], 0.0, wts[:, k, :], ALU.not_equal, ALU.mult).then_inc(S2["edge"], 1)

            def mix_gates2(t, k):
                c = Chain(S2["mixing"], t, 7)
                dve.wait_ge(S2["agg"], t + 1)
                c.then(v.tensor_scalar(g1[:, 0:1], ps[:, k, D:D + 1], EPS, None, ALU.add))
                c.then(v.reciprocal(g1[:, 1:2], g1[:, 0:1]))
                c.then(v.tensor_tensor(g1[:, 2:4], ps[:, 2 + k, D:D + 2], GB[:, t, D + 2:GW], ALU.add))
                v.tensor_tensor(g1[:, 2:4], g1[:, 2:4], bar[:, :], ALU.add).then_inc(S2["gate"], 1)
                dve.wait_ge(S2["gexp"], t + 1)
                c.then(v.tensor_scalar(g1[:, 4:6], g1[:, 4:6], 1.0, None, ALU.add))
                c.then(v.reciprocal(g1[:, 6:8], g1[:, 4:6]))
                c.then(v.tensor_tensor(g1[:, 0:1], g1[:, 6:7], g1[:, 1:2], ALU.mult))
                c.then(v.tensor_tensor(res[:, :], ps[:, 2 + k, 0:D], bgr[:, :], ALU.add))
                v.tensor_scalar(res2[:, :], ps[:, k, 0:D], g1[:, 0:1], None, ALU.mult).then_inc(S2["read"], 1)
                dve.wait_ge(S2["read"], t + 1)
                v.scalar_tensor_tensor(res3[:, :], res[:, :], g1[:, 7:8], res2[:, :], ALU.mult, ALU.add).then_inc(S2["z"], 1)
                c.done()

            def add_gated2(t):
                c = Chain(S2["chain"], t, 3)
                dve.wait_ge(S2["zexp"], t + 1)
                c.then(v.tensor_scalar(res[:, :], res2[:, :], 1.0, None, ALU.add))
                c.then(v.reciprocal(res2[:, :], res[:, :]))
                c.then(v.tensor_tensor(res[:, :], res2[:, :], X[:, t, :], ALU.add))
                c.done()

            def finish2(t):
                c = Chain(S2["norm"], t, 1)
                dve.wait_ge(S2["stored"], t)
                layernorm(S2, t, c, res[:, :], xnew[:, :])
                c.done()

            def block_softmax(t):
                dve.wait_ge(B2["scores"], t + 1)
                v.tensor_tensor(pb[:, :, :], ps[:, 6:8, :].rearrange("p b (h n) -> p (b h) n", h=4),
                                mb[:, t, :].unsqueeze(1).broadcast_to([P, H, P]), ALU.add).then_inc(B2["masked"], 1)
                dve.wait_ge(B2["masked"], t + 1)
                v.tensor_reduce(nmax[:, :], pb[:, :, :], AX.X, ALU.max, negate=True).then_inc(B2["max"], 1)

            def flat2(a):
                return a.rearrange("p c n -> p (c n)")

            def keys_low(stage, quarters):
                for piece, count in key_pieces(stage, quarters):
                    dve.wait_ge(SPLIT["khigh"], count)
                    v.tensor_tensor(flat2(KL[:, :, :])[:, piece], flat2(KT3[:, :, :])[:, piece], flat2(KH[:, :, :])[:, piece],
                                    ALU.subtract).then_inc(SPLIT["klow"], 1)

            def block_flat(t):
                dve.wait_ge(B2["pturned"], t + 1)
                v.tensor_copy(pbT[:, 0:4, :].rearrange("p h n -> p (h n)"), ps[:, 6, :]).then_inc(B2["pflat_d"], 1)

            def block_invert(t):
                dve.wait_ge(B2["exp"], t + 1)
                v.reciprocal(rinv[:, :], rsum[:, :]).then_inc(B2["inv"], 1)

            def block_scale(t):
                dve.wait_ge(B2["ctx"], t + 1)
                dve.wait_ge(B2["inv"], t + 1)
                v.tensor_tensor(mixed[:, :].rearrange("p (h k) -> p h k", h=H), ps[:, 4, :].rearrange("p (h k) -> p h k", h=H),
                                rinv[:, :].unsqueeze(2).broadcast_to([P, H, KD]), ALU.mult).then_inc(B2["mixed"], 1)

            def block_residual(t):
                dve.wait_ge(B2["wo"], t + 1)
                v.tensor_tensor(x3res[:, :], ps[:, 6, 0:D], X[:, t, :], ALU.add).then_inc(B2["res"], 1)
                dve.wait_ge(B2["res"], t + 1)
                v.bn_stats(bn3[:, :], x3res[:, :]).then_inc(B2["stats"], 1)

            def block_finish(t):
                dve.wait_ge(init["early"], 32)
                dve.wait_ge(B2["stats"], t + 1)
                v.bn_aggr(mv3[:, :], bn3[:, :]).then_inc(B2["agg"], 1)
                dve.wait_ge(B2["agg"], t + 1)
                v.tensor_scalar(veps3[:, :], mv3[:, 1:2], EPS, None, ALU.add).then_inc(B2["var"], 1)
                dve.wait_ge(B2["std"], t + 1)
                v.tensor_scalar(x3[:, :], x3res[:, :], mv3[:, 0:1], rstd3[:, :], ALU.subtract, ALU.mult).then_inc(B2["new"], 1)

            def stage2_blocks(t, k, r):
                at = t if isinstance(t, int) else NT // 2
                now, after1, after2 = at < NT, 0 < at <= NT, 1 < at
                if after1:
                    mix_gates2(t - 1, 1 - k)
                if after2:
                    block_flat(t - 2)
                    block_invert(t - 2)
                if after1:
                    add_gated2(t - 1)
                if after2:
                    block_scale(t - 2)
                if at == NT + 1:
                    keys_low(0, range(Q - 1))
                if after1:
                    finish2(t - 1)
                if after2:
                    dve.wait_ge(B2["mflat"], t - 1)
                    v.tensor_tensor(flat2(mixedTL[:, :, :]), ps[:, 5, :], flat2(mixedTH[:, :, :]),
                                    ALU.subtract).then_inc(B2["mlow"], 1)
                if at < NT - 1:
                    slope_scores(t + 1, 1 - k)
                if after2:
                    block_residual(t - 2)
                if at < NT - 1:
                    clamp_scores(t + 1, 1 - k)
                if after1:
                    dve.wait_ge(B2["xhigh"], t)
                    v.tensor_tensor(xTL[:, :, :], xnewT[:, :, :], xTH[:, :, :], ALU.subtract).then_inc(B2["xlow"], 1)
                if after2:
                    block_finish(t - 2)
                if after1:
                    block_softmax(t - 1)
                if at < NT - 1:
                    keep_edges(t + 1, 1 - k, r + k)

            def make_mask(t):
                dve.wait_ge(S3["slab0"], t * 16 + 16)
                v.tensor_scalar(mask, slab[:, 0, :], 0.0, -1.0, ALU.max, ALU.add).then_inc(S3["masked"], 1)
                dve.wait_ge(S3["masked"], t + 1)
                v.tensor_tensor(mask[:, bass.ts(t, P)], mask[:, bass.ts(t, P)], eye_less_one[:, :], ALU.max).then_inc(S3["step"], 1)
                dve.wait_ge(S3["step"], t * 2 + 1)
                v.tensor_scalar(mask, mask, HUGE, None, ALU.mult).then_inc(S3["step"], 1)
                dve.wait_ge(S3["step"], t * 2 + 2)

            def mask_scores(n, h):
                dve.wait_ge(S3["qk"], n + 1)
                if not (isinstance(n, int) and n < 2):
                    dve.wait_ge(S3["trn1"], n * 2 - 2)
                dve.sem_inc(S3["waited"], 1)
                v.tensor_tensor_reduce(wts[:, h % 2, :], ps[:, 0:Q, :].rearrange("p q n -> p (q n)"), mask, 1.0, -3e38,
                                       ALU.add, ALU.max, rmax[:, h:h + 1]).then_inc(S3["rowmax"], 1)
                dve.wait_ge(S3["rowmax"], n + 1)
                v.tensor_scalar(nmax[:, h:h + 1], rmax[:, h:h + 1], -1.0, None, ALU.mult).then_inc(S3["max"], 1)

            def invert_sums(t):
                dve.wait_ge(S3["exp"], t * H + H)
                v.reciprocal(rinv[:, :], rsum[:, :]).then_inc(S3["inv"], 1)

            def scale_mixed(t):
                dve.wait_ge(S3["pv"], t * H + H)
                dve.wait_ge(S3["inv"], t + 1)
                v.tensor_tensor(mixed[:, :].rearrange("p (h k) -> p h k", h=H), ps[:, 6, :].rearrange("p (h k) -> p h k", h=H),
                                rinv[:, :].unsqueeze(2).broadcast_to([P, H, KD]), ALU.mult).then_inc(S3["mixed"], 1)

            def finish3(t):
                c = Chain(S3["chain"], t, 1)
                dve.wait_ge(S3["wo"], t + 1)
                v.tensor_tensor(res[:, :], ps[:, 7, 0:D], X[:, t, :], ALU.add).then_inc(S3["read"], 1)
                dve.wait_ge(S3["read"], t + 1)
                layernorm(S3, t, c, res[:, :], xnew[:, :])
                c.done()

            def body2(t, first, last):
                for h in range(H):
                    n = t * H + h
                    if h == 0 and not first:
                        scale_mixed(t - 1)
                    if h == H - 1:
                        invert_sums(t)
                        if not last:
                            make_mask(t + 1)
                    if h < H - 1 or not last:
                        mask_scores(n + 1, (h + 1) % H)
                    if h == 2 and not first:
                        finish3(t - 1)
                    for q in (0, 2):
                        dve.wait_ge(S3["trn0"], n * 2 + (q // 2 + 1))
                        v.tensor_copy(wtsT[:, q, :], ps[:, 4, :]).then_inc(S3["ev0"], 1)

            def general_layer2():
                def both(t, k):
                    mix_gates2(t, k)
                    add_gated2(t)
                    finish2(t)

                def all_edges(t, k, r):
                    slope_scores(t, k)
                    clamp_scores(t, k)
                    keep_edges(t, k, r)

                all_edges(1, 1, 0)
                both(0, 0)
                with dve.Fori(1, NT // 2) as u:
                    all_edges(u * 2, 0, u)
                    both(u * 2 - 1, 1)
                    all_edges(u * 2 + 1, 1, u)
                    both(u * 2, 0)
                both(NT - 1, 1)
                dve.wait_ge(S2["stored"], NT)
                dve.wait_ge(PJ["kept"], NT)
                make_mask(0)
                mask_scores(0, 0)
                body2(0, True, False)
                with dve.Fori(1, NT - 1) as t:
                    body2(t, False, False)
                body2(NT - 1, False, True)
                scale_mixed(NT - 1)
                finish3(NT - 1)

            dve.wait_ge(FL["seen"], NT)
            v.memset(block_max[:, ::NT + 1], 0.0).then_inc(FL["cleared"], 1)
            dve.wait_ge(FL["cleared"], 1)
            v.tensor_reduce(extremes[:, 0:1], block_max[:, :], AX.X, ALU.max).then_inc(FL["reduced"], 1)
            dve.wait_ge(S1["stored"], NT)
            dve.wait_ge(S1["kept_g"], NT)
            slope_scores(0, 0)
            clamp_scores(0, 0)
            keep_edges(0, 0, 0)
            dve.wait_ge(FL["all"], 1)
            v.tensor_tensor(tests[:, 0:2], extremes_all[:, 1:4:2], extremes_all[:, 2:5:2], ALU.max).then_inc(FL["tests"], 1)
            dve.wait_ge(FL["tests"], 1)
            v.tensor_tensor(tests[:, 2:3], tests[:, 0:1], tests[:, 1:2], ALU.mult).then_inc(FL["tests"], 1)
            v.tensor_scalar(tests[:, 3:4], extremes_all[:, 0:1], 1.0, None, ALU.is_lt).then_inc(FL["tests"], 1)
            dve.wait_ge(FL["tests"], 3)
            v.scalar_tensor_tensor(blocks_only[:, :], tests[:, 2:3], WEIGHT_BOUND, tests[:, 3:4], ALU.is_le,
                                   ALU.mult).then_inc(FL["ready"], 1)
            flag = chosen(dve)
            with dve.If(flag > 0):
                dve.wait_ge(BL["masked"], 3)
                for n, (whole_weights, high, low) in enumerate(((wv, WvH, WvL), (wo, WoH, WoL))):
                    dve.wait_ge(B2["whigh"], n + 1)
                    v.tensor_tensor(low[:, :, :], whole_weights[:, :, :], high[:, :, :], ALU.subtract).then_inc(B2["wlow"], 1)
                staggered(dve, stage2_blocks)
            with dve.Else():
                general_layer2()
                keys_low(0, range(Q - 1))

            def row_max(s, t, k):
                dve.wait_ge(s["qk"], t + 1)
                v.tensor_reduce(nmax[:, k:k + 1], ps[:, 0:Q, :].rearrange("p q n -> p (q n)"), AX.X, ALU.max,
                                negate=True).then_inc(s["max"], 1)

            def cut(s, t, k, q):
                b = q % 2
                dve.wait_ge(s["trn1"] if b else s["trn0"], t * 2 + (q // 2 + 1))
                if not (isinstance(t, int) and t == 0 and q < 2):
                    dve.wait_ge(s["low"], t * Q + (q - 1))
                v.tensor_tensor(whole[b], ps[:, 4 + b, :], slab[:, k, q * BANK:(q + 1) * BANK], ALU.mult).then_inc(s["cut"], 1)

            def weights_low(s, t, q):
                dve.wait_ge(s["high"], t * Q + (q + 1))
                v.tensor_tensor(WL[:, q, :], whole[q % 2], WH[:, q, :], ALU.subtract).then_inc(s["low"], 1)

            def query_low(s, t):
                dve.wait_ge(s["qhigh"], t + 1)
                v.tensor_tensor(QL[:, :, :].rearrange("p c n -> p (c n)"), ps[:, 7, 0:D],
                                QH[:, :, :].rearrange("p c n -> p (c n)"), ALU.subtract).then_inc(s["qlow"], 1)

            def take_sum(s, t, k, x_in):
                dve.wait_ge(s["pv"], t + 1)
                v.reciprocal(rinv[:, 0:1], rsum[:, k:k + 1]).then_inc(s["inv"], 1)
                dve.wait_ge(s["inv"], t + 1)
                v.scalar_tensor_tensor(res[:, :], ps[:, 6, 0:D], rinv[:, 0:1], x_in[:, t, :], ALU.mult, ALU.add).then_inc(s["read"], 1)

            def finish4(t, k, r):
                dve.wait_ge(S4["read"], t + 1)
                dve.wait_ge(S4["turned"], t)
                dve.wait_ge(S4["stored"], t)
                v.scalar_tensor_tensor(xnew[:, :], res[:, :], SLOPE, res[:, :], ALU.mult, ALU.max).then_inc(S4["new"], 1)

            def finish5(t, k, r):
                c = Chain(S5["chain"], t, 3)
                dve.wait_ge(S5["read"], t + 1)
                c.then(v.scalar_tensor_tensor(res2[:, :], res[:, :], SLOPE, res[:, :], ALU.mult, ALU.max))
                c.then(v.tensor_tensor(res3[:, :], res2[:, :], X[:, t, :], ALU.add))
                if not (isinstance(r, int) and r == 0):
                    dve.wait_ge(S5["out1"] if k else S5["out0"], r * 16)
                layernorm(S5, t, c, res3[:, :], outt[:, k, :])
                c.done()

            def step3(s, finish, x_in):
                def body(t, k, r):
                    at = t if isinstance(t, int) else NT // 2
                    if at > 0:
                        take_sum(s, t - 1, 1 - k, x_in)
                    dve.wait_ge(s["slab1"] if k else s["slab0"], r * 16 + 16)
                    for q in (0, 2):
                        cut(s, t, k, q)
                        cut(s, t, k, q + 1)
                        weights_low(s, t, q)
                        weights_low(s, t, q + 1)
                        if at > 0 and q == 0:
                            finish(t - 1, 1 - k, r if k else r - 1)
                    if at < NT - 1:
                        row_max(s, t + 1, 1 - k)
                    if at < NT - 2:
                        query_low(s, t + 2)
                    if at == NT - 1 and s is S4:
                        keys_low(1, range(Q - 1))
                return body

            for i, (s, prev, finish, x_in) in enumerate(((S4, L2, finish4, X), (S5, S4, finish5, X4))):
                dve.wait_ge(prev["kept"], NT)
                query_low(s, 0)
                keys_low(i, (Q - 1,))
                for n in range(DC * Q):
                    piece = slice(n * BANK, (n + 1) * BANK)
                    dve.wait_ge(SPLIT["vhigh"], i * DC * Q + n + 1)
                    v.tensor_tensor(flat2(VL[:, :, :])[:, piece], flat2(V3[:, :, :])[:, piece], flat2(VH[:, :, :])[:, piece],
                                    ALU.subtract).then_inc(SPLIT["vlow"], 1)
                row_max(s, 0, 0)
                query_low(s, 1)
                two_by_two(dve, step3(s, finish, x_in))
                take_sum(s, NT - 1, 1, x_in)
                finish(NT - 1, 1, NT // 2 - 1)


def kernel(x, adj, L0_gnn_W, L0_gnn_b, L1_gnn_W_sa, L1_gnn_a_sa, L1_gnn_W_gcnb, L1_gnn_b_gcnb, L1_gnn_Wa, L1_gnn_ba,
           L1_gnn_Wb, L1_gnn_bb, L2_gnn_Wks, L2_gnn_Wqs, L2_gnn_Wvs, L2_gnn_Wo, L3_gnn_W_stack):
    import numpy as np
    import concourse.bacc as bacc
    from concourse.bass_utils import run_bass_kernel_spmd

    x, adj = np.asarray(x), np.asarray(adj)
    Wa, Wb = np.asarray(L1_gnn_Wa), np.asarray(L1_gnn_Wb)

    def heads_side_by_side(a):
        return np.asarray(a).transpose(1, 0, 2).reshape(D, HD)

    arrays = {
        "x": x,
        "adj": adj.reshape(NT, P, N),
        "adjT": adj.reshape(NT, P, NT, P).transpose(0, 3, 2, 1).reshape(NT, P, N),
        "W0T": np.asarray(L0_gnn_W).T,
        "b0": np.asarray(L0_gnn_b),
        "W_sa": np.asarray(L1_gnn_W_sa),
        "a_sa": np.asarray(L1_gnn_a_sa).reshape(2 * D),
        "W_gates": np.concatenate([np.asarray(L1_gnn_W_gcnb), Wa[:, :D].T, Wb[:, :D].T, Wa[:, D:].T, Wb[:, D:].T], axis=1),
        "b_gcnb": np.asarray(L1_gnn_b_gcnb),
        "b_gates": np.concatenate([np.asarray(L1_gnn_ba), np.asarray(L1_gnn_bb)]),
        "Wk": heads_side_by_side(L2_gnn_Wks),
        "Wq": heads_side_by_side(L2_gnn_Wqs),
        "Wv": heads_side_by_side(L2_gnn_Wvs),
        "Wo": np.asarray(L2_gnn_Wo).reshape(HD, D),
        "W_values": np.asarray(L3_gnn_W_stack)[:, :, :D],
        "W_hT": np.asarray(L3_gnn_W_stack)[:, :, :D].transpose(0, 2, 1),
        "W_sT": np.asarray(L3_gnn_W_stack)[:, :, D:].transpose(0, 2, 1),
    }
    arrays = {n: np.ascontiguousarray(a) for n, a in arrays.items()}
    nc = bacc.Bacc("TRN2", target_bir_lowering=False, num_devices=1)
    args = [nc.dram_tensor(n, a.shape, F32, kind="ExternalInput").ap() for n, a in arrays.items()]
    args_by_name = dict(zip(arrays, args))
    out = nc.dram_tensor("out", (NT, P, D), F32, kind="ExternalOutput").ap()
    graph_layers(nc, **args_by_name, out=out)
    r = run_bass_kernel_spmd(nc, [arrays], core_ids=[0])
    return r.results[0]["out"].reshape(N, D)
```
